# Optimizing a Trainium2 kernel written in Bass

```python
import numpy as np
import jax
import jax.numpy as jnp

def _softmax(x, axis=-1):
    return jax.nn.softmax(x, axis=axis)

def _gelu(x):
    return jax.nn.gelu(x, approximate=True)

def _silu(x):
    return jax.nn.silu(x)

def _sigmoid(x):
    return jax.nn.sigmoid(x)

def _layernorm(x, axis=-1, eps=1e-05):
    m = jnp.mean(x, axis=axis, keepdims=True)
    v = jnp.var(x, axis=axis, keepdims=True)
    return (x - m) / jnp.sqrt(v + eps)

def _scatter_add(tgt, idx, src, axis=0):
    return tgt.at[idx].add(src)

def _segment_sum(src, seg, n):
    return jax.ops.segment_sum(src, seg, n)
kernel_name = 'mk_macaron_d2_jaxref_r8_16f5ef'

def setup_inputs(seed: int=0):
    np.random.seed(seed)
    _w = jnp.asarray

    def _L0_attn_setup():
        import jax, jax.numpy as jnp
        import numpy as np
        D_MODEL, D_STATE, EXPAND, D_CONV, HEADDIM = (128, 128, 2, 4, 64)
        D_INNER = EXPAND * D_MODEL
        NHEADS = D_INNER // HEADDIM
        NGROUPS = 1
        CONV_DIM = D_INNER + 2 * NGROUPS * D_STATE
        D_IN_PROJ = 2 * D_INNER + 2 * NGROUPS * D_STATE + NHEADS
        BATCH, SEQ = (2, 512)
        EPS = 1e-05

        def _mamba2(u, in_proj_w, conv_w, conv_b, dt_bias, A_log, Dp, norm_w, out_proj_w):
            b, l, _ = u.shape
            zxbcdt = u @ in_proj_w.T
            z, xBC, dt = jnp.split(zxbcdt, [D_INNER, D_INNER + CONV_DIM], axis=-1)
            xBC = jnp.transpose(xBC, (0, 2, 1))
            xBC = jax.lax.conv_general_dilated(xBC, conv_w[:, None, :], window_strides=(1,), padding=[(D_CONV - 1, 0)], feature_group_count=CONV_DIM, dimension_numbers=('NCH', 'OIH', 'NCH'))
            xBC = jax.nn.silu(jnp.transpose(xBC, (0, 2, 1)) + conv_b)
            x, Bm, Cm = jnp.split(xBC, [D_INNER, D_INNER + NGROUPS * D_STATE], axis=-1)
            dt = jax.nn.softplus(dt + dt_bias)
            A = -jnp.exp(A_log)
            xh = x.reshape(b, l, NHEADS, HEADDIM)
            dt_t, x_t = (jnp.moveaxis(dt, 1, 0), jnp.moveaxis(xh, 1, 0))
            B_t, C_t = (jnp.moveaxis(Bm, 1, 0), jnp.moveaxis(Cm, 1, 0))

            def step(h, inputs):
                dtk, xk, Bk, Ck = inputs
                decay = jnp.exp(dtk * A)
                h = h * decay[:, :, None, None] + dtk[:, :, None, None] * xk[..., None] * Bk[:, None, None, :]
                y = jnp.einsum('bhpn,bn->bhp', h, Ck)
                return (h, y)
            h0 = jnp.zeros((b, NHEADS, HEADDIM, D_STATE), u.dtype)
            _, ys = jax.lax.scan(step, h0, (dt_t, x_t, B_t, C_t))
            y = jnp.moveaxis(ys, 0, 1) + Dp[None, None, :, None] * xh
            y = y.reshape(b, l, D_INNER)
            y = y * jax.nn.silu(z)
            y = y * jax.lax.rsqrt(jnp.mean(y * y, axis=-1, keepdims=True) + EPS) * norm_w
            return y @ out_proj_w.T
        key = jax.random.key(seed)
        ks = jax.random.split(key, 6)
        sn = lambda k, shape, sc: jax.random.normal(k, shape, jnp.float32) * sc
        dt = jnp.linspace(0.001, 0.1, NHEADS)
        return {'x': sn(ks[0], (BATCH, SEQ, D_MODEL), 1.0), 'ln_w': jnp.ones((D_MODEL,), jnp.float32), 'ln_b': jnp.zeros((D_MODEL,), jnp.float32), 'in_proj_w': sn(ks[1], (D_IN_PROJ, D_MODEL), D_MODEL ** (-0.5)), 'conv_w': sn(ks[2], (CONV_DIM, D_CONV), D_CONV ** (-0.5)), 'conv_b': jnp.zeros((CONV_DIM,), jnp.float32), 'dt_bias': jnp.log(jnp.expm1(dt)).astype(jnp.float32), 'A_log': jnp.log(jnp.arange(1, NHEADS + 1, dtype=jnp.float32)), 'D': jnp.ones((NHEADS,), jnp.float32), 'norm_w': jnp.ones((D_INNER,), jnp.float32), 'out_proj_w': sn(ks[3], (D_MODEL, D_INNER), D_INNER ** (-0.5))}
    _L0_attn_in = _L0_attn_setup()

    def _L0_ffn_setup():
        import jax, jax.numpy as jnp
        import numpy as np
        key = jax.random.key(seed)
        ks = jax.random.split(key, 5)
        B, S, D_in, D_out, E, R = (4, 128, 128, 128, 8, 16)
        x = jax.random.normal(ks[0], (B, S, D_in), dtype=jnp.float32)
        weight = jax.random.normal(ks[1], (D_out, D_in), dtype=jnp.float32) / np.sqrt(D_in)
        gate_w = jax.random.normal(ks[2], (E, D_in), dtype=jnp.float32) / np.sqrt(D_in)
        lora_U = jax.random.normal(ks[3], (E, R, D_in), dtype=jnp.float32) / np.sqrt(D_in)
        lora_V = jax.random.normal(ks[4], (E, D_out, R), dtype=jnp.float32) / np.sqrt(R)
        return {'x': x, 'weight': weight, 'gate_w': gate_w, 'lora_U': lora_U, 'lora_V': lora_V}
    _L0_ffn_in = _L0_ffn_setup()

    def _L1_attn_setup():
        import jax, jax.numpy as jnp
        import numpy as np
        N_HEAD = 16
        key = jax.random.key(seed)
        ks = jax.random.split(key, 10)
        C = 128
        B, T = (4, 1024)
        s = 1.0 / np.sqrt(C)
        return {'x': jax.random.normal(ks[0], (B, T, C), dtype=jnp.float32), 'Wq': jax.random.normal(ks[1], (C, C), dtype=jnp.float32) * s, 'bq': jax.random.normal(ks[2], (C,), dtype=jnp.float32) * s, 'Wk': jax.random.normal(ks[3], (C, C), dtype=jnp.float32) * s, 'bk': jax.random.normal(ks[4], (C,), dtype=jnp.float32) * s, 'Wv': jax.random.normal(ks[5], (C, C), dtype=jnp.float32) * s, 'bv': jax.random.normal(ks[6], (C,), dtype=jnp.float32) * s, 'Wp': jax.random.normal(ks[7], (C, C), dtype=jnp.float32) * s, 'bp': jax.random.normal(ks[8], (C,), dtype=jnp.float32) * s}
    _L1_attn_in = _L1_attn_setup()

    def _L1_ffn_setup():
        import jax, jax.numpy as jnp
        import numpy as np
        HIDDEN_SIZE = 128
        NUM_EXPERTS = 8
        MOE_INTERMEDIATE_SIZE = 176
        NUM_EXPERTS_PER_TOK = 2
        SHARED_EXPERT_INTERMEDIATE_SIZE = 352
        B, T = (2, 128)
        W_SCALE = 0.02
        key = jax.random.key(seed)
        ks = jax.random.split(key, 8)
        H, E, I, SI = (HIDDEN_SIZE, NUM_EXPERTS, MOE_INTERMEDIATE_SIZE, SHARED_EXPERT_INTERMEDIATE_SIZE)
        return {'x': jax.random.normal(ks[0], (B, T, H), jnp.float32), 'gate_w': jax.random.normal(ks[1], (E, H), jnp.float32) * W_SCALE, 'experts_gate_up': jax.random.normal(ks[2], (E, 2 * I, H), jnp.float32) * W_SCALE, 'experts_down': jax.random.normal(ks[3], (E, H, I), jnp.float32) * W_SCALE, 'shared_gate_w': jax.random.normal(ks[4], (SI, H), jnp.float32) * W_SCALE, 'shared_up_w': jax.random.normal(ks[5], (SI, H), jnp.float32) * W_SCALE, 'shared_down_w': jax.random.normal(ks[6], (H, SI), jnp.float32) * W_SCALE, 'shared_expert_gate_w': jax.random.normal(ks[7], (1, H), jnp.float32) * W_SCALE}
    _L1_ffn_in = _L1_ffn_setup()
    _d = {'L0_attn_x': _L0_attn_in['x'], 'L0_attn_ln_w': _L0_attn_in['ln_w'], 'L0_attn_ln_b': _L0_attn_in['ln_b'], 'L0_attn_in_proj_w': _L0_attn_in['in_proj_w'], 'L0_attn_conv_w': _L0_attn_in['conv_w'], 'L0_attn_conv_b': _L0_attn_in['conv_b'], 'L0_attn_dt_bias': _L0_attn_in['dt_bias'], 'L0_attn_A_log': _L0_attn_in['A_log'], 'L0_attn_D': _L0_attn_in['D'], 'L0_attn_norm_w': _L0_attn_in['norm_w'], 'L0_attn_out_proj_w': _L0_attn_in['out_proj_w'], 'L0_ffn_weight': _L0_ffn_in['weight'], 'L0_ffn_gate_w': _L0_ffn_in['gate_w'], 'L0_ffn_lora_U': _L0_ffn_in['lora_U'], 'L0_ffn_lora_V': _L0_ffn_in['lora_V'], 'L1_attn_Wq': _L1_attn_in['Wq'], 'L1_attn_bq': _L1_attn_in['bq'], 'L1_attn_Wk': _L1_attn_in['Wk'], 'L1_attn_bk': _L1_attn_in['bk'], 'L1_attn_Wv': _L1_attn_in['Wv'], 'L1_attn_bv': _L1_attn_in['bv'], 'L1_attn_Wp': _L1_attn_in['Wp'], 'L1_attn_bp': _L1_attn_in['bp'], 'L1_ffn_gate_w': _L1_ffn_in['gate_w'], 'L1_ffn_experts_gate_up': _L1_ffn_in['experts_gate_up'], 'L1_ffn_experts_down': _L1_ffn_in['experts_down'], 'L1_ffn_shared_gate_w': _L1_ffn_in['shared_gate_w'], 'L1_ffn_shared_up_w': _L1_ffn_in['shared_up_w'], 'L1_ffn_shared_down_w': _L1_ffn_in['shared_down_w'], 'L1_ffn_shared_expert_gate_w': _L1_ffn_in['shared_expert_gate_w']}
    _x0 = _d['L0_attn_x']
    _d['L0_attn_x'] = jax.random.normal(jax.random.fold_in(jax.random.key(seed), 1), (2, 2048, 128), dtype=_x0.dtype)
    del _x0
    return _d

def reference(L0_attn_x, L0_attn_ln_w, L0_attn_ln_b, L0_attn_in_proj_w, L0_attn_conv_w, L0_attn_conv_b, L0_attn_dt_bias, L0_attn_A_log, L0_attn_D, L0_attn_norm_w, L0_attn_out_proj_w, L0_ffn_weight, L0_ffn_gate_w, L0_ffn_lora_U, L0_ffn_lora_V, L1_attn_Wq, L1_attn_bq, L1_attn_Wk, L1_attn_bk, L1_attn_Wv, L1_attn_bv, L1_attn_Wp, L1_attn_bp, L1_ffn_gate_w, L1_ffn_experts_gate_up, L1_ffn_experts_down, L1_ffn_shared_gate_w, L1_ffn_shared_up_w, L1_ffn_shared_down_w, L1_ffn_shared_expert_gate_w):

    def _L0_attn_ref(x, ln_w, ln_b, in_proj_w, conv_w, conv_b, dt_bias, A_log, D, norm_w, out_proj_w):
        import jax, jax.numpy as jnp
        import numpy as np
        D_MODEL, D_STATE, EXPAND, D_CONV, HEADDIM = (128, 128, 2, 4, 64)
        D_INNER = EXPAND * D_MODEL
        NHEADS = D_INNER // HEADDIM
        NGROUPS = 1
        CONV_DIM = D_INNER + 2 * NGROUPS * D_STATE
        D_IN_PROJ = 2 * D_INNER + 2 * NGROUPS * D_STATE + NHEADS
        BATCH, SEQ = (2, 512)
        EPS = 1e-05

        def _mamba2(u, in_proj_w, conv_w, conv_b, dt_bias, A_log, Dp, norm_w, out_proj_w):
            b, l, _ = u.shape
            zxbcdt = u @ in_proj_w.T
            z, xBC, dt = jnp.split(zxbcdt, [D_INNER, D_INNER + CONV_DIM], axis=-1)
            xBC = jnp.transpose(xBC, (0, 2, 1))
            xBC = jax.lax.conv_general_dilated(xBC, conv_w[:, None, :], window_strides=(1,), padding=[(D_CONV - 1, 0)], feature_group_count=CONV_DIM, dimension_numbers=('NCH', 'OIH', 'NCH'))
            xBC = jax.nn.silu(jnp.transpose(xBC, (0, 2, 1)) + conv_b)
            x, Bm, Cm = jnp.split(xBC, [D_INNER, D_INNER + NGROUPS * D_STATE], axis=-1)
            dt = jax.nn.softplus(dt + dt_bias)
            A = -jnp.exp(A_log)
            xh = x.reshape(b, l, NHEADS, HEADDIM)
            dt_t, x_t = (jnp.moveaxis(dt, 1, 0), jnp.moveaxis(xh, 1, 0))
            B_t, C_t = (jnp.moveaxis(Bm, 1, 0), jnp.moveaxis(Cm, 1, 0))

            def step(h, inputs):
                dtk, xk, Bk, Ck = inputs
                decay = jnp.exp(dtk * A)
                h = h * decay[:, :, None, None] + dtk[:, :, None, None] * xk[..., None] * Bk[:, None, None, :]
                y = jnp.einsum('bhpn,bn->bhp', h, Ck)
                return (h, y)
            h0 = jnp.zeros((b, NHEADS, HEADDIM, D_STATE), u.dtype)
            _, ys = jax.lax.scan(step, h0, (dt_t, x_t, B_t, C_t))
            y = jnp.moveaxis(ys, 0, 1) + Dp[None, None, :, None] * xh
            y = y.reshape(b, l, D_INNER)
            y = y * jax.nn.silu(z)
            y = y * jax.lax.rsqrt(jnp.mean(y * y, axis=-1, keepdims=True) + EPS) * norm_w
            return y @ out_proj_w.T
        mu = jnp.mean(x, -1, keepdims=True)
        var = jnp.mean((x - mu) ** 2, -1, keepdims=True)
        xn = (x - mu) * jax.lax.rsqrt(var + EPS) * ln_w + ln_b
        return x + _mamba2(xn, in_proj_w, conv_w, conv_b, dt_bias, A_log, D, norm_w, out_proj_w)

    def _L0_ffn_ref(x, weight, gate_w, lora_U, lora_V):
        import jax, jax.numpy as jnp
        import numpy as np
        scaling = 1.0 / lora_U.shape[1]
        B, S, D_in = x.shape
        xt = x.reshape(-1, D_in)
        gate = jax.nn.softmax(xt @ gate_w.T, axis=-1)
        base = xt @ weight.T
        t = jnp.einsum('nh,erh->ner', xt, lora_U)
        lora = jnp.einsum('ne,eor,ner->no', gate, lora_V, t)
        out = base + scaling * lora
        return out.reshape(B, S, -1)

    def _L1_attn_ref(x, Wq, bq, Wk, bk, Wv, bv, Wp, bp):
        import jax, jax.numpy as jnp
        import numpy as np
        N_HEAD = 16
        B, T, C = x.shape
        H = N_HEAD
        d = C // H

        def proj_heads(W, b):
            h = x @ W.T + b
            return h.reshape(B, T, H, d).transpose(0, 2, 1, 3)
        q = proj_heads(Wq, bq)
        k = proj_heads(Wk, bk)
        v = proj_heads(Wv, bv)
        q = jax.nn.softmax(q, axis=-1)
        k = jax.nn.softmax(k, axis=-1)
        k_sum = k.sum(axis=-2, keepdims=True)
        D_inv = 1.0 / (q * k_sum).sum(axis=-1, keepdims=True)
        context = jnp.einsum('bhnd,bhnv->bhdv', k, v)
        out = jnp.einsum('bhqd,bhdv->bhqv', q, context)
        out = out * D_inv + q
        out = out.transpose(0, 2, 1, 3).reshape(B, T, C)
        return out @ Wp.T + bp

    def _L1_ffn_ref(x, gate_w, experts_gate_up, experts_down, shared_gate_w, shared_up_w, shared_down_w, shared_expert_gate_w):
        import jax, jax.numpy as jnp
        import numpy as np
        HIDDEN_SIZE = 128
        NUM_EXPERTS = 8
        MOE_INTERMEDIATE_SIZE = 176
        NUM_EXPERTS_PER_TOK = 2
        SHARED_EXPERT_INTERMEDIATE_SIZE = 352
        B, T = (2, 128)
        W_SCALE = 0.02
        Bx, Tx, H = x.shape
        E = gate_w.shape[0]
        I = experts_down.shape[2]
        x_flat = x.reshape(Bx * Tx, H)
        logits = x_flat @ gate_w.T
        scores = jax.nn.softmax(logits, axis=-1)
        _, topk_ids = jax.lax.top_k(scores, NUM_EXPERTS_PER_TOK)
        in_topk = jax.nn.one_hot(topk_ids, E, dtype=x.dtype).sum(axis=1)
        w = scores * in_topk
        gu = jnp.einsum('nh,eih->nei', x_flat, experts_gate_up)
        g, u = (gu[..., :I], gu[..., I:])
        h = jax.nn.silu(g) * u
        expert_out = jnp.einsum('nei,ehi->neh', h, experts_down)
        out = jnp.einsum('neh,ne->nh', expert_out, w)
        shared = jax.nn.silu(x_flat @ shared_gate_w.T) * (x_flat @ shared_up_w.T) @ shared_down_w.T
        shared_weight = jax.nn.sigmoid(x_flat @ shared_expert_gate_w.T)
        out = out + shared_weight * shared
        return out.reshape(Bx, Tx, H)
    x = L0_attn_x
    x = x + 0.5 * _L0_ffn_ref(_layernorm(x, axis=-1), L0_ffn_weight, L0_ffn_gate_w, L0_ffn_lora_U, L0_ffn_lora_V)
    x = x + _L0_attn_ref(_layernorm(x, axis=-1), L0_attn_ln_w, L0_attn_ln_b, L0_attn_in_proj_w, L0_attn_conv_w, L0_attn_conv_b, L0_attn_dt_bias, L0_attn_A_log, L0_attn_D, L0_attn_norm_w, L0_attn_out_proj_w)
    x = x + 0.5 * _L0_ffn_ref(_layernorm(x, axis=-1), L0_ffn_weight, L0_ffn_gate_w, L0_ffn_lora_U, L0_ffn_lora_V)
    x = x + 0.5 * _L1_ffn_ref(_layernorm(x, axis=-1), L1_ffn_gate_w, L1_ffn_experts_gate_up, L1_ffn_experts_down, L1_ffn_shared_gate_w, L1_ffn_shared_up_w, L1_ffn_shared_down_w, L1_ffn_shared_expert_gate_w)
    x = x + _L1_attn_ref(_layernorm(x, axis=-1), L1_attn_Wq, L1_attn_bq, L1_attn_Wk, L1_attn_bk, L1_attn_Wv, L1_attn_bv, L1_attn_Wp, L1_attn_bp)
    x = x + 0.5 * _L1_ffn_ref(_layernorm(x, axis=-1), L1_ffn_gate_w, L1_ffn_experts_gate_up, L1_ffn_experts_down, L1_ffn_shared_gate_w, L1_ffn_shared_up_w, L1_ffn_shared_down_w, L1_ffn_shared_expert_gate_w)
    return x

_drawn_inputs = setup_inputs


def setup_inputs(seed=0):
    import zlib

    import numpy as np

    out = dict(_drawn_inputs(seed))
    spreads = {'L0_attn_ln_w': (1.0, 0.2),
     'L0_attn_ln_b': (0.0, 0.1),
     'L0_attn_conv_b': (0.0, 0.1),
     'L0_attn_D': (1.0, 0.6),
     'L0_attn_norm_w': (1.0, 0.2)}
    factors = {'L0_ffn_gate_w': 4.598,
     'L0_ffn_lora_U': 3.076,
     'L0_ffn_lora_V': 3.075,
     'L1_attn_bq': 8.0,
     'L1_attn_Wk': 4.376,
     'L1_attn_bk': 8.0,
     'L1_ffn_gate_w': 8.0,
     'L1_ffn_experts_gate_up': 8.0,
     'L1_ffn_experts_down': 8.0,
     'L1_ffn_shared_gate_w': 8.0,
     'L1_ffn_shared_up_w': 8.0,
     'L1_ffn_shared_down_w': 8.0,
     'L1_ffn_shared_expert_gate_w': 8.0}
    for name, (base, spread) in spreads.items():
        noise = np.random.default_rng([zlib.crc32(name.encode()), seed]).standard_normal(out[name].shape)
        drawn = base * np.exp(spread * noise) if base else spread * noise
        out[name] = jnp.asarray(drawn.astype(out[name].dtype))
    for name, factor in factors.items():
        out[name] = (out[name] * factor).astype(out[name].dtype)
    return out
```

```python
from contextlib import ExitStack

import numpy as np

import concourse.bass as bass
import concourse.mybir as mybir
from concourse.alu_op_type import AluOpType as ALU

ACT = mybir.ActivationFunctionType
F32 = mybir.dt.float32
BF16 = mybir.dt.bfloat16
AX = mybir.AxisListType

P = 128
BATCH, SEQ, DM = 2, 2048, 128
TILES_PER_BLOCK = 4
BT = TILES_PER_BLOCK * P
NBLK = BATCH * SEQ // BT
BLK_PER_BATCH = SEQ // BT
E0, RANK = 8, 16
HEADS, HDIM, DSTATE, DCONV = 4, 64, 128, 4
DINNER = HEADS * HDIM
XBC_CHUNKS = (DINNER + 2 * DSTATE) // P
CH_B, CH_C = DINNER // P, DINNER // P + 1
E1, IEXP, ISHARED = 8, 176, 352
CHANNELS = E1 * IEXP + ISHARED
NCH = -(-CHANNELS // P)
GATES = E1 + 1
PARTS = 3
HALF = BT // 2
AHEADS, ADIM = 16, 8
QKV = 3 * DM
EPS = 1e-5
ATANH = [2.0 / (2 * k + 1) for k in range(8)]


class Steps:

    def __init__(self, nc, ctx):
        self.nc, self.ctx = nc, ctx
        self.engine = {"tensor": nc.tensor, "vector": nc.vector, "scalar": nc.scalar, "gpsimd": nc.gpsimd,
                       "sync": nc.sync}
        self.sems, self.count, self.waited = {}, {}, {}

    def wait(self, engine, *waits):
        for sem, value in waits:
            if self.waited.get((engine, sem), 0) < value:
                self.waited[(engine, sem)] = value
                self.engine[engine].wait_ge(self.sems[sem], value)

    def step(self, engine, name, emit, *waits, inc=1):
        key = f"{engine}_{name}"
        if key not in self.sems:
            self.sems[key] = self.ctx.enter_context(self.nc.semaphore(key))
            self.count[key] = 0
        self.wait(engine, *(w for w in waits if w is not None))
        emit(self.engine[engine]).then_inc(self.sems[key], inc)
        self.count[key] += inc
        return key, self.count[key]


def build(nc, d, out):
    with ExitStack() as ctx:
        q = Steps(nc, ctx)

        def sb(name, shape, dt=F32):
            return ctx.enter_context(nc.sbuf_tensor(name, shape, dt))

        def pe(name, emit, *w):
            return q.step("tensor", name, emit, *w)

        def dve(name, emit, *w):
            return q.step("vector", name, emit, *w)

        def act(name, emit, *w):
            return q.step("scalar", name, emit, *w)

        def pool(name, emit, *w):
            return q.step("gpsimd", name, emit, *w)

        def load(name, *copies, engine="sync"):
            for dst, src in copies:
                t = q.step(engine, "load_" + name, lambda e, dst=dst, src=src: e.dma_start(dst, src), inc=16)
            return t

        xs = sb("xs", [P, NBLK * TILES_PER_BLOCK, DM])
        ident = sb("ident", [P, P])
        tri_incl = sb("tri_incl", [P, P])
        tri_strict = sb("tri_strict", [P, P])
        ones = sb("ones", [P, P])
        head_mask = sb("head_mask", [P, AHEADS])
        first_key = sb("first_key", [P, E1])
        gate_rows = PARTS * GATES
        sel = sb("sel", [gate_rows, NCH * P], BF16)
        identb = sb("identb", [P, P], BF16)
        neghalf = sb("neghalf", [P, TILES_PER_BLOCK])

        w0 = sb("w0", [P, DM])
        u0 = sb("u0", [P, E0 * RANK])
        gate0 = sb("gate0", [P, E0])
        v0 = sb("v0", [P, DM])
        xbc_w = sb("xbc_w", [P, XBC_CHUNKS * P])
        zdt_w = sb("zdt_w", [P, DINNER + HEADS])
        conv_w = sb("conv_w", [P, XBC_CHUNKS, DCONV])
        conv_b = sb("conv_b", [P, XBC_CHUNKS])
        ln_w = sb("ln_w", [P, 1])
        ln_b = sb("ln_b", [P, 1])
        dt_bias = sb("dt_bias", [P, HEADS])
        a_log = sb("a_log", [P, HEADS])
        a_neg = sb("a_neg", [P, HEADS])
        d_skip = sb("d_skip", [P, HEADS])
        norm_w = sb("norm_w", [P, DINNER // P])
        out_w = sb("out_w", [P, DINNER // P, DM])
        g_w = sb("g_w", [P, NCH * P])
        u_w = sb("u_w", [P, NCH * P])
        d_w = sb("d_w", [P, NCH, DM])
        gate1 = sb("gate1", [P, GATES])
        qkv_w = sb("qkv_w", [P, QKV])
        qkv_b = sb("qkv_b", [P, QKV])
        p_w = sb("p_w", [P, DM])
        p_b = sb("p_b", [P, DM])

        gu_bank = [ctx.enter_context(nc.psum_tensor(f"gu{i}", [P, 2 * HALF], F32)) for i in range(2)]
        wb_bank = ctx.enter_context(nc.psum_tensor("wb", [P, 2 * HALF], F32))
        down_bank = ctx.enter_context(nc.psum_tensor("down", [P, 2 * HALF], F32))
        ring_bank = [ctx.enter_context(nc.psum_tensor(f"ring{i}", [P, 512], F32)) for i in range(4)]
        ring = {"next": 0, "read": [()] * 4}

        def take():
            i = ring["next"]
            ring["next"] = (i + 1) % 4
            return i, ring_bank[i], ring["read"][i]

        def give(i, *readers):
            ring["read"][i] = readers

        x_tiles = d["x"].rearrange("(t p) c -> p t c", p=P)
        loaded_x = []
        L = {}

        def load_block(b):
            t = b * TILES_PER_BLOCK
            loaded_x.append(load(f"x{b}", (xs[:, t:t + TILES_PER_BLOCK, :], x_tiles[:, t:t + TILES_PER_BLOCK, :])))

        def load_weights(group, engine="sync", **tiles):
            t = load(group, *((tile, d[name]) for name, tile in tiles.items()), engine=engine)
            for name in tiles:
                L[name] = t

        load_block(0)
        load_weights("ffn0", ident=ident[:, :], w0=w0[:, :], u0=u0[:, :], gate0=gate0[:, :], v0=v0[:, :])
        load_weights("proj", engine="scalar", xbc_w=xbc_w[:, :], zdt_w=zdt_w[:, :], conv_w=conv_w[:, :, :],
                     conv_b=conv_b[:, :], ln_w=ln_w[:, :], ln_b=ln_b[:, :])
        rows = {n: d[n].broadcast_to([P, w]) for n, w in
                (("dt_bias", HEADS), ("a_log", HEADS), ("d_skip", HEADS), ("first_key", E1), ("qkv_b", QKV), ("p_b", DM))}
        d.update(rows)
        load_weights("scan", dt_bias=dt_bias[:, :], a_log=a_log[:, :], d_skip=d_skip[:, :], norm_w=norm_w[:, :],
                     out_w=out_w[:, :, :], tri_incl=tri_incl[:, :], tri_strict=tri_strict[:, :])
        load_block(1)
        load_weights("sel", engine="gpsimd", sel=sel[:, :])
        load_weights("gates", first_key=first_key[:, :], gate1=gate1[:, :])
        load_weights("experts", g_w=g_w[:, :], u_w=u_w[:, :], d_w=d_w[:, :, :])
        load_weights("attn", head_mask=head_mask[:, :], qkv_w=qkv_w[:, :], qkv_b=qkv_b[:, :], p_w=p_w[:, :],
                     p_b=p_b[:, :])
        for b in range(2, NBLK):
            load_block(b)

        L["neghalf"] = pool("const", lambda e: e.memset(neghalf[:, :], -0.5))
        L["ones"] = pool("const", lambda e: e.memset(ones[:, :], 1.0))
        L["identb"] = pool("identb", lambda e: e.tensor_copy(identb[:, :], ident[:, :]), L["ident"])
        t = act("a_exp", lambda e: e.activation(a_neg[:, :], a_log[:, :], ACT.Exp), L["a_log"])
        L["a_neg"] = dve("a_neg", lambda e: e.tensor_scalar(a_neg[:, :], a_neg[:, :], -1.0, None, ALU.mult), t)

        xs_ready = [None] * NBLK

        def blk(b):
            return xs[:, b * TILES_PER_BLOCK:(b + 1) * TILES_PER_BLOCK, :]

        T4 = range(TILES_PER_BLOCK)

        def buffers(name, shape, n=2, dt=F32):
            return {"t": [sb(f"{name}{i}", shape, dt) for i in range(n)], "n": n, "k": 0, "read": [()] * n}

        def turn(bufs):
            i = bufs["k"] % bufs["n"]
            bufs["k"] += 1
            return i, bufs["t"][i], bufs["read"][i]

        def read_by(bufs, i, *steps):
            bufs["read"][i] = steps

        ln_bufs = {}

        def layernorm(tag, src, dst, ready, dst_read):
            if tag not in ln_bufs:
                ln_bufs[tag] = buffers(f"lnb_{tag}", [P, 4 * 6 + 4 * 2 + 4 + 4])
            i, t, read = turn(ln_bufs[tag])
            stats = t[:, 0:24].rearrange("p (j s) -> p j s", s=6)
            mv = t[:, 24:32].rearrange("p (j s) -> p j s", s=2)
            veps, rstd = t[:, 32:36], t[:, 36:40]

            def stat(e):
                for j in T4:
                    last = e.bn_stats(stats[:, j, :], src[:, j, :])
                return last
            s = dve("ln_stats", stat, *ready, *read)

            def aggr(e):
                for j in T4:
                    last = e.bn_aggr(mv[:, j, :], stats[:, j, :])
                return last
            s = dve("ln_aggr", aggr, s)
            yield
            g = pool("ln_veps", lambda e: e.tensor_scalar(veps, mv[:, :, 1], EPS, None, ALU.add), s)
            g = pool("ln_rstd", lambda e: e.tensor_tensor(rstd, veps, neghalf[:, :], ALU.pow),
                     g, L["neghalf"])
            yield

            def norm(e):
                for j in T4:
                    last = e.tensor_scalar(dst[:, j, :], src[:, j, :], mv[:, j, 0:1], rstd[:, j:j + 1],
                                           ALU.subtract, ALU.mult)
                return last
            done = dve("ln_norm", norm, g, s, *dst_read)
            read_by(ln_bufs[tag], i, done)
            yield done

        def to_channels(tag, src, dst, ready, dst_read, scale=None, bias=None):
            i, bank, read = take()

            def tr(e):
                for j in T4:
                    last = e.transpose(bank[:, j * P:(j + 1) * P], src(j), ident[:, :])
                return last
            s = pe("turn", tr, *ready, *read, L["ident"])
            yield
            if bias is not None:
                f = lambda e: e.activation(dst, bank[:, :], ACT.Identity, scale=scale, bias=bias)
            elif scale is not None:
                f = lambda e: e.activation(dst, bank[:, :], ACT.Copy, scale=scale)
            else:
                f = lambda e: e.activation(dst, bank[:, :], ACT.Copy)
            done = act("turned", f, s, *dst_read)
            give(i, done)
            yield s, done

        def run(gen):
            last = None
            for last in gen:
                if last is None:
                    yield None
            return last

        f0_xn = buffers("f0_xn", [P, 4, DM], 1)
        f0_xT = buffers("f0_xT", [P, BT])
        f0_g = buffers("f0_g", [P, 4, 2 * E0 + 3])
        f0_tg = buffers("f0_tg", [P, 4, DM], 1)
        f0_tT = buffers("f0_tT", [P, BT], 1)

        def ffn0(b):
            x = blk(b)
            i_xn, xn, r_xn = turn(f0_xn)
            normed = yield from run(layernorm("f0", x, xn, [xs_ready[b]], r_xn))
            i_xT, xT, r_xT = turn(f0_xT)
            tr, xT_ready = yield from run(to_channels("f0x", lambda j: xn[:, j, :], xT[:, :], [normed], r_xT))
            read_by(f0_xn, i_xn, tr)
            i_l, lbank, l_read = take()
            i_t, tbank, t_read = take()
            logits = lbank[:, 0:4 * E0].rearrange("p (j e) -> p j e", e=E0)

            def mm_gate(e):
                for j in T4:
                    last = e.matmul(logits[:, j, :], xT[:, j * P:(j + 1) * P], gate0[:, :], start=True, stop=True)
                return last
            s_l = pe("f0_gate", mm_gate, xT_ready, L["gate0"], *l_read)

            def mm_t(e):
                for j in T4:
                    last = e.matmul(tbank[:, j * P:(j + 1) * P], xT[:, j * P:(j + 1) * P], u0[:, :],
                                    start=True, stop=True)
                return last
            s_t = pe("f0_down", mm_t, L["u0"], *t_read)
            yield
            i_g, gt, r_g = turn(f0_g)
            ex, gg = gt[:, :, 0:E0], gt[:, :, E0:2 * E0]
            mx, sm, rs = (gt[:, :, 2 * E0 + k:2 * E0 + k + 1] for k in range(3))
            s = dve("f0_max", lambda e: e.tensor_reduce(mx, logits, AX.X, ALU.max), s_l, *r_g)
            s = dve("f0_sub", lambda e: e.tensor_tensor(ex, logits, mx.broadcast_to([P, 4, E0]), ALU.subtract), s)
            give(i_l, s)
            yield
            s = act("f0_exp", lambda e: e.activation(ex, ex, ACT.Exp), s)
            yield
            s1 = dve("f0_sum", lambda e: e.tensor_reduce(sm, ex, AX.X, ALU.add), s)
            s1 = dve("f0_rec", lambda e: e.reciprocal(rs, sm), s1)
            s1 = dve("f0_gates", lambda e: e.scalar_tensor_tensor(
                gg, ex, 1.0 / RANK, rs.broadcast_to([P, 4, E0]), ALU.mult, ALU.mult), s1)
            i_tg, tg, r_tg = turn(f0_tg)

            def scale_t(e):
                for j in T4:
                    last = e.tensor_tensor(tg[:, j, :].rearrange("p (e r) -> p e r", r=RANK),
                                           tbank[:, j * P:(j + 1) * P].rearrange("p (e r) -> p e r", r=RANK),
                                           gg[:, j, :].unsqueeze(2).broadcast_to([P, E0, RANK]), ALU.mult)
                return last
            s = dve("f0_tg", scale_t, s1, s_t, *r_tg)
            give(i_t, s)
            read_by(f0_g, i_g, s)
            yield
            i_tT, tT, r_tT = turn(f0_tT)
            tr, tT_ready = yield from run(to_channels("f0t", lambda j: tg[:, j, :], tT[:, :], [s], r_tT))
            read_by(f0_tg, i_tg, tr)
            i, bank, read = take()

            def mm_out(e):
                for j in T4:
                    o = bank[:, j * P:(j + 1) * P]
                    e.matmul(o, xT[:, j * P:(j + 1) * P], w0[:, :], start=True, stop=False)
                    last = e.matmul(o, tT[:, j * P:(j + 1) * P], v0[:, :], start=False, stop=True)
                return last
            s = pe("f0_out", mm_out, tT_ready, L["w0"], L["v0"], *read)
            read_by(f0_xT, i_xT, s)
            read_by(f0_tT, i_tT, s)
            yield
            s = dve("f0_res", lambda e: e.scalar_tensor_tensor(
                x, bank[:, :].rearrange("p (j c) -> p j c", c=DM), 0.5, x, ALU.mult, ALU.add), s)
            give(i, s)
            xs_ready[b] = s
            yield

        m_xa = buffers("m_xa", [P, 4, DM])
        m_xb = buffers("m_xb", [P, 4, DM], 1)
        m_xT = buffers("m_xT", [P, BT], 1)
        halo = DCONV - 1
        m_pre = buffers("m_pre", [P, halo + BT], 3)
        m_halo = [sb(f"m_halo{i}", [P, XBC_CHUNKS, halo]) for i in range(2)]
        m_cv = buffers("m_cv", [P, XBC_CHUNKS, BT])
        m_sz = buffers("m_sz", [P, 4, DINNER])
        m_dt = buffers("m_dt", [P, 16, 4 * HEADS])
        m_ex = buffers("m_ex", [P, 3, 4 * HEADS])
        m_seg = buffers("m_seg", [P, HEADS, P])
        m_e = buffers("m_e", [P, HEADS, P])
        m_gm = buffers("m_gm", [P, P])
        m_xt = buffers("m_xt", [P, 3 * P])
        m_xd = buffers("m_xd", [P, 3, DINNER])
        m_y = buffers("m_y", [P, 2, DINNER])
        m_g = buffers("m_g", [P, 4, DINNER])
        m_gT = buffers("m_gT", [P, 2, BT], 1)
        m_rs = buffers("m_rs", [P, 3, 4])
        m_sq = sb("m_sq", [P, DINNER])
        state = [sb(f"state{i}", [P, DINNER]) for i in range(2)]
        state_q = sb("state_q", [P, DINNER])
        m_state = {"ready": None, "k": 0, "read": [(), ()], "q_read": ()}

        def heads(ap, h=HEADS):
            return ap.rearrange("p (h c) -> p h c", h=h)

        def per_head(ap):
            return ap.unsqueeze(2).broadcast_to([P, HEADS, HDIM])

        def mamba(b):
            x = blk(b)
            first = b % BLK_PER_BATCH == 0
            i_xa, xa, r_xa = turn(m_xa)
            xa_ready = yield from run(layernorm("ma", x, xa, [xs_ready[b]], r_xa))
            i_xb, xb, r_xb = turn(m_xb)
            xb_ready = yield from run(layernorm("mb", xa, xb, [xa_ready], r_xb))
            summed = pool("m_sum", lambda e: e.tensor_tensor(x, x, xa[:, :, :], ALU.add), xa_ready)
            i_xT, xT, r_xT = turn(m_xT)
            tr, xT_ready = yield from run(to_channels("mx", lambda j: xb[:, j, :], xT[:, :], [xb_ready, L["ln_w"], L["ln_b"]],
                                                      r_xT, ln_w[:, 0:1], ln_b[:, 0:1]))
            read_by(m_xb, i_xb, tr)
            read_by(m_xa, i_xa, summed, xb_ready)
            i_sz, sz, r_sz = turn(m_sz)
            i_dt, dtt, r_dt = turn(m_dt)
            dt3 = dtt[:, :, :].rearrange("p k (j h) -> p k j h", h=HEADS)
            raw = dt3[:, 0, :, :]
            dt_parts, sz_parts = [], []
            for j in T4:
                i, bank, read = take()
                s = pe("m_zdt", lambda e, bank=bank, j=j: e.matmul(
                    bank[:, 0:DINNER + HEADS], xT[:, j * P:(j + 1) * P], zdt_w[:, :], start=True, stop=True),
                    xT_ready, L["zdt_w"], *read)
                yield
                a = act("m_silu_z", lambda e, bank=bank, j=j: e.activation(sz[:, j, :], bank[:, 0:DINNER], ACT.Silu),
                        s, *r_sz)
                v = dve("m_dtraw", lambda e, bank=bank, j=j: e.tensor_tensor(
                    raw[:, j, :], bank[:, DINNER:DINNER + HEADS], dt_bias[:, :], ALU.add), s, a, L["dt_bias"], *r_dt)
                give(i, a, v)
            sz_ready, raw_ready = a, v
            yield
            i_cv, cv, r_cv = turn(m_cv)
            old_halo, new_halo = m_halo[(b + 1) % 2], m_halo[b % 2]
            convs, halos = [], []
            for c in range(XBC_CHUNKS):
                i_pre, pre, r_pre = turn(m_pre)
                if first:
                    h_in = pool("m_halo0", lambda e, pre=pre: e.memset(pre[:, 0:halo], 0.0), *r_pre)
                else:
                    h_in = pool("m_halo", lambda e, pre=pre, c=c: e.tensor_copy(pre[:, 0:halo], old_halo[:, c, :]),
                                m_state["halos"][c], *r_pre)
                i, bank, read = take()
                s = pe("m_xbc", lambda e, bank=bank, c=c: e.matmul(
                    bank[:, :], xbc_w[:, c * P:(c + 1) * P], xT[:, :], start=True, stop=True),
                    L["xbc_w"], *read)
                yield
                a0 = act("m_pre", lambda e, bank=bank, pre=pre: e.activation(
                    pre[:, halo:halo + BT], bank[:, :], ACT.Copy), s, *r_pre)
                a1 = act("m_tap", lambda e, bank=bank, c=c: e.activation(
                    cv[:, c, :], bank[:, :], ACT.Identity, scale=conv_w[:, c, halo:halo + 1],
                    bias=conv_b[:, c:c + 1]), L["conv_w"], L["conv_b"], *r_cv)
                give(i, a1)
                h_out = pool("m_halo_out", lambda e, pre=pre, c=c: e.tensor_copy(
                    new_halo[:, c, :], pre[:, BT:BT + halo]), a0, h_in)
                halos.append(h_out)
                v = a1
                for k in range(halo):
                    v = dve("m_conv", lambda e, k=k, c=c, pre=pre: e.scalar_tensor_tensor(
                        cv[:, c, :], pre[:, k:k + BT], conv_w[:, c, k:k + 1], cv[:, c, :],
                        ALU.mult, ALU.add), v, a0, h_in)
                read_by(m_pre, i_pre, v, h_out)
                convs.append(v)
                yield
            read_by(m_xT, i_xT, s)
            m_state["halos"] = halos
            cv_ready = []
            for c in range(XBC_CHUNKS):
                cv_ready.append(act("m_silu", lambda e, c=c: e.activation(cv[:, c, :], cv[:, c, :], ACT.Silu),
                                    convs[c]))
                yield
            row = lambda k: dtt[:, k, :]
            s = dve("m_sp", lambda e: e.tensor_scalar(row(1), row(0), -1.0, None, ALU.mult), raw_ready)
            s = dve("m_sp", lambda e: e.tensor_tensor(row(1), row(0), row(1), ALU.min), s)
            s = act("m_spexp", lambda e: e.activation(row(2), row(1), ACT.Exp), s)
            yield
            s = dve("m_sp", lambda e: e.tensor_scalar(row(3), row(2), 2.0, None, ALU.add), s)
            s = dve("m_sp", lambda e: e.reciprocal(row(4), row(3)), s)
            s = dve("m_sp", lambda e: e.tensor_tensor(row(5), row(2), row(4), ALU.mult), s)
            s = dve("m_sp", lambda e: e.tensor_tensor(row(6), row(5), row(5), ALU.mult), s)
            s = dve("m_sp", lambda e: e.tensor_scalar(row(7), row(6), ATANH[7], ATANH[6], ALU.mult, ALU.add), s)
            for k in (5, 4, 3, 2, 1, 0):
                s = dve("m_sp", lambda e: e.tensor_tensor(row(7), row(7), row(6), ALU.mult), s)
                s = dve("m_sp", lambda e, k=k: e.tensor_scalar(row(7), row(7), ATANH[k], None, ALU.add), s)
            s = dve("m_sp", lambda e: e.tensor_tensor(row(7), row(7), row(5), ALU.mult), s)
            dt_ready = dve("m_dt", lambda e: e.scalar_tensor_tensor(
                row(8), row(0), 0.0, row(7), ALU.max, ALU.add), s)
            dta_ready = dve("m_dta", lambda e: e.tensor_tensor(
                dt3[:, 9, :, :], dt3[:, 8, :, :], a_neg[:, :].unsqueeze(1).broadcast_to([P, 4, HEADS]), ALU.mult),
                dt_ready, L["a_neg"])
            dt, dta = row(8), row(9)
            yield
            i_ex, ex, r_ex = turn(m_ex)
            i, bank, read = take()

            def mm_sums(e):
                n = 4 * HEADS
                e.matmul(bank[:, 0:n], tri_incl[:, :], dta, start=True, stop=True)
                e.matmul(bank[:, n:2 * n], tri_strict[:, :], dta, start=True, stop=True)
                return e.matmul(bank[:, 2 * n:3 * n], ones[:, :], dta, start=True, stop=True)
            s = pe("m_sums", mm_sums, dta_ready, L["tri_incl"], L["tri_strict"], L["ones"], *read)
            ex_ready = act("m_exps", lambda e: e.activation(
                ex[:, :, :], bank[:, 0:12 * HEADS].rearrange("p (k n) -> p k n", k=3), ACT.Exp), s, *r_ex)
            give(i, ex_ready)
            yield
            dtr = dve("m_dtr", lambda e: e.tensor_tensor(row(10), dt, ex[:, 1, :], ALU.mult), ex_ready)
            i_g, g, r_g = turn(m_g)
            i_rs, rs, r_rs = turn(m_rs)
            squares = []
            for j in T4:
                tok = slice(j * P, (j + 1) * P)
                hj = slice(j * HEADS, (j + 1) * HEADS)
                i_seg, seg, r_seg = turn(m_seg)
                s_seg = pool("m_seg", lambda e, seg=seg, hj=hj: e.tensor_tensor(
                    seg[:, :, :], tri_incl[:, :].unsqueeze(1).broadcast_to([P, HEADS, P]),
                    dta[:, hj].unsqueeze(2).broadcast_to([P, HEADS, P]), ALU.mult), dta_ready, *r_seg)
                i_tp, tbank, t_read = take()

                def tr(e, tbank=tbank, tok=tok):
                    for c in range(3):
                        last = e.transpose(tbank[:, c * P:(c + 1) * P], cv[:, c, tok], ident[:, :])
                    return last
                s_tr = pe("m_tr", tr, *cv_ready[0:3], *t_read)
                i_gb, gbank, g_read = take()
                s_g = pe("m_G", lambda e, gbank=gbank, tok=tok: e.matmul(
                    gbank[:, 0:P], cv[:, CH_B, tok], cv[:, CH_C, tok], start=True, stop=True),
                    cv_ready[3], *g_read)
                yield
                i_xt, xt, r_xt = turn(m_xt)
                xt_ready = act("m_xt", lambda e, xt=xt, tbank=tbank: e.activation(
                    xt[:, :], tbank[:, 0:3 * P], ACT.Copy), s_tr, *r_xt)
                give(i_tp, xt_ready)
                i_gm, gm, r_gm = turn(m_gm)
                gm_ready = dve("m_gm", lambda e, gm=gm, gbank=gbank: e.tensor_tensor(
                    gm[:, :], gbank[:, 0:P], tri_incl[:, :], ALU.mult), s_g, *r_gm)
                give(i_gb, gm_ready)
                i_d, dbank, d_read = take()
                s_d = pe("m_D", lambda e, dbank=dbank, seg=seg: e.matmul(
                    dbank[:, :], tri_strict[:, :], seg[:, :, :].rearrange("p h t -> p (h t)"),
                    start=True, stop=True), s_seg, *d_read)
                read_by(m_seg, i_seg, s_d)
                yield
                i_e, et, r_e = turn(m_e)
                s = act("m_decay", lambda e, et=et, dbank=dbank: e.activation(
                    et[:, :, :], dbank[:, :].rearrange("p (h t) -> p h t", h=HEADS), ACT.Exp), s_d, *r_e)
                give(i_d, s)
                i_xd, xd, r_xd = turn(m_xd)
                xh = heads(xt[:, 0:DINNER])
                s_xd = pool("m_xdt", lambda e, xd=xd, xh=xh, hj=hj: e.tensor_tensor(
                    heads(xd[:, 0, :]), xh, per_head(dt[:, hj]), ALU.mult), xt_ready, dt_ready, *r_xd)
                s_xs = pool("m_xds", lambda e, xd=xd, xh=xh, hj=hj: e.tensor_tensor(
                    heads(xd[:, 1, :]), xh, per_head(row(10)[:, hj]), ALU.mult), dtr)
                s_dx = pool("m_dx", lambda e, xd=xd, xh=xh: e.tensor_tensor(
                    heads(xd[:, 2, :]), xh, per_head(d_skip[:, :]), ALU.mult), L["d_skip"])
                yield
                m_ready = dve("m_M", lambda e, et=et, gm=gm: e.tensor_tensor(
                    et[:, :, :], et[:, :, :], gm[:, :].unsqueeze(1).broadcast_to([P, HEADS, P]), ALU.mult),
                    s, gm_ready)
                read_by(m_gm, i_gm, m_ready)
                yield
                start_of_batch = first and j == 0
                i_y, ybank, y_read = take()
                old = state[m_state["k"] % 2]

                def mm_y(e, ybank=ybank, mt=et, xd=xd, tok=tok, old=old, start_of_batch=start_of_batch):
                    if not start_of_batch:
                        e.matmul(ybank[:, DINNER:2 * DINNER], cv[:, CH_C, tok], old[:, :], start=True, stop=True)
                    for h in range(HEADS):
                        c = slice(h * HDIM, (h + 1) * HDIM)
                        last = e.matmul(ybank[:, c], mt[:, h, :], xd[:, 0, c], start=True, stop=True)
                    return last
                s_y = pe("m_Y", mm_y, m_ready, s_xd, m_state["ready"] if not start_of_batch else None, *y_read)
                read_by(m_e, i_e, s_y)
                i_s, sbank, s_read = take()
                s_st = pe("m_S", lambda e, sbank=sbank, xt=xt, xd=xd: e.matmul(
                    sbank[:, 0:DINNER], xt[:, 2 * P:3 * P], xd[:, 1, :], start=True, stop=True), s_xs, *s_read)
                new_k = (m_state["k"] + 1) % 2
                new = state[new_k]
                if start_of_batch:
                    st = dve("m_state", lambda e, new=new, sbank=sbank: e.tensor_copy(new[:, :], sbank[:, 0:DINNER]),
                             s_st, *m_state["read"][new_k])
                else:
                    sq = pool("m_stateq", lambda e, old=old, hj=hj: e.tensor_tensor(
                        heads(state_q[:, :]), heads(old[:, :]), per_head(ex[:, 2, hj]), ALU.mult),
                        m_state["ready"], ex_ready, *m_state["q_read"])
                    st = dve("m_state", lambda e, new=new, sbank=sbank: e.tensor_tensor(
                        new[:, :], state_q[:, :], sbank[:, 0:DINNER], ALU.add), s_st, sq, *m_state["read"][new_k])
                    m_state["q_read"] = (st,)
                    m_state["read"][m_state["k"] % 2] = (s_y, sq)
                m_state["ready"] = st
                m_state["k"] = new_k
                give(i_s, st)
                yield
                i_yy, yy, r_yy = turn(m_y)
                s1 = dve("m_y1", lambda e, yy=yy, ybank=ybank, xd=xd: e.tensor_tensor(
                    yy[:, 0, :], ybank[:, 0:DINNER], xd[:, 2, :], ALU.add), s_y, s_dx, *r_yy)
                if not start_of_batch:
                    s2 = dve("m_y2", lambda e, yy=yy, ybank=ybank, hj=hj: e.tensor_tensor(
                        heads(yy[:, 1, :]), heads(ybank[:, DINNER:2 * DINNER]), per_head(ex[:, 0, hj]), ALU.mult),
                        ex_ready)
                    s3 = dve("m_y3", lambda e, yy=yy: e.tensor_tensor(
                        yy[:, 0, :], yy[:, 0, :], yy[:, 1, :], ALU.add), s1, s2)
                else:
                    s2, s3 = s1, s1
                give(i_y, s1, s2)
                read_by(m_xt, i_xt, s_st, s_dx)
                read_by(m_xd, i_xd, s_y, s_st, s1)
                s4 = dve("m_gated", lambda e, yy=yy, j=j: e.tensor_tensor(
                    g[:, j, :], yy[:, 0, :], sz[:, j, :], ALU.mult), s3, sz_ready, *r_g)
                read_by(m_y, i_yy, s4)
                squares.append(act("m_sq", lambda e, j=j: e.activation(
                    m_sq[:, :], g[:, j, :], ACT.Square, accum_out=rs[:, 0, j:j + 1]), s4, *r_rs,
                    squares[-1] if squares else m_state.get("sq")))
                m_state["sq"] = squares[-1]
                yield
            read_by(m_cv, i_cv, s_y)
            read_by(m_sz, i_sz, s4)
            read_by(m_dt, i_dt, s_xs, s_seg)
            read_by(m_ex, i_ex, s2, sq if not start_of_batch else st)
            s = pool("m_ms", lambda e: e.tensor_scalar(rs[:, 1, :], rs[:, 0, :], 1.0 / DINNER, EPS, ALU.mult, ALU.add),
                     squares[-1])
            rstd_ready = pool("m_rstd", lambda e: e.tensor_tensor(rs[:, 2, :], rs[:, 1, :], neghalf[:, :], ALU.pow), s)
            i_gT, gT, r_gT = turn(m_gT)
            for c in range(DINNER // P):
                tr, gT_ready = yield from run(to_channels(
                    "mg", lambda j, c=c: g[:, j, c * P:(c + 1) * P], gT[:, c, :], [s4, L["norm_w"]], r_gT,
                    norm_w[:, c:c + 1]))
            read_by(m_g, i_g, tr, squares[-1])
            i, bank, read = take()

            def mm_out(e):
                for j in T4:
                    for c in range(DINNER // P):
                        last = e.matmul(bank[:, j * P:(j + 1) * P], gT[:, c, j * P:(j + 1) * P], out_w[:, c, :],
                                        start=(c == 0), stop=(c == DINNER // P - 1))
                return last
            s = pe("m_out", mm_out, gT_ready, L["out_w"], *read)
            read_by(m_gT, i_gT, s)
            yield

            def res(e):
                for j in T4:
                    last = e.scalar_tensor_tensor(x[:, j, :], bank[:, j * P:(j + 1) * P], rs[:, 2, j:j + 1],
                                                  x[:, j, :], ALU.mult, ALU.add)
                return last
            s = dve("m_res", res, s, rstd_ready, summed)
            give(i, s)
            read_by(m_rs, i_rs, s)
            xs_ready[b] = s
            yield

        f1_xn = buffers("f1_xn", [P, 4, DM])
        f1_xT = buffers("f1_xT", [P, BT])
        f1_g = buffers("f1_g", [P, 12, 4 * E1])
        f1_s = buffers("f1_s", [P, 8, 4])
        f1_w9 = buffers("f1_w9", [P, 3, 4, GATES])
        f1_w27 = buffers("f1_w27", [P, 4, PARTS, GATES], 2, BF16)
        f1_wT = buffers("f1_wT", [gate_rows, BT], 2, BF16)
        f1_ready = {}

        def ffn1_gates(b):
            x = blk(b)
            i_xn, xn, r_xn = turn(f1_xn)
            normed = yield from run(layernorm("f1", x, xn, [xs_ready[b]], r_xn))
            i_xT, xT, r_xT = turn(f1_xT)
            tr, xT_ready = yield from run(to_channels("f1x", lambda j: xn[:, j, :], xT[:, :], [normed], r_xT))
            read_by(f1_xn, i_xn, tr)
            i, bank, read = take()
            logits = bank[:, 0:4 * GATES].rearrange("p (j e) -> p j e", e=GATES)

            def mm_gate(e):
                for j in T4:
                    last = e.matmul(logits[:, j, :], xT[:, j * P:(j + 1) * P], gate1[:, :], start=True, stop=True)
                return last
            s_l = pe("f1_gate", mm_gate, xT_ready, L["gate1"], *read)
            yield
            i_g, gt, r_g = turn(f1_g)
            i_s, st, r_s = turn(f1_s)
            i_w9, w9, r_w9 = turn(f1_w9)
            col = lambda k: gt[:, k, :].rearrange("p (j e) -> p j e", e=E1)
            one = lambda k: st[:, k, :]
            wide = lambda k: one(k).unsqueeze(2).broadcast_to([P, 4, E1])
            keys = first_key[:, :].unsqueeze(1).broadcast_to([P, 4, E1])
            s = dve("f1_max", lambda e: e.tensor_reduce(one(0), logits[:, :, 0:E1], AX.X, ALU.max), s_l, *r_s, *r_g)
            s = dve("f1_sub", lambda e: e.tensor_tensor(col(0), logits[:, :, 0:E1], wide(0), ALU.subtract), s)
            s_sg = act("f1_sgexp", lambda e: e.activation(one(7), logits[:, :, E1], ACT.Exp, scale=-1.0), s_l, s, *r_s)
            yield
            give(i, s, s_sg)
            s = act("f1_exp", lambda e: e.activation(gt[:, 1, :], gt[:, 0, :], ACT.Exp), s)
            yield
            s = dve("f1_r", lambda e: e.tensor_reduce(one(1), col(1), AX.X, ALU.add), s)
            s = dve("f1_r", lambda e: e.reciprocal(one(2), one(1)), s)
            s = dve("f1_r", lambda e: e.tensor_tensor(col(2), col(1), wide(2), ALU.mult), s)
            chosen = []
            cur = 2
            for k in range(2):
                s = dve("f1_r", lambda e, c=cur, k=k: e.tensor_reduce(one(3 + k), col(c), AX.X, ALU.max), s)
                s = dve("f1_r", lambda e, c=cur, k=k: e.tensor_tensor(col(3), col(c), wide(3 + k), ALU.is_equal), s)
                s = dve("f1_r", lambda e: e.tensor_tensor(col(4), col(3), keys, ALU.mult), s, L["first_key"])
                s = dve("f1_r", lambda e, k=k: e.tensor_reduce(one(5 + k), col(4), AX.X, ALU.max), s)
                s = dve("f1_r", lambda e, k=k: e.tensor_tensor(col(5 + k), col(4), wide(5 + k), ALU.is_equal), s)
                if k == 0:
                    s = dve("f1_r", lambda e: e.scalar_tensor_tensor(
                        col(7), col(5), -2.0, col(2), ALU.mult, ALU.add), s)
                    cur = 7
                yield
            s = dve("f1_r", lambda e: e.tensor_tensor(col(8), col(5), col(6), ALU.add), s)
            s = dve("f1_r", lambda e: e.tensor_tensor(w9[:, 0, :, 0:E1], col(8), col(2), ALU.mult), s, *r_w9)
            s = dve("f1_r", lambda e: e.tensor_scalar(one(7), one(7), 1.0, None, ALU.add), s, s_sg)
            s = dve("f1_r", lambda e: e.reciprocal(w9[:, 0, :, E1], one(7)), s)
            yield
            i_w, w27, r_w = turn(f1_w27)
            s = dve("f1_r", lambda e: e.tensor_copy(w27[:, :, 0, :], w9[:, 0, :, :]), s, *r_w)
            s = dve("f1_r", lambda e: e.tensor_tensor(w9[:, 1, :, :], w9[:, 0, :, :], w27[:, :, 0, :], ALU.subtract), s)
            s = dve("f1_r", lambda e: e.tensor_copy(w27[:, :, 1, :], w9[:, 1, :, :]), s)
            s = dve("f1_r", lambda e: e.tensor_tensor(w9[:, 2, :, :], w9[:, 1, :, :], w27[:, :, 1, :], ALU.subtract), s)
            s = dve("f1_w27", lambda e: e.tensor_copy(w27[:, :, 2, :], w9[:, 2, :, :]), s)
            for bufs, n in ((f1_g, i_g), (f1_s, i_s), (f1_w9, i_w9)):
                read_by(bufs, n, s)
            yield
            i, bank, read = take()
            bankb = bank[:, :].bitcast(BF16)

            def tr_w(e):
                for j in T4:
                    last = e.transpose(bankb[0:gate_rows, j * P:(j + 1) * P],
                                       w27[:, j, :, :].rearrange("p a e -> p (a e)"), identb[:, :])
                return last
            s = pe("f1_wtr", tr_w, s, L["identb"], *read)
            read_by(f1_w27, i_w, s)
            i_wT, wT, r_wT = turn(f1_wT)
            wT_ready = act("f1_wT", lambda e: e.activation(wT[:, :], bankb[0:gate_rows, 0:BT], ACT.Copy), s, *r_wT)
            give(i, wT_ready)
            f1_ready[b] = (xT, xT_ready, i_xT, wT, wT_ready, i_wT)
            yield

        f1_sg = buffers("f1_sg", [P, HALF], 3)
        f1_t = buffers("f1_t", [P, HALF], 2)
        f1_h = buffers("f1_h", [P, HALF], 4)
        f1_o = buffers("f1_o", [P, BT], 1)
        gu_read, once = [(), ()], {"wb": (), "down": ()}
        f1_count = {"k": 0}
        LAG = 2

        def ffn1_experts(b, store):
            x = blk(b)
            xT, xT_ready, i_xT, wT, wT_ready, i_wT = f1_ready[b]
            for half in range(2):
                tok = slice(half * HALF, (half + 1) * HALF)
                h_ready = {}
                down = down_bank[:, tok]
                for c in range(NCH + LAG):
                    if c < NCH:
                        k = f1_count["k"] % 2
                        f1_count["k"] += 1
                        ch = slice(c * P, (c + 1) * P)
                        gu = gu_bank[k]

                        def mm_gu(e, gu=gu, ch=ch, tok=tok):
                            e.matmul(gu[:, 0:HALF], g_w[:, ch], xT[:, tok], start=True, stop=True)
                            return e.matmul(gu[:, HALF:2 * HALF], u_w[:, ch], xT[:, tok], start=True, stop=True)
                        s_gu = pe("f1_gu", mm_gu, xT_ready, L["g_w"], L["u_w"], *gu_read[k])
                    if c >= LAG:
                        n = c - LAG
                        i_h, h, ready = h_ready[n]
                        s_d = pe("f1_down", lambda e, h=h, n=n, down=down: e.matmul(
                            down, d_w[:, n, :], h[:, :], start=(n == 0), stop=(n == NCH - 1)),
                            ready, L["d_w"], *(once["down"] if n == 0 and half == 0 else ()))
                        read_by(f1_h, i_h, s_d)
                    if c < NCH:
                        s_wb = pe("f1_wb", lambda e, ch=ch, tok=tok: e.matmul(
                            wb_bank[:, 0:HALF], sel[:, ch], wT[:, tok], start=True, stop=True),
                            wT_ready, L["sel"], *once["wb"])
                        i_sg, sg, r_sg = turn(f1_sg)
                        a = act("f1_silu", lambda e, sg=sg, gu=gu: e.activation(sg[:, :], gu[:, 0:HALF], ACT.Silu),
                                s_gu, *r_sg)
                        i_t, t, r_t = turn(f1_t)
                        v = dve("f1_su", lambda e, sg=sg, gu=gu, t=t: e.tensor_tensor(
                            t[:, :], sg[:, :], gu[:, HALF:2 * HALF], ALU.mult), a, *r_t)
                        gu_read[k] = (a, v)
                        read_by(f1_sg, i_sg, v)
                        i_h, h, r_h = turn(f1_h)
                        v = dve("f1_h", lambda e, t=t, h=h: e.tensor_tensor(
                            h[:, :], t[:, :], wb_bank[:, 0:HALF], ALU.mult), v, s_wb, *r_h)
                        once["wb"] = (v,)
                        read_by(f1_t, i_t, v)
                        h_ready[c] = (i_h, h, v)
                    yield
            read_by(f1_xT, i_xT, s_gu)
            read_by(f1_wT, i_wT, s_wb)
            i_o, o, r_o = turn(f1_o)
            o_ready = act("f1_o", lambda e: e.activation(o[:, :], down_bank[:, :], ACT.Copy), s_d, *r_o)
            once["down"] = (o_ready,)
            yield
            i, bank, read = take()

            def tr(e):
                for j in T4:
                    last = e.transpose(bank[:, j * P:(j + 1) * P], o[:, j * P:(j + 1) * P], ident[:, :])
                return last
            s = pe("f1_otr", tr, o_ready, *read)
            read_by(f1_o, i_o, s)
            yield
            s = dve("f1_res", lambda e: e.scalar_tensor_tensor(
                x, bank[:, :].rearrange("p (j c) -> p j c", c=DM), 0.5, x, ALU.mult, ALU.add), s)
            give(i, s)
            xs_ready[b] = s
            if store:
                t0 = b * TILES_PER_BLOCK
                q.step("sync", "store", lambda e: e.dma_start(out_tiles[:, t0:t0 + TILES_PER_BLOCK, :], x), s, inc=16)

        out_tiles = out.rearrange("(t p) c -> p t c", p=P)

        a_xn = buffers("a_xn", [P, 4, DM], 1)
        a_xT = buffers("a_xT", [P, BT])
        VW = QKV + 1
        a_qkv = buffers("a_qkv", [P, 4, VW], 2)
        a_q = [sb(f"a_q{b}", [P, 4, DM]) for b in range(BLK_PER_BATCH)]
        a_st = buffers("a_st", [P, 3, 4 * 2 * AHEADS])
        a_ctx = sb("a_ctx", [P, DM + 1])
        a_cm = sb("a_cm", [P, DM + AHEADS])
        a_qT = buffers("a_qT", [P, BT], 1)
        a_o = buffers("a_o", [P, 4, DM], 1)
        a_oT = buffers("a_oT", [P, BT], 1)
        a_di = buffers("a_di", [P, 4, AHEADS])
        att = {"q_read": [()] * BLK_PER_BATCH, "ctx_read": (), "cm_read": (), "ctx": None, "ones": [], "q": {}}
        for t in a_qkv["t"]:
            att["ones"].append(pool("a_ones", lambda e, t=t: e.memset(t[:, :, QKV:VW], 1.0)))

        def attn_kv(b):
            x = blk(b)
            n = b % BLK_PER_BATCH
            i_xn, xn, r_xn = turn(a_xn)
            normed = yield from run(layernorm("at", x, xn, [xs_ready[b]], r_xn))
            i_xT, xT, r_xT = turn(a_xT)
            tr, xT_ready = yield from run(to_channels("atx", lambda j: xn[:, j, :], xT[:, :], [normed], r_xT))
            read_by(a_xn, i_xn, tr)
            i_k, qkv, r_k = turn(a_qkv)
            for j in T4:
                i, bank, read = take()
                s = pe("a_qkv", lambda e, bank=bank, j=j: e.matmul(
                    bank[:, 0:QKV], xT[:, j * P:(j + 1) * P], qkv_w[:, :], start=True, stop=True),
                    xT_ready, L["qkv_w"], *read)
                v = dve("a_bias", lambda e, bank=bank, j=j: e.tensor_tensor(
                    qkv[:, j, 0:QKV], bank[:, 0:QKV], qkv_b[:, :], ALU.add), s, L["qkv_b"], *r_k)
                give(i, v)
                yield
            read_by(a_xT, i_xT, s)
            i_st, st, r_st = turn(a_st)
            G = 2 * AHEADS
            qk = lambda j: qkv[:, j, 0:2 * DM].rearrange("p (g c) -> p g c", c=ADIM)
            sj = lambda k, j: st[:, k, j * G:(j + 1) * G]
            wide = lambda k, j: sj(k, j).unsqueeze(2).broadcast_to([P, G, ADIM])

            def each(f):
                def emit(e):
                    for j in T4:
                        last = f(e, j)
                    return last
                return emit
            s = dve("a_max", each(lambda e, j: e.tensor_reduce(sj(0, j), qk(j), AX.X, ALU.max)), v, *r_st)
            s = dve("a_sub", each(lambda e, j: e.tensor_tensor(qk(j), qk(j), wide(0, j), ALU.subtract)), s)
            yield
            s = act("a_exp", lambda e: e.activation(qkv[:, :, 0:2 * DM], qkv[:, :, 0:2 * DM], ACT.Exp), s)
            yield
            s = dve("a_sumd", each(lambda e, j: e.tensor_reduce(sj(1, j), qk(j), AX.X, ALU.add)), s)
            s = dve("a_rec", lambda e: e.reciprocal(st[:, 2, :], st[:, 1, :]), s)
            k_part = lambda j: qkv[:, j, DM:2 * DM].rearrange("p (g c) -> p g c", c=ADIM)
            wk = lambda j: sj(2, j)[:, AHEADS:].unsqueeze(2).broadcast_to([P, AHEADS, ADIM])
            wq = lambda j: sj(2, j)[:, :AHEADS].unsqueeze(2).broadcast_to([P, AHEADS, ADIM])
            k_ready = dve("a_k", each(lambda e, j: e.tensor_tensor(k_part(j), k_part(j), wk(j), ALU.mult)), s)
            qn = a_q[n]
            q_ready = dve("a_q", each(lambda e, j: e.tensor_tensor(
                qn[:, j, :].rearrange("p (g c) -> p g c", c=ADIM),
                qkv[:, j, 0:DM].rearrange("p (g c) -> p g c", c=ADIM), wq(j), ALU.mult)), s, *att["q_read"][n])
            att["q"][b] = q_ready
            read_by(a_st, i_st, q_ready)
            yield
            i, bank, read = take()

            def mm_ctx(e):
                for j in T4:
                    last = e.matmul(bank[:, 0:DM + 1], qkv[:, j, DM:2 * DM], qkv[:, j, 2 * DM:VW],
                                    start=(j == 0), stop=(j == 3))
                return last
            s = pe("a_ctx", mm_ctx, k_ready, att["ones"][i_k], *read)
            read_by(a_qkv, i_k, s, q_ready)
            if n == 0:
                s = dve("a_ctxsum", lambda e: e.tensor_copy(a_ctx[:, :], bank[:, 0:DM + 1]), s, *att["ctx_read"])
            else:
                s = dve("a_ctxsum", lambda e: e.tensor_tensor(a_ctx[:, :], a_ctx[:, :], bank[:, 0:DM + 1], ALU.add),
                        s, att["ctx"])
            give(i, s)
            att["ctx"] = s
            if n == BLK_PER_BATCH - 1:
                s1 = dve("a_cm", lambda e: e.tensor_tensor(
                    a_cm[:, 0:DM].rearrange("p (h c) -> p h c", c=ADIM),
                    a_ctx[:, 0:DM].rearrange("p (h c) -> p h c", c=ADIM),
                    head_mask[:, :].unsqueeze(2).broadcast_to([P, AHEADS, ADIM]), ALU.mult),
                    s, L["head_mask"], *att["cm_read"])
                s1 = dve("a_cm", lambda e: e.tensor_scalar(
                    a_cm[:, DM:DM + AHEADS], head_mask[:, :], a_ctx[:, DM:DM + 1], None, ALU.mult), s)
                att["ctx_read"] = (s1,)
                att["cm"] = s1
                att["cm_read"] = ()
            yield

        def attn_out(b):
            x = blk(b)
            n = b % BLK_PER_BATCH
            qn = a_q[n]
            i_qT, qT, r_qT = turn(a_qT)
            tr, qT_ready = yield from run(to_channels("aq", lambda j: qn[:, j, :], qT[:, :], [att["q"][b]], r_qT))
            biased = pool("a_bp", lambda e: e.tensor_tensor(
                x, x, p_b[:, :].unsqueeze(1).broadcast_to([P, 4, DM]), ALU.add), xs_ready[b], L["p_b"])
            i_n, nbank, n_read = take()
            i_d, dbank, d_read = take()

            def mm(e):
                for j in T4:
                    lhs = qT[:, j * P:(j + 1) * P]
                    e.matmul(nbank[:, j * P:(j + 1) * P], lhs, a_cm[:, 0:DM], start=True, stop=True)
                    last = e.matmul(dbank[:, j * AHEADS:(j + 1) * AHEADS], lhs, a_cm[:, DM:DM + AHEADS],
                                    start=True, stop=True)
                return last
            s = pe("a_num", mm, qT_ready, att["cm"], *n_read, *d_read)
            att["cm_read"] = att["cm_read"] + (s,)
            read_by(a_qT, i_qT, s)
            yield
            i_di, di, r_di = turn(a_di)
            v = dve("a_dinv", lambda e: e.reciprocal(
                di[:, :, :], dbank[:, 0:4 * AHEADS].rearrange("p (j h) -> p j h", h=AHEADS)), s, *r_di)
            give(i_d, v)
            i_o, o, r_o = turn(a_o)

            def div(e):
                for j in T4:
                    last = e.tensor_tensor(o[:, j, :].rearrange("p (h c) -> p h c", c=ADIM),
                                           nbank[:, j * P:(j + 1) * P].rearrange("p (h c) -> p h c", c=ADIM),
                                           di[:, j, :].unsqueeze(2).broadcast_to([P, AHEADS, ADIM]), ALU.mult)
                return last
            v = dve("a_div", div, v, *r_o)
            give(i_n, v)
            read_by(a_di, i_di, v)
            yield
            v = pool("a_addq", lambda e: e.tensor_tensor(o[:, :, :], o[:, :, :], qn[:, :, :], ALU.add), v)
            att["q_read"][n] = (v, tr)
            yield
            i_oT, oT, r_oT = turn(a_oT)
            tr, oT_ready = yield from run(to_channels("ao", lambda j: o[:, j, :], oT[:, :], [v], r_oT))
            read_by(a_o, i_o, tr)
            i, bank, read = take()

            def mm_p(e):
                for j in T4:
                    last = e.matmul(bank[:, j * P:(j + 1) * P], oT[:, j * P:(j + 1) * P], p_w[:, :],
                                    start=True, stop=True)
                return last
            s = pe("a_proj", mm_p, oT_ready, L["p_w"], *read)
            read_by(a_oT, i_oT, s)
            yield
            s = dve("a_res", lambda e: e.tensor_tensor(
                x, bank[:, :].rearrange("p (j c) -> p j c", c=DM), x, ALU.add), s, biased)
            give(i, s)
            xs_ready[b] = s
            yield

        for b in range(NBLK):
            xs_ready[b] = loaded_x[b]

        def chain(*gens):
            for g in gens:
                yield from g()

        def front(b):
            return chain(lambda: ffn0(b), lambda: mamba(b), lambda: ffn0(b), lambda: ffn1_gates(b))

        def back(b):
            return chain(lambda: attn_out(b), lambda: ffn1_gates(b))

        def together(heavy, other, ratio):
            live = [heavy, other]
            credit = 0.0
            while live[0] or live[1]:
                if live[0]:
                    if next(live[0], "end") == "end":
                        live[0] = None
                credit = credit + ratio if live[0] else 1
                while credit >= 1 and live[1]:
                    credit -= 1
                    if next(live[1], "end") == "end":
                        live[1] = None
                if not live[1]:
                    credit = 0

        H = BLK_PER_BATCH
        first_ffn = lambda b: (lambda: ffn1_experts(b, False))
        second_ffn = lambda b: (lambda: ffn1_experts(b, True))
        kv = lambda b: (lambda: attn_kv(b))
        fr = lambda b: (lambda: front(b))
        bk = lambda b: (lambda: back(b))
        plan = [(lambda: iter(()), [fr(0)]), (first_ffn(0), [fr(1)])]
        for b in range(1, H):
            plan.append((first_ffn(b), [kv(b - 1), fr(b + 1)]))
        for b in range(H):
            plan.append((first_ffn(H + b), [kv(H - 1), bk(0)] if b == 0 else [bk(b)]))
            plan.append((second_ffn(b), [kv(H + b), fr(H + b + 1)] if b < H - 1 else [kv(H + b), bk(H)]))
        for b in range(H, 2 * H):
            plan.append((second_ffn(b), [bk(b + 1)] if b < 2 * H - 1 else []))
        for heavy, others in plan:
            together(heavy(), chain(*others), RATIO)
        q.wait("sync", ("sync_store", q.count["sync_store"]))


RATIO = 3.0


def constants():
    u = np.arange(P)
    channel = np.arange(NCH * P)
    gate = np.where(channel < E1 * IEXP, channel // IEXP, np.where(channel < CHANNELS, E1, -1))
    return {
        "ident": np.eye(P, dtype=np.float32),
        "tri_incl": (u[:, None] <= u[None, :]).astype(np.float32),
        "tri_strict": (u[:, None] > u[None, :]).astype(np.float32),
        "head_mask": (u[:, None] // ADIM == np.arange(AHEADS)[None, :]).astype(np.float32),
        "first_key": (E1 - np.arange(E1, dtype=np.float32))[None, :],
        "sel": (np.tile(np.arange(GATES), PARTS)[:, None] == gate[None, :]).astype(np.float32),
    }


def kernel(**inputs):
    import concourse.bacc as bacc
    from concourse.bass_utils import run_bass_kernel_spmd

    i = {k: np.asarray(v) for k, v in inputs.items()}
    in_proj = i["L0_attn_in_proj_w"]
    conv = DINNER + 2 * DSTATE
    pad = NCH * P - CHANNELS
    gu = i["L1_ffn_experts_gate_up"]
    zero = np.zeros((pad, DM), np.float32)
    rows_g = np.concatenate([gu[:, :IEXP].reshape(-1, DM), i["L1_ffn_shared_gate_w"], zero])
    rows_u = np.concatenate([gu[:, IEXP:].reshape(-1, DM), i["L1_ffn_shared_up_w"], zero])
    rows_d = np.concatenate([i["L1_ffn_experts_down"].transpose(0, 2, 1).reshape(-1, DM),
                             i["L1_ffn_shared_down_w"].T, zero])
    arrays = {
        "x": i["L0_attn_x"].reshape(-1, DM),
        "w0": i["L0_ffn_weight"].T,
        "u0": i["L0_ffn_lora_U"].reshape(-1, DM).T,
        "gate0": i["L0_ffn_gate_w"].T,
        "v0": i["L0_ffn_lora_V"].transpose(0, 2, 1).reshape(-1, DM),
        "xbc_w": in_proj[DINNER:DINNER + conv].T,
        "zdt_w": np.concatenate([in_proj[:DINNER], in_proj[DINNER + conv:]]).T,
        "conv_w": i["L0_attn_conv_w"].reshape(XBC_CHUNKS, P, DCONV).transpose(1, 0, 2),
        "conv_b": i["L0_attn_conv_b"].reshape(XBC_CHUNKS, P).T,
        "ln_w": i["L0_attn_ln_w"][:, None],
        "ln_b": i["L0_attn_ln_b"][:, None],
        "dt_bias": i["L0_attn_dt_bias"][None, :],
        "a_log": i["L0_attn_A_log"][None, :],
        "d_skip": i["L0_attn_D"][None, :],
        "norm_w": i["L0_attn_norm_w"].reshape(-1, P).T,
        "out_w": i["L0_attn_out_proj_w"].T.reshape(-1, P, DM).transpose(1, 0, 2),
        "g_w": rows_g.T,
        "u_w": rows_u.T,
        "d_w": rows_d.reshape(NCH, P, DM).transpose(1, 0, 2),
        "gate1": np.concatenate([i["L1_ffn_gate_w"], i["L1_ffn_shared_expert_gate_w"]]).T,
        "qkv_w": np.concatenate([i["L1_attn_Wq"], i["L1_attn_Wk"], i["L1_attn_Wv"]]).T,
        "qkv_b": np.concatenate([i["L1_attn_bq"], i["L1_attn_bk"], i["L1_attn_bv"]])[None, :],
        "p_w": i["L1_attn_Wp"].T,
        "p_b": i["L1_attn_bp"][None, :],
    }
    arrays.update(constants())
    arrays = {f"in_{k}": np.ascontiguousarray(v) for k, v in arrays.items()}
    nc = bacc.Bacc("TRN2", target_bir_lowering=False, num_devices=1)
    d = {k[3:]: nc.dram_tensor(k, v.shape, mybir.dt.from_np(v.dtype), kind="ExternalInput").ap()
         for k, v in arrays.items()}
    out = nc.dram_tensor("out", (BATCH * SEQ, DM), F32, kind="ExternalOutput").ap()
    build(nc, d, out)
    r = run_bass_kernel_spmd(nc, [arrays], core_ids=[0])
    return r.results[0]["out"].reshape(BATCH, SEQ, DM)
```

```python
from contextlib import ExitStack

import numpy as np

import concourse.bass as bass
import concourse.mybir as mybir
from concourse.alu_op_type import AluOpType as ALU

ACT = mybir.ActivationFunctionType
F32 = mybir.dt.float32
BF16 = mybir.dt.bfloat16
AX = mybir.AxisListType

P = 128
BATCH, SEQ, DM = 2, 2048, 128
TILES_PER_BLOCK = 4
BT = TILES_PER_BLOCK * P
NBLK = BATCH * SEQ // BT
BLK_PER_BATCH = SEQ // BT
E0, RANK = 8, 16
HEADS, HDIM, DSTATE, DCONV = 4, 64, 128, 4
DINNER = HEADS * HDIM
XBC_CHUNKS = (DINNER + 2 * DSTATE) // P
CH_B, CH_C = DINNER // P, DINNER // P + 1
E1, IEXP, ISHARED = 8, 176, 352
CHANNELS = E1 * IEXP + ISHARED
NCH = -(-CHANNELS // P)
GATES = E1 + 1
PARTS = 3
HALF = BT // 2
AHEADS, ADIM = 16, 8
QKV = 3 * DM
EPS = 1e-5
ATANH = [2.0 / (2 * k + 1) for k in range(8)]


class Steps:

    def __init__(self, nc, ctx):
        self.nc, self.ctx = nc, ctx
        self.engine = {"tensor": nc.tensor, "vector": nc.vector, "scalar": nc.scalar, "gpsimd": nc.gpsimd,
                       "sync": nc.sync}
        self.sems, self.count, self.waited = {}, {}, {}

    def wait(self, engine, *waits):
        for sem, value in waits:
            if self.waited.get((engine, sem), 0) < value:
                self.waited[(engine, sem)] = value
                self.engine[engine].wait_ge(self.sems[sem], value)

    def step(self, engine, name, emit, *waits, inc=1):
        key = f"{engine}_{name}"
        if key not in self.sems:
            self.sems[key] = self.ctx.enter_context(self.nc.semaphore(key))
            self.count[key] = 0
        self.wait(engine, *(w for w in waits if w is not None))
        emit(self.engine[engine]).then_inc(self.sems[key], inc)
        self.count[key] += inc
        return key, self.count[key]


def build(nc, d, out):
    with ExitStack() as ctx:
        q = Steps(nc, ctx)

        def sb(name, shape, dt=F32):
            return ctx.enter_context(nc.sbuf_tensor(name, shape, dt))

        def pe(name, emit, *w):
            return q.step("tensor", name, emit, *w)

        def dve(name, emit, *w):
            return q.step("vector", name, emit, *w)

        def act(name, emit, *w):
            return q.step("scalar", name, emit, *w)

        def pool(name, emit, *w):
            return q.step("gpsimd", name, emit, *w)

        def load(name, *copies, engine="sync"):
            for dst, src in copies:
                t = q.step(engine, "load_" + name, lambda e, dst=dst, src=src: e.dma_start(dst, src), inc=16)
            return t

        xs = sb("xs", [P, NBLK * TILES_PER_BLOCK, DM])
        ident = sb("ident", [P, P])
        tri_incl = sb("tri_incl", [P, P])
        tri_strict = sb("tri_strict", [P, P])
        ones = sb("ones", [P, P])
        head_mask = sb("head_mask", [P, AHEADS])
        first_key = sb("first_key", [P, E1])
        gate_rows = PARTS * GATES
        sel = sb("sel", [gate_rows, NCH * P], BF16)
        identb = sb("identb", [P, P], BF16)
        neghalf = sb("neghalf", [P, TILES_PER_BLOCK])

        w0 = sb("w0", [P, DM])
        u0 = sb("u0", [P, E0 * RANK])
        gate0 = sb("gate0", [P, E0])
        v0 = sb("v0", [P, DM])
        xbc_w = sb("xbc_w", [P, XBC_CHUNKS * P])
        zdt_w = sb("zdt_w", [P, DINNER + HEADS])
        conv_w = sb("conv_w", [P, XBC_CHUNKS, DCONV])
        conv_b = sb("conv_b", [P, XBC_CHUNKS])
        ln_w = sb("ln_w", [P, 1])
        ln_b = sb("ln_b", [P, 1])
        dt_bias = sb("dt_bias", [P, HEADS])
        a_log = sb("a_log", [P, HEADS])
        a_neg = sb("a_neg", [P, HEADS])
        d_skip = sb("d_skip", [P, HEADS])
        norm_w = sb("norm_w", [P, DINNER // P])
        out_w = sb("out_w", [P, DINNER // P, DM])
        g_w = sb("g_w", [P, NCH * P])
        u_w = sb("u_w", [P, NCH * P])
        d_w = sb("d_w", [P, NCH, DM])
        gate1 = sb("gate1", [P, GATES])
        qkv_w = sb("qkv_w", [P, QKV])
        qkv_b = sb("qkv_b", [P, QKV])
        p_w = sb("p_w", [P, DM])
        p_b = sb("p_b", [P, DM])

        gu_bank = [ctx.enter_context(nc.psum_tensor(f"gu{i}", [P, 2 * HALF], F32)) for i in range(2)]
        wb_bank = ctx.enter_context(nc.psum_tensor("wb", [P, 2 * HALF], F32))
        down_bank = ctx.enter_context(nc.psum_tensor("down", [P, 2 * HALF], F32))
        ring_bank = [ctx.enter_context(nc.psum_tensor(f"ring{i}", [P, 512], F32)) for i in range(4)]
        def store_of(tiles):
            return {"tiles": tiles, "free": [(i, ()) for i in range(len(tiles))]}

        def buffers(name, shape, n=2, dt=F32):
            return store_of([sb(f"{name}{i}", shape, dt) for i in range(n)])

        def turn(bufs):
            while not bufs["free"]:
                yield None
            i, readers = bufs["free"].pop(0)
            return i, bufs["tiles"][i], readers

        def read_by(bufs, i, *readers):
            bufs["free"].append((i, readers))

        banks = store_of(ring_bank)

        def take():
            return (yield from turn(banks))

        def give(i, *readers):
            read_by(banks, i, *readers)

        x_tiles = d["x"].rearrange("(t p) c -> p t c", p=P)
        loaded_x = []
        L = {}

        def load_block(b):
            t = b * TILES_PER_BLOCK
            loaded_x.append(load(f"x{b}", (xs[:, t:t + TILES_PER_BLOCK, :], x_tiles[:, t:t + TILES_PER_BLOCK, :])))

        def load_weights(group, engine="sync", **tiles):
            t = load(group, *((tile, d[name]) for name, tile in tiles.items()), engine=engine)
            for name in tiles:
                L[name] = t

        load_block(0)
        load_weights("ffn0", ident=ident[:, :], w0=w0[:, :], u0=u0[:, :], gate0=gate0[:, :], v0=v0[:, :])
        load_weights("proj", engine="scalar", xbc_w=xbc_w[:, :], zdt_w=zdt_w[:, :], conv_w=conv_w[:, :, :],
                     conv_b=conv_b[:, :], ln_w=ln_w[:, :], ln_b=ln_b[:, :])
        rows = {n: d[n].broadcast_to([P, w]) for n, w in
                (("dt_bias", HEADS), ("a_log", HEADS), ("d_skip", HEADS), ("first_key", E1), ("qkv_b", QKV), ("p_b", DM))}
        d.update(rows)
        load_weights("scan", dt_bias=dt_bias[:, :], a_log=a_log[:, :], d_skip=d_skip[:, :], norm_w=norm_w[:, :],
                     out_w=out_w[:, :, :], tri_incl=tri_incl[:, :], tri_strict=tri_strict[:, :])
        load_block(1)
        load_weights("sel", engine="gpsimd", sel=sel[:, :])
        load_weights("gates", first_key=first_key[:, :], gate1=gate1[:, :])
        load_weights("experts", g_w=g_w[:, :], u_w=u_w[:, :], d_w=d_w[:, :, :])
        load_weights("attn", head_mask=head_mask[:, :], qkv_w=qkv_w[:, :], qkv_b=qkv_b[:, :], p_w=p_w[:, :],
                     p_b=p_b[:, :])
        for b in range(2, NBLK):
            load_block(b)

        L["neghalf"] = pool("const", lambda e: e.memset(neghalf[:, :], -0.5))
        L["ones"] = pool("const", lambda e: e.memset(ones[:, :], 1.0))
        L["identb"] = pool("identb", lambda e: e.tensor_copy(identb[:, :], ident[:, :]), L["ident"])
        t = act("a_exp", lambda e: e.activation(a_neg[:, :], a_log[:, :], ACT.Exp), L["a_log"])
        L["a_neg"] = dve("a_neg", lambda e: e.tensor_scalar(a_neg[:, :], a_neg[:, :], -1.0, None, ALU.mult), t)

        xs_ready = [None] * NBLK

        def blk(b):
            return xs[:, b * TILES_PER_BLOCK:(b + 1) * TILES_PER_BLOCK, :]

        T4 = range(TILES_PER_BLOCK)

        ln_bufs = {}

        def layernorm(tag, src, dst, ready, dst_read):
            if tag not in ln_bufs:
                ln_bufs[tag] = buffers(f"lnb_{tag}", [P, 4 * 6 + 4 * 2 + 4 + 4])
            i, t, read = yield from turn(ln_bufs[tag])
            stats = t[:, 0:24].rearrange("p (j s) -> p j s", s=6)
            mv = t[:, 24:32].rearrange("p (j s) -> p j s", s=2)
            veps, rstd = t[:, 32:36], t[:, 36:40]

            def stat(e):
                for j in T4:
                    last = e.bn_stats(stats[:, j, :], src[:, j, :])
                return last
            s = dve("ln_stats", stat, *ready, *read)

            def aggr(e):
                for j in T4:
                    last = e.bn_aggr(mv[:, j, :], stats[:, j, :])
                return last
            s = dve("ln_aggr", aggr, s)
            yield
            g = pool("ln_veps", lambda e: e.tensor_scalar(veps, mv[:, :, 1], EPS, None, ALU.add), s)
            g = pool("ln_rstd", lambda e: e.tensor_tensor(rstd, veps, neghalf[:, :], ALU.pow),
                     g, L["neghalf"])
            yield

            def norm(e):
                for j in T4:
                    last = e.tensor_scalar(dst[:, j, :], src[:, j, :], mv[:, j, 0:1], rstd[:, j:j + 1],
                                           ALU.subtract, ALU.mult)
                return last
            done = dve("ln_norm", norm, g, s, *dst_read)
            read_by(ln_bufs[tag], i, done)
            yield done

        def to_channels(tag, src, dst, ready, dst_read, scale=None, bias=None):
            i, bank, read = yield from take()

            def tr(e):
                for j in T4:
                    last = e.transpose(bank[:, j * P:(j + 1) * P], src(j), ident[:, :])
                return last
            s = pe("turn", tr, *ready, *read, L["ident"])
            yield
            if bias is not None:
                f = lambda e: e.activation(dst, bank[:, :], ACT.Identity, scale=scale, bias=bias)
            elif scale is not None:
                f = lambda e: e.activation(dst, bank[:, :], ACT.Copy, scale=scale)
            else:
                f = lambda e: e.activation(dst, bank[:, :], ACT.Copy)
            done = act("turned", f, s, *dst_read)
            give(i, done)
            yield s, done

        def run(gen):
            last = None
            for last in gen:
                if last is None:
                    yield None
            return last

        f0_xn = buffers("f0_xn", [P, 4, DM], 1)
        f0_xT = buffers("f0_xT", [P, BT])
        f0_g = buffers("f0_g", [P, 4, 2 * E0 + 3])
        f0_tg = buffers("f0_tg", [P, 4, DM], 1)
        f0_tT = buffers("f0_tT", [P, BT], 1)

        def ffn0(b):
            x = blk(b)
            i_xn, xn, r_xn = yield from turn(f0_xn)
            normed = yield from run(layernorm("f0", x, xn, [xs_ready[b]], r_xn))
            i_xT, xT, r_xT = yield from turn(f0_xT)
            tr, xT_ready = yield from run(to_channels("f0x", lambda j: xn[:, j, :], xT[:, :], [normed], r_xT))
            read_by(f0_xn, i_xn, tr)
            i_l, lbank, l_read = yield from take()
            i_t, tbank, t_read = yield from take()
            logits = lbank[:, 0:4 * E0].rearrange("p (j e) -> p j e", e=E0)

            def mm_gate(e):
                for j in T4:
                    last = e.matmul(logits[:, j, :], xT[:, j * P:(j + 1) * P], gate0[:, :], start=True, stop=True)
                return last
            s_l = pe("f0_gate", mm_gate, xT_ready, L["gate0"], *l_read)

            def mm_t(e):
                for j in T4:
                    last = e.matmul(tbank[:, j * P:(j + 1) * P], xT[:, j * P:(j + 1) * P], u0[:, :],
                                    start=True, stop=True)
                return last
            s_t = pe("f0_down", mm_t, L["u0"], *t_read)
            yield
            i_g, gt, r_g = yield from turn(f0_g)
            ex, gg = gt[:, :, 0:E0], gt[:, :, E0:2 * E0]
            mx, sm, rs = (gt[:, :, 2 * E0 + k:2 * E0 + k + 1] for k in range(3))
            s = dve("f0_max", lambda e: e.tensor_reduce(mx, logits, AX.X, ALU.max), s_l, *r_g)
            s = dve("f0_sub", lambda e: e.tensor_tensor(ex, logits, mx.broadcast_to([P, 4, E0]), ALU.subtract), s)
            give(i_l, s)
            yield
            s = act("f0_exp", lambda e: e.activation(ex, ex, ACT.Exp), s)
            yield
            s1 = dve("f0_sum", lambda e: e.tensor_reduce(sm, ex, AX.X, ALU.add), s)
            s1 = dve("f0_rec", lambda e: e.reciprocal(rs, sm), s1)
            s1 = dve("f0_gates", lambda e: e.scalar_tensor_tensor(
                gg, ex, 1.0 / RANK, rs.broadcast_to([P, 4, E0]), ALU.mult, ALU.mult), s1)
            i_tg, tg, r_tg = yield from turn(f0_tg)

            def scale_t(e):
                for j in T4:
                    last = e.tensor_tensor(tg[:, j, :].rearrange("p (e r) -> p e r", r=RANK),
                                           tbank[:, j * P:(j + 1) * P].rearrange("p (e r) -> p e r", r=RANK),
                                           gg[:, j, :].unsqueeze(2).broadcast_to([P, E0, RANK]), ALU.mult)
                return last
            s = dve("f0_tg", scale_t, s1, s_t, *r_tg)
            give(i_t, s)
            read_by(f0_g, i_g, s)
            yield
            i_tT, tT, r_tT = yield from turn(f0_tT)
            tr, tT_ready = yield from run(to_channels("f0t", lambda j: tg[:, j, :], tT[:, :], [s], r_tT))
            read_by(f0_tg, i_tg, tr)
            i, bank, read = yield from take()

            def mm_out(e):
                for j in T4:
                    o = bank[:, j * P:(j + 1) * P]
                    e.matmul(o, xT[:, j * P:(j + 1) * P], w0[:, :], start=True, stop=False)
                    last = e.matmul(o, tT[:, j * P:(j + 1) * P], v0[:, :], start=False, stop=True)
                return last
            s = pe("f0_out", mm_out, tT_ready, L["w0"], L["v0"], *read)
            read_by(f0_xT, i_xT, s)
            read_by(f0_tT, i_tT, s)
            yield
            s = dve("f0_res", lambda e: e.scalar_tensor_tensor(
                x, bank[:, :].rearrange("p (j c) -> p j c", c=DM), 0.5, x, ALU.mult, ALU.add), s)
            give(i, s)
            xs_ready[b] = s
            yield

        m_xa = buffers("m_xa", [P, 4, DM])
        m_xb = buffers("m_xb", [P, 4, DM], 1)
        m_xT = buffers("m_xT", [P, BT], 1)
        halo = DCONV - 1
        m_pre = buffers("m_pre", [P, halo + BT], 3)
        m_halo = [[sb(f"m_halo{n}_{i}", [P, XBC_CHUNKS, halo]) for i in range(2)] for n in range(BATCH)]
        m_cv = buffers("m_cv", [P, XBC_CHUNKS, BT])
        m_sz = buffers("m_sz", [P, 4, DINNER])
        m_dt = buffers("m_dt", [P, 16, 4 * HEADS])
        m_ex = buffers("m_ex", [P, 3, 4 * HEADS])
        m_seg = buffers("m_seg", [P, HEADS, P])
        m_e = buffers("m_e", [P, HEADS, P])
        m_gm = buffers("m_gm", [P, P])
        m_xt = buffers("m_xt", [P, 3 * P])
        m_xd = buffers("m_xd", [P, 3, DINNER])
        m_y = buffers("m_y", [P, 2, DINNER])
        m_g = buffers("m_g", [P, 4, DINNER])
        m_gT = buffers("m_gT", [P, 2, BT], 1)
        m_rs = buffers("m_rs", [P, 3, 4])
        m_sq = sb("m_sq", [P, DINNER])
        states = [[sb(f"state{n}_{i}", [P, DINNER]) for i in range(2)] for n in range(BATCH)]
        state_qs = [sb(f"state_q{n}", [P, DINNER]) for n in range(BATCH)]
        m_states = [{"ready": None, "k": 0, "read": [(), ()], "q_read": (), "convolved": 0, "scanned": 0}
                    for n in range(BATCH)]
        square = {"last": None}

        def heads(ap, h=HEADS):
            return ap.rearrange("p (h c) -> p h c", h=h)

        def per_head(ap):
            return ap.unsqueeze(2).broadcast_to([P, HEADS, HDIM])

        def mamba(b):
            x = blk(b)
            batch, nth = divmod(b, BLK_PER_BATCH)
            first = nth == 0
            m_state, state, state_q = m_states[batch], states[batch], state_qs[batch]
            i_xa, xa, r_xa = yield from turn(m_xa)
            xa_ready = yield from run(layernorm("ma", x, xa, [xs_ready[b]], r_xa))
            i_xb, xb, r_xb = yield from turn(m_xb)
            xb_ready = yield from run(layernorm("mb", xa, xb, [xa_ready], r_xb))
            summed = pool("m_sum", lambda e: e.tensor_tensor(x, x, xa[:, :, :], ALU.add), xa_ready)
            i_xT, xT, r_xT = yield from turn(m_xT)
            tr, xT_ready = yield from run(to_channels("mx", lambda j: xb[:, j, :], xT[:, :], [xb_ready, L["ln_w"], L["ln_b"]],
                                                      r_xT, ln_w[:, 0:1], ln_b[:, 0:1]))
            read_by(m_xb, i_xb, tr)
            read_by(m_xa, i_xa, summed, xb_ready)
            i_sz, sz, r_sz = yield from turn(m_sz)
            i_dt, dtt, r_dt = yield from turn(m_dt)
            dt3 = dtt[:, :, :].rearrange("p k (j h) -> p k j h", h=HEADS)
            raw = dt3[:, 0, :, :]
            dt_parts, sz_parts = [], []
            for j in T4:
                i, bank, read = yield from take()
                s = pe("m_zdt", lambda e, bank=bank, j=j: e.matmul(
                    bank[:, 0:DINNER + HEADS], xT[:, j * P:(j + 1) * P], zdt_w[:, :], start=True, stop=True),
                    xT_ready, L["zdt_w"], *read)
                yield
                a = act("m_silu_z", lambda e, bank=bank, j=j: e.activation(sz[:, j, :], bank[:, 0:DINNER], ACT.Silu),
                        s, *r_sz)
                v = dve("m_dtraw", lambda e, bank=bank, j=j: e.tensor_tensor(
                    raw[:, j, :], bank[:, DINNER:DINNER + HEADS], dt_bias[:, :], ALU.add), s, a, L["dt_bias"], *r_dt)
                give(i, a, v)
            sz_ready, raw_ready = a, v
            yield
            while m_state["convolved"] < nth:
                yield None
            i_cv, cv, r_cv = yield from turn(m_cv)
            old_halo, new_halo = m_halo[batch][(b + 1) % 2], m_halo[batch][b % 2]
            convs, halos = [], []
            for c in range(XBC_CHUNKS):
                i_pre, pre, r_pre = yield from turn(m_pre)
                if first:
                    h_in = pool("m_halo0", lambda e, pre=pre: e.memset(pre[:, 0:halo], 0.0), *r_pre)
                else:
                    h_in = pool("m_halo", lambda e, pre=pre, c=c: e.tensor_copy(pre[:, 0:halo], old_halo[:, c, :]),
                                m_state["halos"][c], *r_pre)
                i, bank, read = yield from take()
                s = pe("m_xbc", lambda e, bank=bank, c=c: e.matmul(
                    bank[:, :], xbc_w[:, c * P:(c + 1) * P], xT[:, :], start=True, stop=True),
                    L["xbc_w"], *read)
                yield
                a0 = act("m_pre", lambda e, bank=bank, pre=pre: e.activation(
                    pre[:, halo:halo + BT], bank[:, :], ACT.Copy), s, *r_pre)
                a1 = act("m_tap", lambda e, bank=bank, c=c: e.activation(
                    cv[:, c, :], bank[:, :], ACT.Identity, scale=conv_w[:, c, halo:halo + 1],
                    bias=conv_b[:, c:c + 1]), L["conv_w"], L["conv_b"], *r_cv)
                give(i, a1)
                h_out = pool("m_halo_out", lambda e, pre=pre, c=c: e.tensor_copy(
                    new_halo[:, c, :], pre[:, BT:BT + halo]), a0, h_in)
                halos.append(h_out)
                v = a1
                for k in range(halo):
                    v = dve("m_conv", lambda e, k=k, c=c, pre=pre: e.scalar_tensor_tensor(
                        cv[:, c, :], pre[:, k:k + BT], conv_w[:, c, k:k + 1], cv[:, c, :],
                        ALU.mult, ALU.add), v, a0, h_in)
                read_by(m_pre, i_pre, v, h_out)
                convs.append(v)
                yield
            read_by(m_xT, i_xT, s)
            m_state["halos"] = halos
            m_state["convolved"] += 1
            cv_ready = []
            for c in range(XBC_CHUNKS):
                cv_ready.append(act("m_silu", lambda e, c=c: e.activation(cv[:, c, :], cv[:, c, :], ACT.Silu),
                                    convs[c]))
                yield
            row = lambda k: dtt[:, k, :]
            s = dve("m_sp", lambda e: e.tensor_scalar(row(1), row(0), -1.0, None, ALU.mult), raw_ready)
            s = dve("m_sp", lambda e: e.tensor_tensor(row(1), row(0), row(1), ALU.min), s)
            s = act("m_spexp", lambda e: e.activation(row(2), row(1), ACT.Exp), s)
            yield
            s = dve("m_sp", lambda e: e.tensor_scalar(row(3), row(2), 2.0, None, ALU.add), s)
            s = dve("m_sp", lambda e: e.reciprocal(row(4), row(3)), s)
            s = dve("m_sp", lambda e: e.tensor_tensor(row(5), row(2), row(4), ALU.mult), s)
            s = dve("m_sp", lambda e: e.tensor_tensor(row(6), row(5), row(5), ALU.mult), s)
            s = dve("m_sp", lambda e: e.tensor_scalar(row(7), row(6), ATANH[7], ATANH[6], ALU.mult, ALU.add), s)
            for k in (5, 4, 3, 2, 1, 0):
                s = dve("m_sp", lambda e: e.tensor_tensor(row(7), row(7), row(6), ALU.mult), s)
                s = dve("m_sp", lambda e, k=k: e.tensor_scalar(row(7), row(7), ATANH[k], None, ALU.add), s)
            s = dve("m_sp", lambda e: e.tensor_tensor(row(7), row(7), row(5), ALU.mult), s)
            dt_ready = dve("m_dt", lambda e: e.scalar_tensor_tensor(
                row(8), row(0), 0.0, row(7), ALU.max, ALU.add), s)
            dta_ready = dve("m_dta", lambda e: e.tensor_tensor(
                dt3[:, 9, :, :], dt3[:, 8, :, :], a_neg[:, :].unsqueeze(1).broadcast_to([P, 4, HEADS]), ALU.mult),
                dt_ready, L["a_neg"])
            dt, dta = row(8), row(9)
            yield
            i_ex, ex, r_ex = yield from turn(m_ex)
            i, bank, read = yield from take()

            def mm_sums(e):
                n = 4 * HEADS
                e.matmul(bank[:, 0:n], tri_incl[:, :], dta, start=True, stop=True)
                e.matmul(bank[:, n:2 * n], tri_strict[:, :], dta, start=True, stop=True)
                return e.matmul(bank[:, 2 * n:3 * n], ones[:, :], dta, start=True, stop=True)
            s = pe("m_sums", mm_sums, dta_ready, L["tri_incl"], L["tri_strict"], L["ones"], *read)
            ex_ready = act("m_exps", lambda e: e.activation(
                ex[:, :, :], bank[:, 0:12 * HEADS].rearrange("p (k n) -> p k n", k=3), ACT.Exp), s, *r_ex)
            give(i, ex_ready)
            yield
            dtr = dve("m_dtr", lambda e: e.tensor_tensor(row(10), dt, ex[:, 1, :], ALU.mult), ex_ready)
            i_g, g, r_g = yield from turn(m_g)
            i_rs, rs, r_rs = yield from turn(m_rs)
            squares = []
            while m_state["scanned"] < nth:
                yield None
            for j in T4:
                tok = slice(j * P, (j + 1) * P)
                hj = slice(j * HEADS, (j + 1) * HEADS)
                i_seg, seg, r_seg = yield from turn(m_seg)
                s_seg = pool("m_seg", lambda e, seg=seg, hj=hj: e.tensor_tensor(
                    seg[:, :, :], tri_incl[:, :].unsqueeze(1).broadcast_to([P, HEADS, P]),
                    dta[:, hj].unsqueeze(2).broadcast_to([P, HEADS, P]), ALU.mult), dta_ready, *r_seg)
                i_tp, tbank, t_read = yield from take()

                def tr(e, tbank=tbank, tok=tok):
                    for c in range(3):
                        last = e.transpose(tbank[:, c * P:(c + 1) * P], cv[:, c, tok], ident[:, :])
                    return last
                s_tr = pe("m_tr", tr, *cv_ready[0:3], *t_read)
                i_gb, gbank, g_read = yield from take()
                s_g = pe("m_G", lambda e, gbank=gbank, tok=tok: e.matmul(
                    gbank[:, 0:P], cv[:, CH_B, tok], cv[:, CH_C, tok], start=True, stop=True),
                    cv_ready[3], *g_read)
                yield
                i_xt, xt, r_xt = yield from turn(m_xt)
                xt_ready = act("m_xt", lambda e, xt=xt, tbank=tbank: e.activation(
                    xt[:, :], tbank[:, 0:3 * P], ACT.Copy), s_tr, *r_xt)
                give(i_tp, xt_ready)
                i_gm, gm, r_gm = yield from turn(m_gm)
                gm_ready = dve("m_gm", lambda e, gm=gm, gbank=gbank: e.tensor_tensor(
                    gm[:, :], gbank[:, 0:P], tri_incl[:, :], ALU.mult), s_g, *r_gm)
                give(i_gb, gm_ready)
                i_d, dbank, d_read = yield from take()
                s_d = pe("m_D", lambda e, dbank=dbank, seg=seg: e.matmul(
                    dbank[:, :], tri_strict[:, :], seg[:, :, :].rearrange("p h t -> p (h t)"),
                    start=True, stop=True), s_seg, *d_read)
                read_by(m_seg, i_seg, s_d)
                yield
                i_e, et, r_e = yield from turn(m_e)
                s = act("m_decay", lambda e, et=et, dbank=dbank: e.activation(
                    et[:, :, :], dbank[:, :].rearrange("p (h t) -> p h t", h=HEADS), ACT.Exp), s_d, *r_e)
                give(i_d, s)
                i_xd, xd, r_xd = yield from turn(m_xd)
                xh = heads(xt[:, 0:DINNER])
                s_xd = pool("m_xdt", lambda e, xd=xd, xh=xh, hj=hj: e.tensor_tensor(
                    heads(xd[:, 0, :]), xh, per_head(dt[:, hj]), ALU.mult), xt_ready, dt_ready, *r_xd)
                s_xs = pool("m_xds", lambda e, xd=xd, xh=xh, hj=hj: e.tensor_tensor(
                    heads(xd[:, 1, :]), xh, per_head(row(10)[:, hj]), ALU.mult), dtr)
                s_dx = pool("m_dx", lambda e, xd=xd, xh=xh: e.tensor_tensor(
                    heads(xd[:, 2, :]), xh, per_head(d_skip[:, :]), ALU.mult), L["d_skip"])
                yield
                m_ready = dve("m_M", lambda e, et=et, gm=gm: e.tensor_tensor(
                    et[:, :, :], et[:, :, :], gm[:, :].unsqueeze(1).broadcast_to([P, HEADS, P]), ALU.mult),
                    s, gm_ready)
                read_by(m_gm, i_gm, m_ready)
                yield
                start_of_batch = first and j == 0
                i_y, ybank, y_read = yield from take()
                old = state[m_state["k"] % 2]

                def mm_y(e, ybank=ybank, mt=et, xd=xd, tok=tok, old=old, start_of_batch=start_of_batch):
                    if not start_of_batch:
                        e.matmul(ybank[:, DINNER:2 * DINNER], cv[:, CH_C, tok], old[:, :], start=True, stop=True)
                    for h in range(HEADS):
                        c = slice(h * HDIM, (h + 1) * HDIM)
                        last = e.matmul(ybank[:, c], mt[:, h, :], xd[:, 0, c], start=True, stop=True)
                    return last
                s_y = pe("m_Y", mm_y, m_ready, s_xd, m_state["ready"] if not start_of_batch else None, *y_read)
                read_by(m_e, i_e, s_y)
                i_s, sbank, s_read = yield from take()
                s_st = pe("m_S", lambda e, sbank=sbank, xt=xt, xd=xd: e.matmul(
                    sbank[:, 0:DINNER], xt[:, 2 * P:3 * P], xd[:, 1, :], start=True, stop=True), s_xs, *s_read)
                new_k = (m_state["k"] + 1) % 2
                new = state[new_k]
                if start_of_batch:
                    st = dve("m_state", lambda e, new=new, sbank=sbank: e.tensor_copy(new[:, :], sbank[:, 0:DINNER]),
                             s_st, *m_state["read"][new_k])
                else:
                    sq = pool("m_stateq", lambda e, old=old, hj=hj: e.tensor_tensor(
                        heads(state_q[:, :]), heads(old[:, :]), per_head(ex[:, 2, hj]), ALU.mult),
                        m_state["ready"], ex_ready, *m_state["q_read"])
                    st = dve("m_state", lambda e, new=new, sbank=sbank: e.tensor_tensor(
                        new[:, :], state_q[:, :], sbank[:, 0:DINNER], ALU.add), s_st, sq, *m_state["read"][new_k])
                    m_state["q_read"] = (st,)
                    m_state["read"][m_state["k"] % 2] = (s_y, sq)
                m_state["ready"] = st
                m_state["k"] = new_k
                give(i_s, st)
                yield
                i_yy, yy, r_yy = yield from turn(m_y)
                s1 = dve("m_y1", lambda e, yy=yy, ybank=ybank, xd=xd: e.tensor_tensor(
                    yy[:, 0, :], ybank[:, 0:DINNER], xd[:, 2, :], ALU.add), s_y, s_dx, *r_yy)
                if not start_of_batch:
                    s2 = dve("m_y2", lambda e, yy=yy, ybank=ybank, hj=hj: e.tensor_tensor(
                        heads(yy[:, 1, :]), heads(ybank[:, DINNER:2 * DINNER]), per_head(ex[:, 0, hj]), ALU.mult),
                        ex_ready)
                    s3 = dve("m_y3", lambda e, yy=yy: e.tensor_tensor(
                        yy[:, 0, :], yy[:, 0, :], yy[:, 1, :], ALU.add), s1, s2)
                else:
                    s2, s3 = s1, s1
                give(i_y, s1, s2)
                read_by(m_xt, i_xt, s_st, s_dx)
                read_by(m_xd, i_xd, s_y, s_st, s1)
                s4 = dve("m_gated", lambda e, yy=yy, j=j: e.tensor_tensor(
                    g[:, j, :], yy[:, 0, :], sz[:, j, :], ALU.mult), s3, sz_ready, *r_g)
                read_by(m_y, i_yy, s4)
                squares.append(act("m_sq", lambda e, j=j: e.activation(
                    m_sq[:, :], g[:, j, :], ACT.Square, accum_out=rs[:, 0, j:j + 1]), s4, *r_rs,
                    square["last"]))
                square["last"] = squares[-1]
                yield
            m_state["scanned"] += 1
            read_by(m_cv, i_cv, s_y)
            read_by(m_sz, i_sz, s4)
            read_by(m_dt, i_dt, s_xs, s_seg)
            read_by(m_ex, i_ex, s2, sq if not start_of_batch else st)
            s = pool("m_ms", lambda e: e.tensor_scalar(rs[:, 1, :], rs[:, 0, :], 1.0 / DINNER, EPS, ALU.mult, ALU.add),
                     squares[-1])
            rstd_ready = pool("m_rstd", lambda e: e.tensor_tensor(rs[:, 2, :], rs[:, 1, :], neghalf[:, :], ALU.pow), s)
            i_gT, gT, r_gT = yield from turn(m_gT)
            for c in range(DINNER // P):
                tr, gT_ready = yield from run(to_channels(
                    "mg", lambda j, c=c: g[:, j, c * P:(c + 1) * P], gT[:, c, :], [s4, L["norm_w"]], r_gT,
                    norm_w[:, c:c + 1]))
            read_by(m_g, i_g, tr, squares[-1])
            i, bank, read = yield from take()

            def mm_out(e):
                for j in T4:
                    for c in range(DINNER // P):
                        last = e.matmul(bank[:, j * P:(j + 1) * P], gT[:, c, j * P:(j + 1) * P], out_w[:, c, :],
                                        start=(c == 0), stop=(c == DINNER // P - 1))
                return last
            s = pe("m_out", mm_out, gT_ready, L["out_w"], *read)
            read_by(m_gT, i_gT, s)
            yield

            def res(e):
                for j in T4:
                    last = e.scalar_tensor_tensor(x[:, j, :], bank[:, j * P:(j + 1) * P], rs[:, 2, j:j + 1],
                                                  x[:, j, :], ALU.mult, ALU.add)
                return last
            s = dve("m_res", res, s, rstd_ready, summed)
            give(i, s)
            read_by(m_rs, i_rs, s)
            xs_ready[b] = s
            yield

        f1_xn = buffers("f1_xn", [P, 4, DM])
        f1_xT = buffers("f1_xT", [P, BT])
        f1_g = buffers("f1_g", [P, 12, 4 * E1])
        f1_s = buffers("f1_s", [P, 8, 4])
        f1_w9 = buffers("f1_w9", [P, 3, 4, GATES])
        f1_w27 = buffers("f1_w27", [P, 4, PARTS, GATES], 2, BF16)
        f1_wT = buffers("f1_wT", [gate_rows, BT], 2, BF16)
        f1_ready = {}

        def ffn1_gates(b):
            x = blk(b)
            i_xn, xn, r_xn = yield from turn(f1_xn)
            normed = yield from run(layernorm("f1", x, xn, [xs_ready[b]], r_xn))
            i_xT, xT, r_xT = yield from turn(f1_xT)
            tr, xT_ready = yield from run(to_channels("f1x", lambda j: xn[:, j, :], xT[:, :], [normed], r_xT))
            read_by(f1_xn, i_xn, tr)
            i, bank, read = yield from take()
            logits = bank[:, 0:4 * GATES].rearrange("p (j e) -> p j e", e=GATES)

            def mm_gate(e):
                for j in T4:
                    last = e.matmul(logits[:, j, :], xT[:, j * P:(j + 1) * P], gate1[:, :], start=True, stop=True)
                return last
            s_l = pe("f1_gate", mm_gate, xT_ready, L["gate1"], *read)
            yield
            i_g, gt, r_g = yield from turn(f1_g)
            i_s, st, r_s = yield from turn(f1_s)
            i_w9, w9, r_w9 = yield from turn(f1_w9)
            col = lambda k: gt[:, k, :].rearrange("p (j e) -> p j e", e=E1)
            one = lambda k: st[:, k, :]
            wide = lambda k: one(k).unsqueeze(2).broadcast_to([P, 4, E1])
            keys = first_key[:, :].unsqueeze(1).broadcast_to([P, 4, E1])
            s = dve("f1_max", lambda e: e.tensor_reduce(one(0), logits[:, :, 0:E1], AX.X, ALU.max), s_l, *r_s, *r_g)
            s = dve("f1_sub", lambda e: e.tensor_tensor(col(0), logits[:, :, 0:E1], wide(0), ALU.subtract), s)
            s_sg = act("f1_sgexp", lambda e: e.activation(one(7), logits[:, :, E1], ACT.Exp, scale=-1.0), s_l, s, *r_s)
            yield
            give(i, s, s_sg)
            s = act("f1_exp", lambda e: e.activation(gt[:, 1, :], gt[:, 0, :], ACT.Exp), s)
            yield
            s = dve("f1_r", lambda e: e.tensor_reduce(one(1), col(1), AX.X, ALU.add), s)
            s = dve("f1_r", lambda e: e.reciprocal(one(2), one(1)), s)
            s = dve("f1_r", lambda e: e.tensor_tensor(col(2), col(1), wide(2), ALU.mult), s)
            chosen = []
            cur = 2
            for k in range(2):
                s = dve("f1_r", lambda e, c=cur, k=k: e.tensor_reduce(one(3 + k), col(c), AX.X, ALU.max), s)
                s = dve("f1_r", lambda e, c=cur, k=k: e.tensor_tensor(col(3), col(c), wide(3 + k), ALU.is_equal), s)
                s = dve("f1_r", lambda e: e.tensor_tensor(col(4), col(3), keys, ALU.mult), s, L["first_key"])
                s = dve("f1_r", lambda e, k=k: e.tensor_reduce(one(5 + k), col(4), AX.X, ALU.max), s)
                s = dve("f1_r", lambda e, k=k: e.tensor_tensor(col(5 + k), col(4), wide(5 + k), ALU.is_equal), s)
                if k == 0:
                    s = dve("f1_r", lambda e: e.scalar_tensor_tensor(
                        col(7), col(5), -2.0, col(2), ALU.mult, ALU.add), s)
                    cur = 7
                yield
            s = dve("f1_r", lambda e: e.tensor_tensor(col(8), col(5), col(6), ALU.add), s)
            s = dve("f1_r", lambda e: e.tensor_tensor(w9[:, 0, :, 0:E1], col(8), col(2), ALU.mult), s, *r_w9)
            s = dve("f1_r", lambda e: e.tensor_scalar(one(7), one(7), 1.0, None, ALU.add), s, s_sg)
            s = dve("f1_r", lambda e: e.reciprocal(w9[:, 0, :, E1], one(7)), s)
            yield
            i_w, w27, r_w = yield from turn(f1_w27)
            s = dve("f1_r", lambda e: e.tensor_copy(w27[:, :, 0, :], w9[:, 0, :, :]), s, *r_w)
            s = dve("f1_r", lambda e: e.tensor_tensor(w9[:, 1, :, :], w9[:, 0, :, :], w27[:, :, 0, :], ALU.subtract), s)
            s = dve("f1_r", lambda e: e.tensor_copy(w27[:, :, 1, :], w9[:, 1, :, :]), s)
            s = dve("f1_r", lambda e: e.tensor_tensor(w9[:, 2, :, :], w9[:, 1, :, :], w27[:, :, 1, :], ALU.subtract), s)
            s = dve("f1_w27", lambda e: e.tensor_copy(w27[:, :, 2, :], w9[:, 2, :, :]), s)
            for bufs, n in ((f1_g, i_g), (f1_s, i_s), (f1_w9, i_w9)):
                read_by(bufs, n, s)
            yield
            i, bank, read = yield from take()
            bankb = bank[:, :].bitcast(BF16)

            def tr_w(e):
                for j in T4:
                    last = e.transpose(bankb[0:gate_rows, j * P:(j + 1) * P],
                                       w27[:, j, :, :].rearrange("p a e -> p (a e)"), identb[:, :])
                return last
            s = pe("f1_wtr", tr_w, s, L["identb"], *read)
            read_by(f1_w27, i_w, s)
            i_wT, wT, r_wT = yield from turn(f1_wT)
            wT_ready = act("f1_wT", lambda e: e.activation(wT[:, :], bankb[0:gate_rows, 0:BT], ACT.Copy), s, *r_wT)
            give(i, wT_ready)
            f1_ready[b] = (xT, xT_ready, i_xT, wT, wT_ready, i_wT)
            yield

        f1_sg = buffers("f1_sg", [P, HALF], 2)
        f1_t = buffers("f1_t", [P, HALF], 2)
        f1_h = buffers("f1_h", [P, HALF], 3)
        f1_o = buffers("f1_o", [P, BT], 1)
        gu_read, once = [(), ()], {"wb": (), "down": (), "busy": False}
        f1_count = {"k": 0}
        LAG = 2

        def ffn1_experts(b, store):
            x = blk(b)
            while once["busy"]:
                yield None
            once["busy"] = True
            xT, xT_ready, i_xT, wT, wT_ready, i_wT = f1_ready[b]
            for half in range(2):
                tok = slice(half * HALF, (half + 1) * HALF)
                h_ready = {}
                down = down_bank[:, tok]
                for c in range(NCH + LAG):
                    if c < NCH:
                        k = f1_count["k"] % 2
                        f1_count["k"] += 1
                        ch = slice(c * P, (c + 1) * P)
                        gu = gu_bank[k]

                        def mm_gu(e, gu=gu, ch=ch, tok=tok):
                            e.matmul(gu[:, 0:HALF], g_w[:, ch], xT[:, tok], start=True, stop=True)
                            return e.matmul(gu[:, HALF:2 * HALF], u_w[:, ch], xT[:, tok], start=True, stop=True)
                        s_gu = pe("f1_gu", mm_gu, xT_ready, L["g_w"], L["u_w"], *gu_read[k])
                    if c >= LAG:
                        n = c - LAG
                        i_h, h, ready = h_ready[n]
                        s_d = pe("f1_down", lambda e, h=h, n=n, down=down: e.matmul(
                            down, d_w[:, n, :], h[:, :], start=(n == 0), stop=(n == NCH - 1)),
                            ready, L["d_w"], *(once["down"] if n == 0 and half == 0 else ()))
                        read_by(f1_h, i_h, s_d)
                    if c < NCH:
                        s_wb = pe("f1_wb", lambda e, ch=ch, tok=tok: e.matmul(
                            wb_bank[:, 0:HALF], sel[:, ch], wT[:, tok], start=True, stop=True),
                            wT_ready, L["sel"], *once["wb"])
                        i_sg, sg, r_sg = yield from turn(f1_sg)
                        a = act("f1_silu", lambda e, sg=sg, gu=gu: e.activation(sg[:, :], gu[:, 0:HALF], ACT.Silu),
                                s_gu, *r_sg)
                        i_t, t, r_t = yield from turn(f1_t)
                        v = dve("f1_su", lambda e, sg=sg, gu=gu, t=t: e.tensor_tensor(
                            t[:, :], sg[:, :], gu[:, HALF:2 * HALF], ALU.mult), a, *r_t)
                        gu_read[k] = (a, v)
                        read_by(f1_sg, i_sg, v)
                        i_h, h, r_h = yield from turn(f1_h)
                        v = dve("f1_h", lambda e, t=t, h=h: e.tensor_tensor(
                            h[:, :], t[:, :], wb_bank[:, 0:HALF], ALU.mult), v, s_wb, *r_h)
                        once["wb"] = (v,)
                        read_by(f1_t, i_t, v)
                        h_ready[c] = (i_h, h, v)
                    yield
            read_by(f1_xT, i_xT, s_gu)
            read_by(f1_wT, i_wT, s_wb)
            i_o, o, r_o = yield from turn(f1_o)
            o_ready = act("f1_o", lambda e: e.activation(o[:, :], down_bank[:, :], ACT.Copy), s_d, *r_o)
            once["down"] = (o_ready,)
            once["busy"] = False
            yield
            i, bank, read = yield from take()

            def tr(e):
                for j in T4:
                    last = e.transpose(bank[:, j * P:(j + 1) * P], o[:, j * P:(j + 1) * P], ident[:, :])
                return last
            s = pe("f1_otr", tr, o_ready, *read)
            read_by(f1_o, i_o, s)
            yield
            s = dve("f1_res", lambda e: e.scalar_tensor_tensor(
                x, bank[:, :].rearrange("p (j c) -> p j c", c=DM), 0.5, x, ALU.mult, ALU.add), s)
            give(i, s)
            xs_ready[b] = s
            if store:
                t0 = b * TILES_PER_BLOCK
                q.step("sync", "store", lambda e: e.dma_start(out_tiles[:, t0:t0 + TILES_PER_BLOCK, :], x), s, inc=16)

        out_tiles = out.rearrange("(t p) c -> p t c", p=P)

        a_xn = buffers("a_xn", [P, 4, DM], 1)
        a_xT = buffers("a_xT", [P, BT])
        VW = QKV + 1
        a_qkv = buffers("a_qkv", [P, 4, VW], 2)
        a_q = [sb(f"a_q{b}", [P, 4, DM]) for b in range(BLK_PER_BATCH)]
        a_st = buffers("a_st", [P, 3, 4 * 2 * AHEADS], 1)
        a_ctx = sb("a_ctx", [P, DM + 1])
        a_cm = sb("a_cm", [P, DM + AHEADS])
        a_qT = buffers("a_qT", [P, BT], 1)
        a_o = buffers("a_o", [P, 4, DM], 1)
        a_oT = buffers("a_oT", [P, BT], 1)
        a_di = buffers("a_di", [P, 4, AHEADS])
        att = {"q_read": [()] * BLK_PER_BATCH, "ctx_read": (), "cm_read": (), "ctx": None, "ones": [], "q": {}}
        for t in a_qkv["tiles"]:
            att["ones"].append(pool("a_ones", lambda e, t=t: e.memset(t[:, :, QKV:VW], 1.0)))

        def attn_kv(b):
            x = blk(b)
            n = b % BLK_PER_BATCH
            i_xn, xn, r_xn = yield from turn(a_xn)
            normed = yield from run(layernorm("at", x, xn, [xs_ready[b]], r_xn))
            i_xT, xT, r_xT = yield from turn(a_xT)
            tr, xT_ready = yield from run(to_channels("atx", lambda j: xn[:, j, :], xT[:, :], [normed], r_xT))
            read_by(a_xn, i_xn, tr)
            i_k, qkv, r_k = yield from turn(a_qkv)
            for j in T4:
                i, bank, read = yield from take()
                s = pe("a_qkv", lambda e, bank=bank, j=j: e.matmul(
                    bank[:, 0:QKV], xT[:, j * P:(j + 1) * P], qkv_w[:, :], start=True, stop=True),
                    xT_ready, L["qkv_w"], *read)
                v = dve("a_bias", lambda e, bank=bank, j=j: e.tensor_tensor(
                    qkv[:, j, 0:QKV], bank[:, 0:QKV], qkv_b[:, :], ALU.add), s, L["qkv_b"], *r_k)
                give(i, v)
                yield
            read_by(a_xT, i_xT, s)
            i_st, st, r_st = yield from turn(a_st)
            G = 2 * AHEADS
            qk = lambda j: qkv[:, j, 0:2 * DM].rearrange("p (g c) -> p g c", c=ADIM)
            sj = lambda k, j: st[:, k, j * G:(j + 1) * G]
            wide = lambda k, j: sj(k, j).unsqueeze(2).broadcast_to([P, G, ADIM])

            def each(f):
                def emit(e):
                    for j in T4:
                        last = f(e, j)
                    return last
                return emit
            s = dve("a_max", each(lambda e, j: e.tensor_reduce(sj(0, j), qk(j), AX.X, ALU.max)), v, *r_st)
            s = dve("a_sub", each(lambda e, j: e.tensor_tensor(qk(j), qk(j), wide(0, j), ALU.subtract)), s)
            yield
            s = act("a_exp", lambda e: e.activation(qkv[:, :, 0:2 * DM], qkv[:, :, 0:2 * DM], ACT.Exp), s)
            yield
            s = dve("a_sumd", each(lambda e, j: e.tensor_reduce(sj(1, j), qk(j), AX.X, ALU.add)), s)
            s = dve("a_rec", lambda e: e.reciprocal(st[:, 2, :], st[:, 1, :]), s)
            k_part = lambda j: qkv[:, j, DM:2 * DM].rearrange("p (g c) -> p g c", c=ADIM)
            wk = lambda j: sj(2, j)[:, AHEADS:].unsqueeze(2).broadcast_to([P, AHEADS, ADIM])
            wq = lambda j: sj(2, j)[:, :AHEADS].unsqueeze(2).broadcast_to([P, AHEADS, ADIM])
            k_ready = dve("a_k", each(lambda e, j: e.tensor_tensor(k_part(j), k_part(j), wk(j), ALU.mult)), s)
            qn = a_q[n]
            q_ready = dve("a_q", each(lambda e, j: e.tensor_tensor(
                qn[:, j, :].rearrange("p (g c) -> p g c", c=ADIM),
                qkv[:, j, 0:DM].rearrange("p (g c) -> p g c", c=ADIM), wq(j), ALU.mult)), s, *att["q_read"][n])
            att["q"][b] = q_ready
            read_by(a_st, i_st, q_ready)
            yield
            i, bank, read = yield from take()

            def mm_ctx(e):
                for j in T4:
                    last = e.matmul(bank[:, 0:DM + 1], qkv[:, j, DM:2 * DM], qkv[:, j, 2 * DM:VW],
                                    start=(j == 0), stop=(j == 3))
                return last
            s = pe("a_ctx", mm_ctx, k_ready, att["ones"][i_k], *read)
            read_by(a_qkv, i_k, s, q_ready)
            if n == 0:
                s = dve("a_ctxsum", lambda e: e.tensor_copy(a_ctx[:, :], bank[:, 0:DM + 1]), s, *att["ctx_read"])
            else:
                s = dve("a_ctxsum", lambda e: e.tensor_tensor(a_ctx[:, :], a_ctx[:, :], bank[:, 0:DM + 1], ALU.add),
                        s, att["ctx"])
            give(i, s)
            att["ctx"] = s
            if n == BLK_PER_BATCH - 1:
                s1 = dve("a_cm", lambda e: e.tensor_tensor(
                    a_cm[:, 0:DM].rearrange("p (h c) -> p h c", c=ADIM),
                    a_ctx[:, 0:DM].rearrange("p (h c) -> p h c", c=ADIM),
                    head_mask[:, :].unsqueeze(2).broadcast_to([P, AHEADS, ADIM]), ALU.mult),
                    s, L["head_mask"], *att["cm_read"])
                s1 = dve("a_cm", lambda e: e.tensor_scalar(
                    a_cm[:, DM:DM + AHEADS], head_mask[:, :], a_ctx[:, DM:DM + 1], None, ALU.mult), s)
                att["ctx_read"] = (s1,)
                att["cm"] = s1
                att["cm_read"] = ()
            yield

        def attn_out(b):
            x = blk(b)
            n = b % BLK_PER_BATCH
            qn = a_q[n]
            i_qT, qT, r_qT = yield from turn(a_qT)
            tr, qT_ready = yield from run(to_channels("aq", lambda j: qn[:, j, :], qT[:, :], [att["q"][b]], r_qT))
            biased = pool("a_bp", lambda e: e.tensor_tensor(
                x, x, p_b[:, :].unsqueeze(1).broadcast_to([P, 4, DM]), ALU.add), xs_ready[b], L["p_b"])
            i_n, nbank, n_read = yield from take()
            i_d, dbank, d_read = yield from take()

            def mm(e):
                for j in T4:
                    lhs = qT[:, j * P:(j + 1) * P]
                    e.matmul(nbank[:, j * P:(j + 1) * P], lhs, a_cm[:, 0:DM], start=True, stop=True)
                    last = e.matmul(dbank[:, j * AHEADS:(j + 1) * AHEADS], lhs, a_cm[:, DM:DM + AHEADS],
                                    start=True, stop=True)
                return last
            s = pe("a_num", mm, qT_ready, att["cm"], *n_read, *d_read)
            att["cm_read"] = att["cm_read"] + (s,)
            read_by(a_qT, i_qT, s)
            yield
            i_di, di, r_di = yield from turn(a_di)
            v = dve("a_dinv", lambda e: e.reciprocal(
                di[:, :, :], dbank[:, 0:4 * AHEADS].rearrange("p (j h) -> p j h", h=AHEADS)), s, *r_di)
            give(i_d, v)
            i_o, o, r_o = yield from turn(a_o)

            def div(e):
                for j in T4:
                    last = e.tensor_tensor(o[:, j, :].rearrange("p (h c) -> p h c", c=ADIM),
                                           nbank[:, j * P:(j + 1) * P].rearrange("p (h c) -> p h c", c=ADIM),
                                           di[:, j, :].unsqueeze(2).broadcast_to([P, AHEADS, ADIM]), ALU.mult)
                return last
            v = dve("a_div", div, v, *r_o)
            give(i_n, v)
            read_by(a_di, i_di, v)
            yield
            v = pool("a_addq", lambda e: e.tensor_tensor(o[:, :, :], o[:, :, :], qn[:, :, :], ALU.add), v)
            att["q_read"][n] = (v, tr)
            yield
            i_oT, oT, r_oT = yield from turn(a_oT)
            tr, oT_ready = yield from run(to_channels("ao", lambda j: o[:, j, :], oT[:, :], [v], r_oT))
            read_by(a_o, i_o, tr)
            i, bank, read = yield from take()

            def mm_p(e):
                for j in T4:
                    last = e.matmul(bank[:, j * P:(j + 1) * P], oT[:, j * P:(j + 1) * P], p_w[:, :],
                                    start=True, stop=True)
                return last
            s = pe("a_proj", mm_p, oT_ready, L["p_w"], *read)
            read_by(a_oT, i_oT, s)
            yield
            s = dve("a_res", lambda e: e.tensor_tensor(
                x, bank[:, :].rearrange("p (j c) -> p j c", c=DM), x, ALU.add), s, biased)
            give(i, s)
            xs_ready[b] = s
            yield

        for b in range(NBLK):
            xs_ready[b] = loaded_x[b]

        def chain(*gens):
            for g in gens:
                yield from g()

        def front(b):
            return chain(lambda: ffn0(b), lambda: mamba(b), lambda: ffn0(b), lambda: ffn1_gates(b))

        def back(b):
            return chain(lambda: attn_out(b), lambda: ffn1_gates(b))

        tasks, done = [], set()
        H = BLK_PER_BATCH

        def task(name, gen, *after):
            tasks.append((name, gen, after))

        for n, b in enumerate(ORDER):
            task(("front", b), lambda b=b: front(b), *([("first", ORDER[n - 2])] if n > 1 else []))
            task(("first", b), lambda b=b: ffn1_experts(b, False), ("front", b))
            task(("kv", b), lambda b=b: attn_kv(b), ("first", b), *([("kv", b - 1)] if b % H else []),
                 *([("back", b - H)] if b >= H else []))
        for n, b in enumerate(ORDER):
            last = b // H * H + H - 1
            task(("back", b), lambda b=b: back(b), ("kv", last), *([("second", ORDER[n - 2])] if n > 1 else []))
            task(("second", b), lambda b=b: ffn1_experts(b, True), ("back", b))
        active = []
        while tasks or active:
            for t in list(tasks):
                if len(active) < ACTIVE and all(a in done for a in t[2]):
                    tasks.remove(t)
                    active.append((t[0], t[1]()))
                    done.add(t[0] + ("started",))
            before = sum(q.count.values())
            for name, gen in list(active):
                for _ in range(STEPS.get(name[0], 1)):
                    if next(gen, "end") == "end":
                        active.remove((name, gen))
                        done.add(name)
                        break
            assert active == [] or sum(q.count.values()) > before, [n for n, _ in active]
        q.wait("sync", ("sync_store", q.count["sync_store"]))


ACTIVE = 4
STEPS = {}
ORDER = range(NBLK)


def constants():
    u = np.arange(P)
    channel = np.arange(NCH * P)
    gate = np.where(channel < E1 * IEXP, channel // IEXP, np.where(channel < CHANNELS, E1, -1))
    return {
        "ident": np.eye(P, dtype=np.float32),
        "tri_incl": (u[:, None] <= u[None, :]).astype(np.float32),
        "tri_strict": (u[:, None] > u[None, :]).astype(np.float32),
        "head_mask": (u[:, None] // ADIM == np.arange(AHEADS)[None, :]).astype(np.float32),
        "first_key": (E1 - np.arange(E1, dtype=np.float32))[None, :],
        "sel": (np.tile(np.arange(GATES), PARTS)[:, None] == gate[None, :]).astype(np.float32),
    }


def kernel(**inputs):
    import concourse.bacc as bacc
    from concourse.bass_utils import run_bass_kernel_spmd

    i = {k: np.asarray(v) for k, v in inputs.items()}
    in_proj = i["L0_attn_in_proj_w"]
    conv = DINNER + 2 * DSTATE
    pad = NCH * P - CHANNELS
    gu = i["L1_ffn_experts_gate_up"]
    zero = np.zeros((pad, DM), np.float32)
    rows_g = np.concatenate([gu[:, :IEXP].reshape(-1, DM), i["L1_ffn_shared_gate_w"], zero])
    rows_u = np.concatenate([gu[:, IEXP:].reshape(-1, DM), i["L1_ffn_shared_up_w"], zero])
    rows_d = np.concatenate([i["L1_ffn_experts_down"].transpose(0, 2, 1).reshape(-1, DM),
                             i["L1_ffn_shared_down_w"].T, zero])
    arrays = {
        "x": i["L0_attn_x"].reshape(-1, DM),
        "w0": i["L0_ffn_weight"].T,
        "u0": i["L0_ffn_lora_U"].reshape(-1, DM).T,
        "gate0": i["L0_ffn_gate_w"].T,
        "v0": i["L0_ffn_lora_V"].transpose(0, 2, 1).reshape(-1, DM),
        "xbc_w": in_proj[DINNER:DINNER + conv].T,
        "zdt_w": np.concatenate([in_proj[:DINNER], in_proj[DINNER + conv:]]).T,
        "conv_w": i["L0_attn_conv_w"].reshape(XBC_CHUNKS, P, DCONV).transpose(1, 0, 2),
        "conv_b": i["L0_attn_conv_b"].reshape(XBC_CHUNKS, P).T,
        "ln_w": i["L0_attn_ln_w"][:, None],
        "ln_b": i["L0_attn_ln_b"][:, None],
        "dt_bias": i["L0_attn_dt_bias"][None, :],
        "a_log": i["L0_attn_A_log"][None, :],
        "d_skip": i["L0_attn_D"][None, :],
        "norm_w": i["L0_attn_norm_w"].reshape(-1, P).T,
        "out_w": i["L0_attn_out_proj_w"].T.reshape(-1, P, DM).transpose(1, 0, 2),
        "g_w": rows_g.T,
        "u_w": rows_u.T,
        "d_w": rows_d.reshape(NCH, P, DM).transpose(1, 0, 2),
        "gate1": np.concatenate([i["L1_ffn_gate_w"], i["L1_ffn_shared_expert_gate_w"]]).T,
        "qkv_w": np.concatenate([i["L1_attn_Wq"], i["L1_attn_Wk"], i["L1_attn_Wv"]]).T,
        "qkv_b": np.concatenate([i["L1_attn_bq"], i["L1_attn_bk"], i["L1_attn_bv"]])[None, :],
        "p_w": i["L1_attn_Wp"].T,
        "p_b": i["L1_attn_bp"][None, :],
    }
    arrays.update(constants())
    arrays = {f"in_{k}": np.ascontiguousarray(v) for k, v in arrays.items()}
    nc = bacc.Bacc("TRN2", target_bir_lowering=False, num_devices=1)
    d = {k[3:]: nc.dram_tensor(k, v.shape, mybir.dt.from_np(v.dtype), kind="ExternalInput").ap()
         for k, v in arrays.items()}
    out = nc.dram_tensor("out", (BATCH * SEQ, DM), F32, kind="ExternalOutput").ap()
    build(nc, d, out)
    r = run_bass_kernel_spmd(nc, [arrays], core_ids=[0])
    return r.results[0]["out"].reshape(BATCH, SEQ, DM)
```

```python
from contextlib import ExitStack

import numpy as np

import concourse.bass as bass
import concourse.mybir as mybir
from concourse.alu_op_type import AluOpType as ALU

ACT = mybir.ActivationFunctionType
F32 = mybir.dt.float32
BF16 = mybir.dt.bfloat16
U32 = mybir.dt.uint32
I32 = mybir.dt.int32
AX = mybir.AxisListType

P = 128
BATCH, SEQ, DM = 2, 2048, 128
TILES_PER_BLOCK = 4
BT = TILES_PER_BLOCK * P
NBLK = BATCH * SEQ // BT
BLK_PER_BATCH = SEQ // BT
E0, RANK = 8, 16
HEADS, HDIM, DSTATE, DCONV = 4, 64, 128, 4
DINNER = HEADS * HDIM
XBC_CHUNKS = (DINNER + 2 * DSTATE) // P
CH_B, CH_C = DINNER // P, DINNER // P + 1
E1, IEXP, ISHARED = 8, 176, 352
TOPK = 2
IHALF = IEXP // 2
SCH = 3
SCW = -(-ISHARED // (2 * SCH)) * 2
GATES = E1 + 1
GROUPS = [[0, 1], [2, 3], [4, 5], [6, 7]]
GB = len(GROUPS[0])
NT = GB * TILES_PER_BLOCK
MAXT = (TOPK * NT * P + E1 * (P - 1)) // P
NGROUP = len(GROUPS)
AHEADS, ADIM = 16, 8
QKV = 3 * DM
EPS = 1e-5
ATANH = [2.0 / (2 * k + 1) for k in range(8)]


ACTIVE = 10
LIMIT = {"experts": 4}
WORK = 20
WAITING = "waiting"

COST = {
    "tensor": {
        "a_ctx": 1.72, "a_num": 0.96, "a_proj": 0.86, "a_qkv": 0.98, "e_down": 0.96, "e_gu": 0.71, "e_tr": 0.52,
        "e_trh": 0.25, "f0_down": 1.28, "f0_gate": 0.08, "f0_out": 2.23, "f1_gate": 0.09, "f1_rank": 0.2,
        "f1_sd": 2.82, "f1_sg": 0.97, "f1_su": 0.92, "m_D": 1.19, "m_G": 0.3, "m_S": 0.63, "m_Y": 1.15,
        "m_out": 1.71, "m_sums": 0.15, "m_tr": 0.47, "m_xbc": 0.93, "m_zdt": 0.6, "turn": 0.66,
    },
    "vector": {
        "a_bias": 0.47, "a_cm": 0.17, "a_ctxsum": 0.2, "a_dinv": 0.47, "a_div": 0.81, "a_k": 0.81, "a_max": 1.34,
        "a_neg": 0.07, "a_q": 0.81, "a_rec": 0.87, "a_res": 0.6, "a_sub": 1.34, "a_sumd": 1.34, "e_h": 0.25,
        "e_y": 0.58, "f0_gates": 0.1, "f0_max": 0.1, "f0_rec": 0.09, "f0_res": 0.6, "f0_sub": 0.1, "f0_sum": 0.1,
        "f0_tg": 0.81, "f1_add": 1.05, "f1_any": 0.1, "f1_max": 0.1, "f1_q": 0.15, "f1_r": 0.09, "f1_sh": 0.6,
        "f1_slot": 0.09, "f1_sres": 1.05, "f1_sub": 0.1, "ln_aggr": 0.3, "ln_stats": 0.81,
        "m_M": 0.6, "m_conv": 0.66, "m_dt": 0.09, "m_dta": 0.09, "m_dtr": 0.09, "m_dtraw": 0.07, 
        "m_gm": 0.2, "m_res": 1.05, "m_sp": 0.09, "m_state": 0.33, "m_y1": 0.34, "m_y2": 0.34, "m_y3": 0.34,
    },
    "scalar": {
        "a_exp": 0.38, "e_hT": 0.29, "e_silu": 0.37, "e_xT": 0.38, "f0_exp": 0.39, "f1_exp": 0.43,
        "f1_sgexp": 0.36, "f1_ssilu": 0.38, "m_decay": 0.36, "ln_norm": 1.3, "turned": 0.5, "m_exps": 0.43,
        "m_pre": 0.45, "m_silu": 0.35,
        "m_silu_z": 0.46, "m_spexp": 0.19, "m_sq": 0.4, "m_tap": 0.48, "m_xt": 0.43, "turned": 0.4,
    },
    "gpsimd": {
        "a_addq": 1.23, "a_bp": 1.23, "a_ones": 0.04, "gather": 1.04, "ln_rstd": 0.96, "ln_veps": 0.19,
        "m_dx": 0.57, "m_halo": 0.13, "m_halo0": 0.04, "m_halo_out": 0.13, "m_gated": 0.57,
        "m_ms": 0.16, "m_rstd": 0.96,
        "m_seg": 1.0, "m_stateq": 0.57, "m_sum": 1.23, "m_xds": 0.57, "m_xdt": 0.57, "scatter": 1.04,
        "tri_b": 0.55,
    },
}
OTHER_COST, DMA_LATENCY, TABLE_LOAD, LATENCY = 0.1, 2.5, 1.3, 0.15


class Steps:

    def __init__(self, nc, ctx):
        self.nc, self.ctx = nc, ctx
        self.engine = {"tensor": nc.tensor, "vector": nc.vector, "scalar": nc.scalar, "gpsimd": nc.gpsimd,
                       "sync": nc.sync}
        self.sems, self.count, self.waited = {}, {}, {}
        self.finish, self.free, self.table, self.last = {}, {}, None, 0.0

    def wait(self, engine, *waits):
        for sem, value in waits:
            if self.waited.get((engine, sem), 0) < value:
                self.waited[(engine, sem)] = value
                self.engine[engine].wait_ge(self.sems[sem], value)

    def step(self, engine, name, emit, *waits, inc=1):
        key = f"{engine}_{name}" if inc > 1 else f"{engine}_{name.split('_')[0]}"
        if key not in self.sems:
            self.sems[key] = self.ctx.enter_context(self.nc.semaphore(key))
            self.count[key] = 0
        self.wait(engine, *(w for w in waits if w is not None))
        emit(self.engine[engine]).then_inc(self.sems[key], inc)
        self.count[key] += inc
        done = key, self.count[key]
        self.estimate(engine, name, waits, done, inc)
        return done

    def estimate(self, engine, name, waits, done, inc):
        cost = COST.get(engine, {}).get(name.rstrip("0123"), OTHER_COST)
        if engine == "scalar":
            table = "silu" if "silu" in name else "exp" if "exp" in name or name == "m_decay" else self.table
            cost += TABLE_LOAD if table != self.table else 0
            self.table = table
        start = max([self.free.get(engine, 0.0)] + [self.finish[w] for w in waits if w is not None])
        self.free[engine] = start + cost
        self.finish[done] = start + cost + (DMA_LATENCY if inc > 1 else LATENCY)
        self.last = start + cost if inc > 1 else self.finish[done]


def build(nc, d, out):
    with ExitStack() as ctx:
        q = Steps(nc, ctx)

        def sb(name, shape, dt=F32):
            return ctx.enter_context(nc.sbuf_tensor(name, shape, dt))

        def pe(name, emit, *w):
            return q.step("tensor", name, emit, *w)

        def dve(name, emit, *w):
            return q.step("vector", name, emit, *w)

        def act(name, emit, *w):
            return q.step("scalar", name, emit, *w)

        def pool(name, emit, *w):
            return q.step("gpsimd", name, emit, *w)

        def load(name, *copies, engine="sync"):
            for dst, src in copies:
                t = q.step(engine, "load_" + name, lambda e, dst=dst, src=src: e.dma_start(dst, src), inc=16)
            return t

        xs = sb("xs", [P, NBLK * TILES_PER_BLOCK, DM])
        ident = sb("ident", [P, P])
        tri_incl = sb("tri_incl", [P, P])
        tri_strict = sb("tri_strict", [P, P])
        ones = sb("ones", [P, P])
        head_mask = sb("head_mask", [P, AHEADS])
        first_key = sb("first_key", [P, E1])
        tri_b = sb("tri_b", [P, P], BF16)
        ones_b = sb("ones_b", [P, P], BF16)
        below = sb("below", [P, E1, E1])
        tile_start = sb("tile_start", [P, NT])
        slot_tile = sb("slot_tile", [P, MAXT])
        neghalf = sb("neghalf", [P, TILES_PER_BLOCK])

        w0 = sb("w0", [P, DM])
        u0 = sb("u0", [P, E0 * RANK])
        gate0 = sb("gate0", [P, E0])
        v0 = sb("v0", [P, DM])
        xbc_w = sb("xbc_w", [P, XBC_CHUNKS * P])
        zdt_w = sb("zdt_w", [P, DINNER + HEADS])
        conv_w = sb("conv_w", [P, XBC_CHUNKS, DCONV])
        conv_b = sb("conv_b", [P, XBC_CHUNKS])
        ln_w = sb("ln_w", [P, 1])
        ln_b = sb("ln_b", [P, 1])
        dt_bias = sb("dt_bias", [P, HEADS])
        a_log = sb("a_log", [P, HEADS])
        a_neg = sb("a_neg", [P, HEADS])
        d_skip = sb("d_skip", [P, HEADS])
        norm_w = sb("norm_w", [P, DINNER // P])
        out_w = sb("out_w", [P, DINNER // P, DM])
        gu_w = sb("gu_w", [P, E1 * 2 * IEXP])
        d_w = sb("d_w", [IHALF, E1 * 2 * DM])
        sg_w = sb("sg_w", [P, SCH * SCW])
        su_w = sb("su_w", [P, SCH * SCW])
        sd_w = sb("sd_w", [SCW, SCH, DM])
        gate1 = sb("gate1", [P, GATES])
        qkv_w = sb("qkv_w", [P, QKV])
        qkv_b = sb("qkv_b", [P, QKV])
        p_w = sb("p_w", [P, DM])
        p_b = sb("p_b", [P, DM])

        bank_tiles = [ctx.enter_context(nc.psum_tensor(f"bank{i}", [P, 512], F32)) for i in range(8)]
        def store_of(tiles):
            return {"tiles": tiles, "free": [(i, ()) for i in range(len(tiles))]}

        def buffers(name, shape, n=2, dt=F32):
            return store_of([sb(f"{name}{i}", shape, dt) for i in range(n)])

        def turn(bufs):
            while not bufs["free"]:
                yield WAITING
            i, readers = bufs["free"].pop(0)
            return i, bufs["tiles"][i], readers

        def read_by(bufs, i, *readers):
            bufs["free"].append((i, readers))

        banks = store_of(bank_tiles)

        halo = DCONV - 1
        work_wide = buffers("work", [P, halo + BT], WORK)
        work = {"tiles": [t[:, 0:BT] for t in work_wide["tiles"]], "free": work_wide["free"]}
        work4 = {"tiles": [t.rearrange("p (j c) -> p j c", j=TILES_PER_BLOCK) for t in work["tiles"]],
                 "free": work_wide["free"]}

        def take():
            return (yield from turn(banks))

        def take_two():
            while len(banks["free"]) < 2:
                yield WAITING
            one = yield from turn(banks)
            return (*one, *(yield from turn(banks)))

        def give(i, *readers):
            read_by(banks, i, *readers)

        x_tiles = d["x"].rearrange("(t p) c -> p t c", p=P)
        loaded_x = []
        L = {}

        def load_block(b):
            t = b * TILES_PER_BLOCK
            loaded_x.append(load(f"x{b}", (xs[:, t:t + TILES_PER_BLOCK, :], x_tiles[:, t:t + TILES_PER_BLOCK, :])))

        def load_weights(group, engine="sync", **tiles):
            t = load(group, *((tile, d[name]) for name, tile in tiles.items()), engine=engine)
            for name in tiles:
                L[name] = t

        load_block(0)
        load_weights("ffn0", ident=ident[:, :], w0=w0[:, :], u0=u0[:, :], gate0=gate0[:, :], v0=v0[:, :])
        load_weights("proj", engine="scalar", xbc_w=xbc_w[:, :], zdt_w=zdt_w[:, :], conv_w=conv_w[:, :, :],
                     conv_b=conv_b[:, :], ln_w=ln_w[:, :], ln_b=ln_b[:, :])
        rows = {n: d[n].broadcast_to([P, w]) for n, w in
                (("dt_bias", HEADS), ("a_log", HEADS), ("d_skip", HEADS), ("first_key", E1), ("qkv_b", QKV),
                 ("p_b", DM))}
        d.update(rows)
        load_weights("scan", dt_bias=dt_bias[:, :], a_log=a_log[:, :], d_skip=d_skip[:, :], norm_w=norm_w[:, :],
                     out_w=out_w[:, :, :], tri_incl=tri_incl[:, :], tri_strict=tri_strict[:, :])
        load_block(1)
        d.update({n: d[n].broadcast_to([P, w]) for n, w in (("tile_start", NT), ("slot_tile", MAXT))})
        d["below"] = d["below"].broadcast_to([P, E1 * E1]).rearrange("p (e f) -> p e f", e=E1)
        load_weights("gates", first_key=first_key[:, :], gate1=gate1[:, :], below=below[:, :, :],
                     tile_start=tile_start[:, :], slot_tile=slot_tile[:, :])
        load_weights("shared", sg_w=sg_w[:, :], su_w=su_w[:, :], sd_w=sd_w[:, :, :])
        load_weights("experts", gu_w=gu_w[:, :], d_w=d_w[:, :])
        load_weights("attn", head_mask=head_mask[:, :], qkv_w=qkv_w[:, :], qkv_b=qkv_b[:, :], p_w=p_w[:, :],
                     p_b=p_b[:, :])
        for b in range(2, NBLK):
            load_block(b)

        L["neghalf"] = pool("const", lambda e: e.memset(neghalf[:, :], -0.5))
        L["ones"] = pool("const", lambda e: e.memset(ones[:, :], 1.0))
        L["ones_b"] = pool("const", lambda e: e.memset(ones_b[:, :], 1.0))
        L["tri_b"] = pool("tri_b", lambda e: e.tensor_copy(tri_b[:, :], tri_incl[:, :]), L["tri_incl"])
        t = act("a_exp", lambda e: e.activation(a_neg[:, :], a_log[:, :], ACT.Exp), L["a_log"])
        L["a_neg"] = dve("a_neg", lambda e: e.tensor_scalar(a_neg[:, :], a_neg[:, :], -1.0, None, ALU.mult), t)

        xs_ready = [None] * NBLK

        def blk(b):
            return xs[:, b * TILES_PER_BLOCK:(b + 1) * TILES_PER_BLOCK, :]

        T4 = range(TILES_PER_BLOCK)
        out_tiles = out.rearrange("(t p) c -> p t c", p=P)

        ln_bufs = {}

        def layernorm(tag, src, dst, ready, dst_read):
            if tag not in ln_bufs:
                ln_bufs[tag] = buffers(f"lnb_{tag}", [P, 4 * 6 + 4 * 2 + 4 + 4 + 4])
            i, t, read = yield from turn(ln_bufs[tag])
            stats = t[:, 0:24].rearrange("p (j s) -> p j s", s=6)
            mv = t[:, 24:32].rearrange("p (j s) -> p j s", s=2)
            veps, rstd, shift = t[:, 32:36], t[:, 36:40], t[:, 40:44]

            def stat(e):
                for j in T4:
                    last = e.bn_stats(stats[:, j, :], src[:, j, :])
                return last
            s = dve("ln_stats", stat, *ready, *read)

            def aggr(e):
                for j in T4:
                    last = e.bn_aggr(mv[:, j, :], stats[:, j, :])
                return last
            s = dve("ln_aggr", aggr, s)
            g = dve("ln_veps", lambda e: e.tensor_scalar(veps, mv[:, :, 1], EPS, None, ALU.add), s)
            yield
            g = pool("ln_rstd", lambda e: e.tensor_tensor(rstd, veps, neghalf[:, :], ALU.pow),
                     g, L["neghalf"])
            yield

            s = dve("ln_shift", lambda e: e.scalar_tensor_tensor(
                shift, mv[:, :, 0], -1.0, rstd, ALU.mult, ALU.mult), g, s)
            yield

            def norm(e):
                for j in T4:
                    last = e.activation(dst[:, j, :], src[:, j, :], ACT.Identity, scale=rstd[:, j:j + 1],
                                        bias=shift[:, j:j + 1])
                return last
            done = act("ln_norm", norm, s, *dst_read)
            read_by(ln_bufs[tag], i, done)
            yield done

        def to_channels(tag, src, dst, ready, dst_read, scale=None, bias=None):
            yield
            i, bank, read = yield from take()

            def tr(e):
                for j in T4:
                    last = e.transpose(bank[:, j * P:(j + 1) * P], src(j), ident[:, :])
                return last
            s = pe("turn", tr, *ready, *read, L["ident"])
            yield
            if bias is not None:
                f = lambda e: e.activation(dst, bank[:, :], ACT.Identity, scale=scale, bias=bias)
            elif scale is not None:
                f = lambda e: e.activation(dst, bank[:, :], ACT.Copy, scale=scale)
            else:
                f = lambda e: e.activation(dst, bank[:, :], ACT.Copy)
            done = act("turned", f, s, *dst_read)
            give(i, done)
            yield s, done

        def latest(steps):
            return max(steps, key=lambda s: s[1])

        def run(gen):
            last = None
            for last in gen:
                if last is None or last is WAITING or isinstance(last, (list, dict)):
                    yield last
            return last

        f0_g = buffers("f0_g", [P, 4, 2 * E0 + 3])

        def ffn0(b):
            x = blk(b)
            i_xn, xn, r_xn = yield from turn(work4)
            normed = yield from run(layernorm("f0", x, xn, [xs_ready[b]], r_xn))
            i_xT, xT, r_xT = yield from turn(work)
            tr, xT_ready = yield from run(to_channels("f0x", lambda j: xn[:, j, :], xT[:, :], [normed], r_xT))
            read_by(work, i_xn, tr)
            i_l, lbank, l_read, i_t, tbank, t_read = yield from take_two()
            logits = lbank[:, 0:4 * E0].rearrange("p (j e) -> p j e", e=E0)

            def mm_gate(e):
                for j in T4:
                    last = e.matmul(logits[:, j, :], xT[:, j * P:(j + 1) * P], gate0[:, :], start=True, stop=True)
                return last
            s_l = pe("f0_gate", mm_gate, xT_ready, L["gate0"], *l_read)

            def mm_t(e):
                for j in T4:
                    last = e.matmul(tbank[:, j * P:(j + 1) * P], xT[:, j * P:(j + 1) * P], u0[:, :],
                                    start=True, stop=True)
                return last
            s_t = pe("f0_down", mm_t, L["u0"], *t_read)
            yield
            i_g, gt, r_g = yield from turn(f0_g)
            ex, gg = gt[:, :, 0:E0], gt[:, :, E0:2 * E0]
            mx, sm, rs = (gt[:, :, 2 * E0 + k:2 * E0 + k + 1] for k in range(3))
            s = dve("f0_max", lambda e: e.tensor_reduce(mx, logits, AX.X, ALU.max), s_l, *r_g)
            s = dve("f0_sub", lambda e: e.tensor_tensor(ex, logits, mx.broadcast_to([P, 4, E0]), ALU.subtract), s)
            give(i_l, s)
            yield
            s = act("f0_exp", lambda e: e.activation(ex, ex, ACT.Exp), s)
            yield
            s1 = dve("f0_sum", lambda e: e.tensor_reduce(sm, ex, AX.X, ALU.add), s)
            s1 = dve("f0_rec", lambda e: e.reciprocal(rs, sm), s1)
            s1 = dve("f0_gates", lambda e: e.scalar_tensor_tensor(
                gg, ex, 1.0 / RANK, rs.broadcast_to([P, 4, E0]), ALU.mult, ALU.mult), s1)
            i_tg, tg, r_tg = yield from turn(work4)

            def scale_t(e):
                for j in T4:
                    last = e.tensor_tensor(tg[:, j, :].rearrange("p (e r) -> p e r", r=RANK),
                                           tbank[:, j * P:(j + 1) * P].rearrange("p (e r) -> p e r", r=RANK),
                                           gg[:, j, :].unsqueeze(2).broadcast_to([P, E0, RANK]), ALU.mult)
                return last
            s = dve("f0_tg", scale_t, s1, s_t, *r_tg)
            give(i_t, s)
            read_by(f0_g, i_g, s)
            yield
            i_tT, tT, r_tT = yield from turn(work)
            tr, tT_ready = yield from run(to_channels("f0t", lambda j: tg[:, j, :], tT[:, :], [s], r_tT))
            read_by(work, i_tg, tr)
            i, bank, read = yield from take()

            def mm_out(e):
                for j in T4:
                    o = bank[:, j * P:(j + 1) * P]
                    e.matmul(o, xT[:, j * P:(j + 1) * P], w0[:, :], start=True, stop=False)
                    last = e.matmul(o, tT[:, j * P:(j + 1) * P], v0[:, :], start=False, stop=True)
                return last
            s = pe("f0_out", mm_out, tT_ready, L["w0"], L["v0"], *read)
            read_by(work, i_xT, s)
            read_by(work, i_tT, s)
            yield
            s = dve("f0_res", lambda e: e.scalar_tensor_tensor(
                x, bank[:, :].rearrange("p (j c) -> p j c", c=DM), 0.5, x, ALU.mult, ALU.add), s)
            give(i, s)
            xs_ready[b] = s
            yield

        m_halo = [[sb(f"m_halo{n}_{i}", [P, XBC_CHUNKS, halo]) for i in range(2)] for n in range(BATCH)]
        m_cv = buffers("m_cv", [P, XBC_CHUNKS, BT])
        m_g = buffers("m_g", [P, 4, DINNER])
        m_dt = buffers("m_dt", [P, 16, 4 * HEADS])
        m_ex = buffers("m_ex", [P, 3, 4 * HEADS])
        m_rs = buffers("m_rs", [P, 3, 4])
        m_ch = buffers("m_ch", [P, 10 * P], 4)
        m_sq = sb("m_sq", [P, DINNER])
        states = [[sb(f"state{n}_{i}", [P, DINNER]) for i in range(2)] for n in range(BATCH)]
        state_qs = [sb(f"state_q{n}", [P, DINNER]) for n in range(BATCH)]
        m_states = [{"ready": None, "k": 0, "read": [(), ()], "q_read": (), "convolved": 0, "scanned": 0}
                    for n in range(BATCH)]
        square = {"last": None}

        def heads(ap, h=HEADS):
            return ap.rearrange("p (h c) -> p h c", h=h)

        def per_head(ap):
            return ap.unsqueeze(2).broadcast_to([P, HEADS, HDIM])

        def mamba(b):
            x = blk(b)
            batch, nth = divmod(b, BLK_PER_BATCH)
            first = nth == 0
            m_state, state, state_q = m_states[batch], states[batch], state_qs[batch]
            i_xa, xa, r_xa = yield from turn(work4)
            xa_ready = yield from run(layernorm("ma", x, xa, [xs_ready[b]], r_xa))
            i_xb, xb, r_xb = yield from turn(work4)
            xb_ready = yield from run(layernorm("mb", xa, xb, [xa_ready], r_xb))
            summed = pool("m_sum", lambda e: e.tensor_tensor(x, x, xa[:, :, :], ALU.add), xa_ready)
            i_xT, xT, r_xT = yield from turn(work)
            tr, xT_ready = yield from run(to_channels("mx", lambda j: xb[:, j, :], xT[:, :],
                                                      [xb_ready, L["ln_w"], L["ln_b"]],
                                                      r_xT, ln_w[:, 0:1], ln_b[:, 0:1]))
            read_by(work, i_xb, tr)
            read_by(work, i_xa, summed, xb_ready)
            i_g, g, r_g = yield from turn(m_g)
            i_dt, dtt, r_dt = yield from turn(m_dt)
            dt3 = dtt[:, :, :].rearrange("p k (j h) -> p k j h", h=HEADS)
            raw = dt3[:, 0, :, :]
            z_ready = [None] * 4

            def z_and_dt(j):
                i, bank, read = yield from take()
                s = pe("m_zdt", lambda e: e.matmul(
                    bank[:, 0:DINNER + HEADS], xT[:, j * P:(j + 1) * P], zdt_w[:, :], start=True, stop=True),
                    xT_ready, L["zdt_w"], *read)
                yield
                a = act("m_silu_z", lambda e: e.activation(g[:, j, :], bank[:, 0:DINNER], ACT.Silu), s, *r_g)
                v = dve("m_dtraw", lambda e: e.tensor_tensor(
                    raw[:, j, :], bank[:, DINNER:DINNER + HEADS], dt_bias[:, :], ALU.add), s, a, L["dt_bias"], *r_dt)
                give(i, a, v)
                z_ready[j] = (s, a, v)
                yield
            yield [z_and_dt(j) for j in T4]
            sz_ready = latest(z[1] for z in z_ready)
            raw_ready = latest(z[2] for z in z_ready)
            while m_state["convolved"] < nth:
                yield WAITING
            i_cv, cv, r_cv = yield from turn(m_cv)
            old_halo, new_halo = m_halo[batch][(b + 1) % 2], m_halo[batch][b % 2]
            cv_ready, halos, read_xT = [None] * XBC_CHUNKS, [None] * XBC_CHUNKS, [None] * XBC_CHUNKS
            old_halos = m_state.get("halos")

            def convolve(c):
                i_pre, pre, r_pre = yield from turn(work_wide)
                if first:
                    h_in = pool("m_halo0", lambda e: e.memset(pre[:, 0:halo], 0.0), *r_pre)
                else:
                    h_in = pool("m_halo", lambda e: e.tensor_copy(pre[:, 0:halo], old_halo[:, c, :]),
                                old_halos[c], *r_pre)
                i, bank, read = yield from take()
                s = pe("m_xbc", lambda e: e.matmul(
                    bank[:, :], xbc_w[:, c * P:(c + 1) * P], xT[:, :], start=True, stop=True),
                    L["xbc_w"], *read)
                read_xT[c] = s
                yield
                a0 = act("m_pre", lambda e: e.activation(pre[:, halo:halo + BT], bank[:, :], ACT.Copy), s, *r_pre)
                a1 = act("m_tap", lambda e: e.activation(
                    cv[:, c, :], bank[:, :], ACT.Identity, scale=conv_w[:, c, halo:halo + 1],
                    bias=conv_b[:, c:c + 1]), L["conv_w"], L["conv_b"], *r_cv)
                give(i, a1)
                yield {"until": a0}
                h_out = pool("m_halo_out", lambda e: e.tensor_copy(new_halo[:, c, :], pre[:, BT:BT + halo]), a0, h_in)
                halos[c] = h_out
                yield
                v = a1
                for k in range(halo):
                    v = dve("m_conv", lambda e, k=k: e.scalar_tensor_tensor(
                        cv[:, c, :], pre[:, k:k + BT], conv_w[:, c, k:k + 1], cv[:, c, :],
                        ALU.mult, ALU.add), v, a0, h_in)
                read_by(work_wide, i_pre, v, h_out)
                yield
                cv_ready[c] = act("m_silu", lambda e: e.activation(cv[:, c, :], cv[:, c, :], ACT.Silu), v)
                yield

            sums = {}

            def time_steps():
                s = dve("m_sp", lambda e: e.tensor_scalar(row(1), row(0), -1.0, None, ALU.mult), raw_ready)
                s = dve("m_sp", lambda e: e.tensor_tensor(row(1), row(0), row(1), ALU.min), s)
                s = act("m_spexp", lambda e: e.activation(row(2), row(1), ACT.Exp), s)
                yield
                s = dve("m_sp", lambda e: e.tensor_scalar(row(3), row(2), 2.0, None, ALU.add), s)
                s = dve("m_sp", lambda e: e.reciprocal(row(4), row(3)), s)
                s = dve("m_sp", lambda e: e.tensor_tensor(row(5), row(2), row(4), ALU.mult), s)
                s = dve("m_sp", lambda e: e.tensor_tensor(row(6), row(5), row(5), ALU.mult), s)
                s = dve("m_sp", lambda e: e.tensor_scalar(row(7), row(6), ATANH[7], ATANH[6], ALU.mult, ALU.add), s)
                for k in (5, 4, 3, 2, 1, 0):
                    s = dve("m_sp", lambda e: e.tensor_tensor(row(7), row(7), row(6), ALU.mult), s)
                    s = dve("m_sp", lambda e, k=k: e.tensor_scalar(row(7), row(7), ATANH[k], None, ALU.add), s)
                s = dve("m_sp", lambda e: e.tensor_tensor(row(7), row(7), row(5), ALU.mult), s)
                dt_ready = dve("m_dt", lambda e: e.scalar_tensor_tensor(
                    row(8), row(0), 0.0, row(7), ALU.max, ALU.add), s)
                dta_ready = dve("m_dta", lambda e: e.tensor_tensor(
                    dt3[:, 9, :, :], dt3[:, 8, :, :], a_neg[:, :].unsqueeze(1).broadcast_to([P, 4, HEADS]), ALU.mult),
                    dt_ready, L["a_neg"])
                yield
                i, bank, read = yield from take()

                def mm_sums(e):
                    n = 4 * HEADS
                    e.matmul(bank[:, 0:n], tri_incl[:, :], dta, start=True, stop=True)
                    e.matmul(bank[:, n:2 * n], tri_strict[:, :], dta, start=True, stop=True)
                    return e.matmul(bank[:, 2 * n:3 * n], ones[:, :], dta, start=True, stop=True)
                s = pe("m_sums", mm_sums, dta_ready, L["tri_incl"], L["tri_strict"], L["ones"], *read)
                yield
                ex_ready = act("m_exps", lambda e: e.activation(
                    ex[:, :, :], bank[:, 0:12 * HEADS].rearrange("p (k n) -> p k n", k=3), ACT.Exp), s, *r_ex)
                give(i, ex_ready)
                yield
                dtr = dve("m_dtr", lambda e: e.tensor_tensor(row(10), dt, ex[:, 1, :], ALU.mult), ex_ready)
                sums.update(dt_ready=dt_ready, dta_ready=dta_ready, ex_ready=ex_ready, dtr=dtr)
                yield
            i_ex, ex, r_ex = yield from turn(m_ex)
            row = lambda k: dtt[:, k, :]
            dt, dta = row(8), row(9)
            yield [time_steps(), *(convolve(c) for c in range(XBC_CHUNKS))]
            dt_ready, dta_ready, ex_ready, dtr = (sums[k] for k in ("dt_ready", "dta_ready", "ex_ready", "dtr"))
            last_read = latest(read_xT)
            read_by(work, i_xT, last_read)
            m_state["halos"] = halos
            m_state["convolved"] += 1
            i_rs, rs, r_rs = yield from turn(m_rs)
            while m_state["scanned"] < nth:
                yield WAITING
            turns = {"started": 0, "state": 0, "y": {}}

            def chunk(j):
                tok = slice(j * P, (j + 1) * P)
                hj = slice(j * HEADS, (j + 1) * HEADS)
                while turns["started"] < j:
                    yield WAITING
                i_ch, ch, r_ch = yield from turn(m_ch)
                turns["started"] += 1
                xt, gm = ch[:, 0:3 * P], ch[:, 3 * P:4 * P]
                x_dt, x_dtr, x_d = (ch[:, (4 + 2 * k) * P:(6 + 2 * k) * P] for k in range(3))
                i_seg, seg, r_seg = yield from turn(work4)
                s_seg = pool("m_seg", lambda e: e.tensor_tensor(
                    seg[:, :, :], tri_incl[:, :].unsqueeze(1).broadcast_to([P, HEADS, P]),
                    dta[:, hj].unsqueeze(2).broadcast_to([P, HEADS, P]), ALU.mult), dta_ready, *r_seg)
                i_tp, tbank, t_read, i_gb, gbank, g_read = yield from take_two()

                def tr(e):
                    for c in range(3):
                        last = e.transpose(tbank[:, c * P:(c + 1) * P], cv[:, c, tok], ident[:, :])
                    return last
                s_tr = pe("m_tr", tr, *cv_ready[0:3], *t_read)
                s_g = pe("m_G", lambda e: e.matmul(
                    gbank[:, 0:P], cv[:, CH_B, tok], cv[:, CH_C, tok], start=True, stop=True),
                    cv_ready[3], *g_read)
                yield
                xt_ready = act("m_xt", lambda e: e.activation(xt, tbank[:, 0:3 * P], ACT.Copy), s_tr, *r_ch)
                give(i_tp, xt_ready)
                gm_ready = dve("m_gm", lambda e: e.tensor_tensor(gm, gbank[:, 0:P], tri_incl[:, :], ALU.mult),
                               s_g, *r_ch)
                give(i_gb, gm_ready)
                i_d, dbank, d_read = yield from take()
                s_d = pe("m_D", lambda e: e.matmul(
                    dbank[:, :], tri_strict[:, :], seg[:, :, :].rearrange("p h t -> p (h t)"),
                    start=True, stop=True), s_seg, *d_read)
                read_by(work, i_seg, s_d)
                yield
                i_e, et, r_e = yield from turn(work4)
                s = act("m_decay", lambda e: e.activation(
                    et[:, :, :], dbank[:, :].rearrange("p (h t) -> p h t", h=HEADS), ACT.Exp), s_d, *r_e)
                give(i_d, s)
                xh = heads(xt[:, 0:DINNER])
                s_xd = pool("m_xdt", lambda e: e.tensor_tensor(heads(x_dt), xh, per_head(dt[:, hj]), ALU.mult),
                            xt_ready, dt_ready, *r_ch)
                s_xs = pool("m_xds", lambda e: e.tensor_tensor(heads(x_dtr), xh, per_head(row(10)[:, hj]), ALU.mult),
                            dtr)
                s_dx = pool("m_dx", lambda e: e.tensor_tensor(heads(x_d), xh, per_head(d_skip[:, :]), ALU.mult),
                            L["d_skip"])
                yield
                m_ready = dve("m_M", lambda e: e.tensor_tensor(
                    et[:, :, :], et[:, :, :], gm.unsqueeze(1).broadcast_to([P, HEADS, P]), ALU.mult),
                    s, gm_ready)
                yield
                while turns["state"] < j:
                    yield WAITING
                start_of_batch = first and j == 0
                i_y, ybank, y_read, i_s, sbank, s_read = yield from take_two()
                old = state[m_state["k"] % 2]
                s_st = pe("m_S", lambda e: e.matmul(
                    sbank[:, 0:DINNER], xt[:, 2 * P:3 * P], x_dtr, start=True, stop=True), s_xs, *s_read)

                def mm_y(e):
                    if not start_of_batch:
                        e.matmul(ybank[:, DINNER:2 * DINNER], cv[:, CH_C, tok], old[:, :], start=True, stop=True)
                    for h in range(HEADS):
                        c = slice(h * HDIM, (h + 1) * HDIM)
                        last = e.matmul(ybank[:, c], et[:, h, :], x_dt[:, c], start=True, stop=True)
                    return last
                s_y = pe("m_Y", mm_y, m_ready, s_xd, m_state["ready"] if not start_of_batch else None, *y_read)
                read_by(work, i_e, s_y)
                new_k = (m_state["k"] + 1) % 2
                new = state[new_k]
                if start_of_batch:
                    yield {"until": s_st}
                    st = dve("m_state", lambda e: e.tensor_copy(new[:, :], sbank[:, 0:DINNER]),
                             s_st, *m_state["read"][new_k])
                    turns["ex"] = st
                else:
                    sq = pool("m_stateq", lambda e: e.tensor_tensor(
                        heads(state_q[:, :]), heads(old[:, :]), per_head(ex[:, 2, hj]), ALU.mult),
                        m_state["ready"], ex_ready, *m_state["q_read"])
                    yield
                    st = dve("m_state", lambda e: e.tensor_tensor(
                        new[:, :], state_q[:, :], sbank[:, 0:DINNER], ALU.add), s_st, sq, *m_state["read"][new_k])
                    m_state["q_read"] = (st,)
                    m_state["read"][m_state["k"] % 2] = (s_y, sq)
                    turns["ex"] = sq
                m_state["ready"] = st
                m_state["k"] = new_k
                turns["state"] += 1
                give(i_s, st)
                yield {"until": s_y}
                s1 = dve("m_y1", lambda e: e.tensor_tensor(x_d, ybank[:, 0:DINNER], x_d, ALU.add), s_y, s_dx)
                s2 = s3 = s1
                if not start_of_batch:
                    s2 = dve("m_y2", lambda e: e.tensor_tensor(
                        heads(xt[:, 0:DINNER]), heads(ybank[:, DINNER:2 * DINNER]), per_head(ex[:, 0, hj]), ALU.mult),
                        ex_ready)
                    s3 = dve("m_y3", lambda e: e.tensor_tensor(x_d, x_d, xt[:, 0:DINNER], ALU.add), s1, s2)
                give(i_y, s1, s2)
                s4 = pool("m_gated", lambda e: e.tensor_tensor(g[:, j, :], x_d, g[:, j, :], ALU.mult), s3, sz_ready)
                read_by(m_ch, i_ch, s_y, s_st, s4)
                yield
                a = act("m_sq", lambda e: e.activation(
                    m_sq[:, :], g[:, j, :], ACT.Square, accum_out=rs[:, 0, j:j + 1]), s4, *r_rs, square["last"])
                square["last"] = a
                turns["y"][j] = (s_y, s2, s4, a)
                yield
            yield [chunk(j) for j in T4]
            s_y, s2, s4, squared = (latest(turns["y"][j][k] for j in T4) for k in range(4))
            s_x = turns["ex"]
            m_state["scanned"] += 1
            read_by(m_cv, i_cv, s_y)
            read_by(m_dt, i_dt, s4)
            read_by(m_ex, i_ex, s2, s_x)
            s = pool("m_ms", lambda e: e.tensor_scalar(rs[:, 1, :], rs[:, 0, :], 1.0 / DINNER, EPS, ALU.mult, ALU.add),
                     squared)
            rstd_ready = pool("m_rstd", lambda e: e.tensor_tensor(rs[:, 2, :], rs[:, 1, :], neghalf[:, :], ALU.pow), s)
            gT = []
            for c in range(DINNER // P):
                i_gT, part, r_gT = yield from turn(work)
                tr, gT_ready = yield from run(to_channels(
                    "mg", lambda j, c=c: g[:, j, c * P:(c + 1) * P], part[:, :], [s4, L["norm_w"]], r_gT,
                    norm_w[:, c:c + 1]))
                gT.append((i_gT, part))
            read_by(m_g, i_g, tr, squared)
            i, bank, read = yield from take()

            def mm_out(e):
                for j in T4:
                    for c in range(DINNER // P):
                        last = e.matmul(bank[:, j * P:(j + 1) * P], gT[c][1][:, j * P:(j + 1) * P], out_w[:, c, :],
                                        start=(c == 0), stop=(c == DINNER // P - 1))
                return last
            s = pe("m_out", mm_out, gT_ready, L["out_w"], *read)
            for i_gT, _ in gT:
                read_by(work, i_gT, s)
            yield

            def res(e):
                for j in T4:
                    last = e.scalar_tensor_tensor(x[:, j, :], bank[:, j * P:(j + 1) * P], rs[:, 2, j:j + 1],
                                                  x[:, j, :], ALU.mult, ALU.add)
                return last
            s = dve("m_res", res, s, rstd_ready, summed)
            give(i, s)
            read_by(m_rs, i_rs, s)
            xs_ready[b] = s
            yield

        f1_xn = buffers("f1_xn", [P, 4, DM], GB + 1)
        f1_g = buffers("f1_g", [P, 6, 4 * E1])
        f1_s = buffers("f1_s", [P, 9, 4])
        groups = store_of([{
            "chosen": sb(f"chosen{i}", [P, TOPK, NT * E1]),
            "score": sb(f"score{i}", [P, TOPK, NT]),
            "any": sb(f"any{i}", [P, (NT + 1) * E1], BF16),
            "slot": sb(f"slot{i}", [P, TOPK, NT], U32),
            "expert": sb(f"expert{i}", [P, MAXT], I32),
        } for i in range(2)])
        for g in groups["tiles"]:
            L["any0"] = pool("const", lambda e, g=g: e.memset(g["any"][:, NT * E1:], 0.0))
        sorted_x = [nc.dram_tensor(f"sorted_x{i}", [MAXT * P, DM], F32, kind="Internal").ap() for i in range(2)]
        sorted_y = [nc.dram_tensor(f"sorted_y{i}", [MAXT * P, DM], F32, kind="Internal").ap() for i in range(2)]
        slots = [{"x_read": (), "y_read": ()} for _ in range(2)]
        zero = sb("zero", [P, 3 * DM])
        z = pool("const", lambda e: e.memset(zero[:, :], 0.0))
        for i in range(2):
            v = sorted_x[i].rearrange("(p k) c -> p (k c)", p=P)
            for k in range(0, MAXT, 3):
                w = min(3, MAXT - k) * DM
                t = q.step("sync", f"zero{i}", lambda e, v=v, k=k: e.dma_start(v[:, k * DM:k * DM + w], zero[:, 0:w]),
                           z, inc=16)
            slots[i]["zeroed"] = t

        def ffn1_gates(b, m, group):
            x = blk(b)
            j0 = m * TILES_PER_BLOCK
            chosen = [group["chosen"][:, k, j0 * E1:(j0 + 4) * E1].rearrange("p (j e) -> p j e", e=E1)
                      for k in range(TOPK)]
            i_xn, xn, r_xn = yield from turn(f1_xn)
            normed = yield from run(layernorm("f1", x, xn, [xs_ready[b]], r_xn))
            i_xT, xT, r_xT = yield from turn(work)
            tr, xT_ready = yield from run(to_channels("f1x", lambda j: xn[:, j, :], xT[:, :], [normed], r_xT))
            i, bank, read = yield from take()
            logits = bank[:, 0:4 * GATES].rearrange("p (j e) -> p j e", e=GATES)

            def mm_gate(e):
                for j in T4:
                    last = e.matmul(logits[:, j, :], xT[:, j * P:(j + 1) * P], gate1[:, :], start=True, stop=True)
                return last
            s_l = pe("f1_gate", mm_gate, xT_ready, L["gate1"], *read)
            yield
            i_g, gt, r_g = yield from turn(f1_g)
            i_s, st, r_s = yield from turn(f1_s)
            col = lambda k: gt[:, k, :].rearrange("p (j e) -> p j e", e=E1)
            one = lambda k: st[:, k, :]
            wide = lambda k: one(k).unsqueeze(2).broadcast_to([P, 4, E1])
            keys = first_key[:, :].unsqueeze(1).broadcast_to([P, 4, E1])
            s = dve("f1_max", lambda e: e.tensor_reduce(one(0), logits[:, :, 0:E1], AX.X, ALU.max), s_l, *r_s, *r_g)
            s = dve("f1_sub", lambda e: e.tensor_tensor(col(0), logits[:, :, 0:E1], wide(0), ALU.subtract), s)
            yield
            s_sg = act("f1_sgexp", lambda e: e.activation(one(7), logits[:, :, E1], ACT.Exp, scale=-1.0), s_l, s, *r_s)
            give(i, s, s_sg)
            s = act("f1_exp", lambda e: e.activation(gt[:, 1, :], gt[:, 0, :], ACT.Exp), s)
            yield
            s = dve("f1_r", lambda e: e.tensor_reduce(one(1), col(1), AX.X, ALU.add), s)
            s = dve("f1_r", lambda e: e.reciprocal(one(2), one(1)), s)
            s = dve("f1_r", lambda e: e.tensor_tensor(col(2), col(1), wide(2), ALU.mult), s)
            cur = 2
            for k in range(TOPK):
                s = dve("f1_r", lambda e: e.tensor_reduce(one(3 + k), col(cur), AX.X, ALU.max), s)
                s = dve("f1_r", lambda e: e.tensor_tensor(col(3), col(cur), wide(3 + k), ALU.is_equal), s)
                s = dve("f1_r", lambda e: e.tensor_tensor(col(4), col(3), keys, ALU.mult), s, L["first_key"])
                s = dve("f1_r", lambda e: e.tensor_reduce(one(5 + k), col(4), AX.X, ALU.max), s)
                s = dve("f1_r", lambda e: e.tensor_tensor(chosen[k], col(4), wide(5 + k), ALU.is_equal), s,
                        *group["read"])
                s = dve("f1_r", lambda e: e.tensor_scalar(
                    group["score"][:, k, j0:j0 + 4], one(3 + k), 0.5, None, ALU.mult), s)
                if k == 0:
                    s = dve("f1_r", lambda e: e.scalar_tensor_tensor(
                        col(5), chosen[0], -2.0, col(2), ALU.mult, ALU.add), s)
                    cur = 5
                yield
            group["ready"] = dve("f1_any", lambda e: e.tensor_tensor(
                group["any"][:, j0 * E1:(j0 + 4) * E1].rearrange("p (j e) -> p j e", e=E1),
                chosen[0], chosen[1], ALU.add), s)
            s = dve("f1_r", lambda e: e.tensor_scalar(one(7), one(7), 1.0, None, ALU.add), s, s_sg)
            s = dve("f1_r", lambda e: e.reciprocal(one(8), one(7)), s)
            s = dve("f1_r", lambda e: e.tensor_scalar(one(8), one(8), 0.5, None, ALU.mult), s)
            shared_weight = s
            read_by(f1_g, i_g, s)
            yield
            h = []
            for c in range(SCH):
                ch = slice(c * SCW, (c + 1) * SCW)
                i_a, abank, a_read, i_b, bbank, b_read = yield from take_two()
                s_g = pe("f1_sg", lambda e: e.matmul(abank[0:SCW, :], sg_w[:, ch], xT[:, :], start=True, stop=True),
                         L["sg_w"], *a_read)
                s_u = pe("f1_su", lambda e: e.matmul(bbank[0:SCW, :], su_w[:, ch], xT[:, :], start=True, stop=True),
                         *b_read)
                yield
                i_sg, sg, r_sg = yield from turn(work)
                a = act("f1_ssilu", lambda e: e.activation(sg[0:SCW, :], abank[0:SCW, :], ACT.Silu), s_g, *r_sg)
                give(i_a, a)
                yield
                v = dve("f1_sh", lambda e: e.tensor_tensor(
                    sg[0:SCW, :], sg[0:SCW, :], bbank[0:SCW, :], ALU.mult), a, s_u)
                give(i_b, v)
                h.append((i_sg, sg))
            read_by(work, i_xT, s_u)
            yield
            i, bank, read = yield from take()

            def mm_sd(e):
                for j in T4:
                    for c in range(SCH):
                        last = e.matmul(bank[:, j * P:(j + 1) * P], h[c][1][0:SCW, j * P:(j + 1) * P], sd_w[:, c, :],
                                        start=(c == 0), stop=(c == SCH - 1))
                return last
            s = pe("f1_sd", mm_sd, v, *read)
            for i_h, _ in h:
                read_by(work, i_h, s)
            yield

            def res(e):
                for j in T4:
                    last = e.scalar_tensor_tensor(x[:, j, :], bank[:, j * P:(j + 1) * P], st[:, 8, j:j + 1],
                                                  x[:, j, :], ALU.mult, ALU.add)
                return last
            s = dve("f1_sres", res, s, shared_weight)
            give(i, s)
            read_by(f1_s, i_s, s)
            xs_ready[b] = s
            group["xn"][m] = (i_xn, xn, normed, tr)
            yield

        f1_before = buffers("f1_before", [P, 2, (NT + 1) * E1], 1, BF16)
        for t in f1_before["tiles"]:
            L["before0"] = pool("const", lambda e, t=t: e.memset(t[:, :, 0:E1], 0.0))
        f1_r = buffers("f1_rank", [P, NT * E1], 1)
        f1_e = buffers("f1_e", [P, 4, E1], 1)
        f1_ee = buffers("f1_ee", [P, max(NT, E1, MAXT) * E1], 1)
        f1_st = buffers("f1_st", [P, 3, max(TOPK * NT, MAXT)], 1)

        def ffn1_sort(group):
            n = group["n"]
            i_b, before, r_b = yield from turn(f1_before)
            s = dve("f1_q", lambda e: e.tensor_copy(before[:, 0, E1:], group["any"][:, 0:NT * E1]), group["ready"],
                    L["before0"], *r_b)
            k, cur = 1, 0
            while k < NT:
                w = k * E1
                s = dve("f1_q", lambda e: e.tensor_copy(before[:, 1 - cur, 0:w + E1], before[:, cur, 0:w + E1]), s)
                s = dve("f1_q", lambda e: e.tensor_tensor(
                    before[:, 1 - cur, w + E1:], before[:, cur, w + E1:],
                    before[:, cur, E1:(NT + 1) * E1 - w], ALU.add), s)
                k, cur = 2 * k, 1 - cur
            i, bank, read = yield from take()

            def mm_rank(e):
                e.matmul(bank[:, 0:(NT + 1) * E1], tri_b[:, :], group["any"][:, :], start=True, stop=False)
                return e.matmul(bank[:, 0:(NT + 1) * E1], ones_b[:, :], before[:, cur, :], start=False, stop=True)
            s_r = pe("f1_rank", mm_rank, s, L["tri_b"], L["ones_b"], L["any0"], *read)
            read_by(f1_before, i_b, s_r)
            yield
            i_e, et, r_e = yield from turn(f1_e)
            i_w, ee, r_w = yield from turn(f1_ee)
            i_r, rank, r_r = yield from turn(f1_r)
            i_t, st, r_t = yield from turn(f1_st)
            total, tiles, base, offs = (et[:, k, :] for k in range(4))
            last_of = lambda ap, n: ap.unsqueeze(2).broadcast_to([P, ap.shape[1], n])
            among = lambda ap, n: ap.unsqueeze(1).broadcast_to([P, n, ap.shape[1]])
            s = dve("f1_q", lambda e: e.tensor_copy(total, bank[:, NT * E1:(NT + 1) * E1]), s_r, *r_e)
            w = ee[:, 0:E1 * NT].rearrange("p (e m) -> p e m", e=E1)
            s = dve("f1_q", lambda e: e.tensor_tensor(w, last_of(total, NT), among(tile_start[:, :], E1), ALU.is_gt),
                    s, L["tile_start"], *r_w)
            s = dve("f1_q", lambda e: e.tensor_reduce(tiles, w, AX.X, ALU.add), s)
            w2 = ee[:, 0:E1 * E1].rearrange("p (e f) -> p e f", e=E1)
            s = dve("f1_q", lambda e: e.tensor_tensor(w2, among(tiles, E1), below[:, :, :], ALU.mult), s, L["below"])
            s = dve("f1_q", lambda e: e.tensor_reduce(base, w2, AX.X, ALU.add), s)
            s = dve("f1_q", lambda e: e.tensor_scalar(offs, base, float(P), -1.0, ALU.mult, ALU.add), s)
            s_base = dve("f1_q", lambda e: e.tensor_tensor(tiles, tiles, base, ALU.add), s)
            s = dve("f1_q", lambda e: e.tensor_tensor(
                rank[:, :].rearrange("p (j e) -> p j e", e=E1), bank[:, 0:NT * E1].rearrange("p (j e) -> p j e", e=E1),
                among(offs, NT), ALU.add), s_base, *r_r)
            give(i, s)
            yield
            w3 = ee[:, 0:NT * E1]
            for k in range(TOPK):
                s = dve("f1_q", lambda e: e.tensor_tensor(w3, rank[:, :], group["chosen"][:, k, :], ALU.mult), s)
                s = dve("f1_q", lambda e: e.tensor_reduce(
                    st[:, 0, k * NT:(k + 1) * NT], w3.rearrange("p (j e) -> p j e", e=E1), AX.X, ALU.add), s, *r_t)
            slot_ready = dve("f1_slot", lambda e: e.tensor_copy(
                group["slot"][:, :, :], st[:, 0, 0:TOPK * NT].rearrange("p (k j) -> p k j", k=TOPK)), s, *group["read"])
            w4 = ee[:, 0:MAXT * E1].rearrange("p (i e) -> p i e", e=E1)
            s = dve("f1_q", lambda e: e.tensor_tensor(w4, last_of(slot_tile[:, :], E1), among(tiles, MAXT), ALU.is_ge),
                    slot_ready, L["slot_tile"])
            s = dve("f1_q", lambda e: e.tensor_reduce(st[:, 1, 0:MAXT], w4, AX.X, ALU.add), s)
            s = dve("f1_q", lambda e: e.tensor_scalar(
                st[:, 2, 0:MAXT], st[:, 1, 0:MAXT], float(E1 - 1), None, ALU.min), s)
            s = dve("f1_q", lambda e: e.tensor_copy(group["expert"][:, :], st[:, 2, 0:MAXT]), s)
            group["expert_ready"] = s
            for bufs, k in ((f1_e, i_e), (f1_ee, i_w), (f1_r, i_r), (f1_st, i_t)):
                read_by(bufs, k, s)
            yield
            first = [slot_ready, slots[n]["zeroed"], *slots[n]["x_read"]]
            for m in range(GB):
                i_xn, xn, normed, tr = group["xn"][m]
                for j in T4:
                    for k in range(TOPK):
                        t = m * TILES_PER_BLOCK + j
                        s = q.step("gpsimd", f"scatter{n}", lambda e: e.indirect_dma_start(
                            out=sorted_x[n],
                            out_offset=bass.IndirectOffsetOnAxis(ap=group["slot"][:, k, t:t + 1], axis=0),
                            in_=xn[:, j, :], in_offset=None), normed, *first, inc=16)
                    yield
            group["scattered"] = s
            for m in range(GB):
                read_by(f1_xn, group["xn"][m][0], s, group["xn"][m][3])
            yield

        def ffn1_experts(group, t0):
            n = group["n"]
            m = min(2, MAXT - t0)
            tiled = lambda dram: dram.rearrange("(t p) c -> p t c", p=P)[:, t0:t0 + m, :]
            yield {"until": group["scattered"]}
            i_sx, sx, read = yield from turn(work4)
            s = q.step("sync", f"load_sx{i_sx}", lambda e: e.dma_start(sx[:, 0:m, :], tiled(sorted_x[n])),
                       group["scattered"], *read, inc=16)
            group["loaded"][i_sx] = s
            slots[n]["x_read"] = tuple(group["loaded"].values())
            yield {"until": s}
            i, bank, read = yield from take()

            def tr(e):
                for j in range(m):
                    last = e.transpose(bank[:, j * P:(j + 1) * P], sx[:, j, :], ident[:, :])
                return last
            s = pe("e_tr", tr, s, *read)
            read_by(work, i_sx, s)
            yield
            i_x, xT, read = yield from turn(work)
            x_ready = act("e_xT", lambda e: e.activation(xT[:, 0:m * P], bank[:, 0:m * P], ACT.Copy), s, *read)
            give(i, x_ready)
            yield
            i_h, h, h_read = yield from turn(work)
            two = yield from take_two()
            experts, products = [], []
            for j in range(m):
                i, bank, read = two[3 * j:3 * j + 3]
                q.wait("tensor", group["expert_ready"])
                experts.append(nc.tensor.value_load(group["expert"][0:1, t0 + j:t0 + j + 1], min_val=0, max_val=E1 - 1))
                s = pe("e_gu", lambda e: e.matmul(
                    bank[:, 0:2 * IEXP], xT[:, j * P:(j + 1) * P],
                    gu_w[:, bass.ds(experts[j] * (2 * IEXP), 2 * IEXP)], start=True, stop=True),
                    x_ready, L["gu_w"], *read)
                products.append(s)
            if m == 1:
                give(two[3], *two[5])
            read_by(work, i_x, s)
            for j in range(m):
                yield {"until": products[j]}
                i, bank, read = two[3 * j:3 * j + 3]
                hj = h[:, j * IEXP:(j + 1) * IEXP]
                a = act("e_silu", lambda e: e.activation(hj, bank[:, 0:IEXP], ACT.Silu), products[j],
                        *h_read)
                yield
                v = dve("e_h", lambda e: e.tensor_tensor(hj, hj, bank[:, IEXP:2 * IEXP], ALU.mult), a)
                give(i, v)
            yield
            i, bank, read = yield from take()

            def tr_h(e):
                for k in range(2 * m):
                    last = e.transpose(bank[0:IHALF, k * P:(k + 1) * P], h[:, k * IHALF:(k + 1) * IHALF], ident[:, :])
                return last
            s = pe("e_trh", tr_h, v, *read)
            read_by(work, i_h, s)
            yield
            i_hT, hT, read = yield from turn(work)
            a = act("e_hT", lambda e: e.activation(hT[0:IHALF, 0:2 * m * P], bank[0:IHALF, 0:2 * m * P], ACT.Copy),
                    s, *read)
            give(i, a)
            yield
            i, bank, read = yield from take()

            def mm_down(e):
                for j in range(m):
                    for c in range(2):
                        k = 2 * j + c
                        last = e.matmul(bank[:, j * P:(j + 1) * P], hT[0:IHALF, k * P:(k + 1) * P],
                                        d_w[:, bass.ds(experts[j] * (2 * DM) + c * DM, DM)],
                                        start=(c == 0), stop=(c == 1))
                return last
            s = pe("e_down", mm_down, a, L["d_w"], *read)
            read_by(work, i_hT, s)
            yield
            i_y, y, read = yield from turn(work)
            v = dve("e_y", lambda e: e.tensor_copy(y[:, 0:m * P], bank[:, 0:m * P]), s, *read)
            give(i, v)
            yield
            s = q.step("sync", f"store_y{i_y}", lambda e: e.dma_start(
                tiled(sorted_y[n]), y[:, 0:m * P].rearrange("p (j c) -> p j c", c=DM)), v, *slots[n]["y_read"], inc=16)
            read_by(work, i_y, s)
            group["stored"][i_y] = s
            yield

        def ffn1_combine(b, m, group, store_out):
            x = blk(b)
            n = group["n"]
            j0 = m * TILES_PER_BLOCK
            for s in group["stored"].values():
                yield {"until": s}
            i, yg0, read = yield from turn(work4)
            i1, yg1, read1 = yield from turn(work4)
            yg = (yg0, yg1)
            for j in T4:
                for k in range(TOPK):
                    s = q.step("gpsimd", f"gather{m}", lambda e: e.indirect_dma_start(
                        out=yg[k][:, j, :], out_offset=None, in_=sorted_y[n],
                        in_offset=bass.IndirectOffsetOnAxis(ap=group["slot"][:, k, j0 + j:j0 + j + 1], axis=0)),
                        *group["stored"].values(), *read, *read1, inc=16)
                yield
            gathered = s
            yield {"until": s}
            for k in range(TOPK):
                def add(e):
                    for j in T4:
                        last = e.scalar_tensor_tensor(x[:, j, :], yg[k][:, j, :],
                                                      group["score"][:, k, j0 + j:j0 + j + 1],
                                                      x[:, j, :], ALU.mult, ALU.add)
                    return last
                s = dve("f1_add", add, s, xs_ready[b])
            read_by(work, i, s)
            read_by(work, i1, s)
            xs_ready[b] = s
            group["done"].append((s, gathered))
            if len(group["done"]) == GB:
                slots[n]["y_read"] = tuple(g for _, g in group["done"])
            yield
            if store_out:
                t0 = b * TILES_PER_BLOCK
                q.step("sync", "store", lambda e: e.dma_start(out_tiles[:, t0:t0 + TILES_PER_BLOCK, :], x), s, inc=16)
            yield

        VW = QKV + 1
        a_qkv = buffers("a_qkv", [P, 4, VW], 2)
        a_q = [sb(f"a_q{b}", [P, 4, DM]) for b in range(NBLK)]
        a_st = buffers("a_st", [P, 3, 4 * 2 * AHEADS], 1)
        a_ctxs = [sb(f"a_ctx{i}", [P, DM + 1]) for i in range(BATCH)]
        a_cms = [sb(f"a_cm{i}", [P, DM + AHEADS]) for i in range(BATCH)]
        a_di = buffers("a_di", [P, 4, AHEADS])
        att = {"ctx": {}, "cm": {}, "ones": [], "q": {}}
        for t in a_qkv["tiles"]:
            att["ones"].append(pool("a_ones", lambda e, t=t: e.memset(t[:, :, QKV:VW], 1.0)))

        def attn_kv(b):
            x = blk(b)
            batch, n = divmod(b, BLK_PER_BATCH)
            a_ctx, a_cm = a_ctxs[batch], a_cms[batch]
            i_xn, xn, r_xn = yield from turn(work4)
            normed = yield from run(layernorm("at", x, xn, [xs_ready[b]], r_xn))
            i_xT, xT, r_xT = yield from turn(work)
            tr, xT_ready = yield from run(to_channels("atx", lambda j: xn[:, j, :], xT[:, :], [normed], r_xT))
            read_by(work, i_xn, tr)
            i_k, qkv, r_k = yield from turn(a_qkv)
            for j in T4:
                i, bank, read = yield from take()
                s = pe("a_qkv", lambda e, bank=bank, j=j: e.matmul(
                    bank[:, 0:QKV], xT[:, j * P:(j + 1) * P], qkv_w[:, :], start=True, stop=True),
                    xT_ready, L["qkv_w"], *read)
                yield
                v = dve("a_bias", lambda e, bank=bank, j=j: e.tensor_tensor(
                    qkv[:, j, 0:QKV], bank[:, 0:QKV], qkv_b[:, :], ALU.add), s, L["qkv_b"], *r_k)
                give(i, v)
                yield
            read_by(work, i_xT, s)
            i_st, st, r_st = yield from turn(a_st)
            G = 2 * AHEADS
            qk = lambda j: qkv[:, j, 0:2 * DM].rearrange("p (g c) -> p g c", c=ADIM)
            sj = lambda k, j: st[:, k, j * G:(j + 1) * G]
            wide = lambda k, j: sj(k, j).unsqueeze(2).broadcast_to([P, G, ADIM])

            def each(f):
                def emit(e):
                    for j in T4:
                        last = f(e, j)
                    return last
                return emit
            s = dve("a_max", each(lambda e, j: e.tensor_reduce(sj(0, j), qk(j), AX.X, ALU.max)), v, *r_st)
            s = dve("a_sub", each(lambda e, j: e.tensor_tensor(qk(j), qk(j), wide(0, j), ALU.subtract)), s)
            yield
            s = act("a_exp", lambda e: e.activation(qkv[:, :, 0:2 * DM], qkv[:, :, 0:2 * DM], ACT.Exp), s)
            yield
            s = dve("a_sumd", each(lambda e, j: e.tensor_reduce(sj(1, j), qk(j), AX.X, ALU.add)), s)
            s = dve("a_rec", lambda e: e.reciprocal(st[:, 2, :], st[:, 1, :]), s)
            yield
            k_part = lambda j: qkv[:, j, DM:2 * DM].rearrange("p (g c) -> p g c", c=ADIM)
            wk = lambda j: sj(2, j)[:, AHEADS:].unsqueeze(2).broadcast_to([P, AHEADS, ADIM])
            wq = lambda j: sj(2, j)[:, :AHEADS].unsqueeze(2).broadcast_to([P, AHEADS, ADIM])
            k_ready = dve("a_k", each(lambda e, j: e.tensor_tensor(k_part(j), k_part(j), wk(j), ALU.mult)), s)
            qn = a_q[b]
            q_ready = dve("a_q", each(lambda e, j: e.tensor_tensor(
                qn[:, j, :].rearrange("p (g c) -> p g c", c=ADIM),
                qkv[:, j, 0:DM].rearrange("p (g c) -> p g c", c=ADIM), wq(j), ALU.mult)), s)
            att["q"][b] = q_ready
            read_by(a_st, i_st, q_ready)
            yield
            i, bank, read = yield from take()

            def mm_ctx(e):
                for j in T4:
                    last = e.matmul(bank[:, 0:DM + 1], qkv[:, j, DM:2 * DM], qkv[:, j, 2 * DM:VW],
                                    start=(j == 0), stop=(j == 3))
                return last
            s = pe("a_ctx", mm_ctx, k_ready, att["ones"][i_k], *read)
            read_by(a_qkv, i_k, s, q_ready)
            if n == 0:
                s = dve("a_ctxsum", lambda e: e.tensor_copy(a_ctx[:, :], bank[:, 0:DM + 1]), s)
            else:
                s = dve("a_ctxsum", lambda e: e.tensor_tensor(a_ctx[:, :], a_ctx[:, :], bank[:, 0:DM + 1], ALU.add),
                        s, att["ctx"][batch])
            give(i, s)
            att["ctx"][batch] = s
            if n == BLK_PER_BATCH - 1:
                s1 = dve("a_cm", lambda e: e.tensor_tensor(
                    a_cm[:, 0:DM].rearrange("p (h c) -> p h c", c=ADIM),
                    a_ctx[:, 0:DM].rearrange("p (h c) -> p h c", c=ADIM),
                    head_mask[:, :].unsqueeze(2).broadcast_to([P, AHEADS, ADIM]), ALU.mult),
                    s, L["head_mask"])
                s1 = dve("a_cm", lambda e: e.tensor_scalar(
                    a_cm[:, DM:DM + AHEADS], head_mask[:, :], a_ctx[:, DM:DM + 1], None, ALU.mult), s)
                att["cm"][batch] = s1
            yield

        def attn_out(b):
            x = blk(b)
            batch = b // BLK_PER_BATCH
            a_cm = a_cms[batch]
            qn = a_q[b]
            i_qT, qT, r_qT = yield from turn(work)
            tr, qT_ready = yield from run(to_channels("aq", lambda j: qn[:, j, :], qT[:, :], [att["q"][b]], r_qT))
            biased = pool("a_bp", lambda e: e.tensor_tensor(
                x, x, p_b[:, :].unsqueeze(1).broadcast_to([P, 4, DM]), ALU.add), xs_ready[b], att["q"][b], L["p_b"])
            i_n, nbank, n_read, i_d, dbank, d_read = yield from take_two()

            def mm(e):
                for j in T4:
                    lhs = qT[:, j * P:(j + 1) * P]
                    e.matmul(nbank[:, j * P:(j + 1) * P], lhs, a_cm[:, 0:DM], start=True, stop=True)
                    last = e.matmul(dbank[:, j * AHEADS:(j + 1) * AHEADS], lhs, a_cm[:, DM:DM + AHEADS],
                                    start=True, stop=True)
                return last
            s = pe("a_num", mm, qT_ready, att["cm"][batch], *n_read, *d_read)
            read_by(work, i_qT, s)
            yield
            i_di, di, r_di = yield from turn(a_di)
            v = dve("a_dinv", lambda e: e.reciprocal(
                di[:, :, :], dbank[:, 0:4 * AHEADS].rearrange("p (j h) -> p j h", h=AHEADS)), s, *r_di)
            give(i_d, v)
            i_o, o, r_o = yield from turn(work4)

            def div(e):
                for j in T4:
                    last = e.tensor_tensor(o[:, j, :].rearrange("p (h c) -> p h c", c=ADIM),
                                           nbank[:, j * P:(j + 1) * P].rearrange("p (h c) -> p h c", c=ADIM),
                                           di[:, j, :].unsqueeze(2).broadcast_to([P, AHEADS, ADIM]), ALU.mult)
                return last
            v = dve("a_div", div, v, *r_o)
            give(i_n, v)
            read_by(a_di, i_di, v)
            yield
            v = pool("a_addq", lambda e: e.tensor_tensor(o[:, :, :], o[:, :, :], qn[:, :, :], ALU.add), v)
            yield
            i_oT, oT, r_oT = yield from turn(work)
            tr, oT_ready = yield from run(to_channels("ao", lambda j: o[:, j, :], oT[:, :], [v], r_oT))
            read_by(work, i_o, tr)
            i, bank, read = yield from take()

            def mm_p(e):
                for j in T4:
                    last = e.matmul(bank[:, j * P:(j + 1) * P], oT[:, j * P:(j + 1) * P], p_w[:, :],
                                    start=True, stop=True)
                return last
            s = pe("a_proj", mm_p, oT_ready, L["p_w"], *read)
            read_by(work, i_oT, s)
            yield
            s = dve("a_res", lambda e: e.tensor_tensor(
                x, bank[:, :].rearrange("p (j c) -> p j c", c=DM), x, ALU.add), s, biased)
            give(i, s)
            xs_ready[b] = s
            yield

        for b in range(NBLK):
            xs_ready[b] = loaded_x[b]

        def open_group(n):
            while not groups["free"]:
                yield WAITING
            i, group, readers = yield from turn(groups)
            group.update(i=i, n=n % 2, read=readers, xn=[None] * GB, done=[], stored={}, loaded={})
            open_groups[n] = group

        def close_group(n):
            group = open_groups.pop(n)
            read_by(groups, group["i"], *(s for pair in group["done"] for s in pair))
            yield None

        open_groups = {}
        tasks, done, ended = [], set(), {}
        last_kv = lambda b: ("kv", b // BLK_PER_BATCH * BLK_PER_BATCH + BLK_PER_BATCH - 1)

        def task(name, gen, *after):
            tasks.append((name, gen, after, len(tasks)))

        def ffn1_tasks(g, blocks, before, store_out):
            gates_of = lambda g: [("gates", g, b) for b in GROUPS[g % NGROUP]] if g >= 0 else []
            task(("open", g), lambda: open_group(g), *gates_of(g - 2))
            for m, b in enumerate(blocks):
                task(("gates", g, b), lambda b=b, m=m: ffn1_gates(b, m, open_groups[g]), ("open", g), (before, b),
                     *gates_of(g - 1))
            task(("sort", g), lambda: ffn1_sort(open_groups[g]), *gates_of(g))
            for t in range(0, MAXT, 2):
                task(("experts", g, t), lambda t=t: ffn1_experts(open_groups[g], t), ("sort", g))
            for m, b in enumerate(blocks):
                task(("combine", g, b), lambda b=b, m=m: ffn1_combine(b, m, open_groups[g], store_out),
                     *(("experts", g, t) for t in range(0, MAXT, 2)))
            task(("close", g), lambda: close_group(g), *(("combine", g, b) for b in blocks))

        for g, blocks in enumerate(GROUPS):
            for b in blocks:
                task(("ffn0", b), lambda b=b: ffn0(b))
                task(("mamba", b), lambda b=b: mamba(b), ("ffn0", b))
                task(("ffn0b", b), lambda b=b: ffn0(b), ("mamba", b))
            ffn1_tasks(g, blocks, "ffn0b", False)
            for b in blocks:
                task(("kv", b), lambda b=b: attn_kv(b), ("combine", g, b),
                     *([("kv", b - 1)] if b % BLK_PER_BATCH else []))
        for g, blocks in enumerate(GROUPS):
            for b in blocks:
                task(("out", b), lambda b=b: attn_out(b), last_kv(b))
            ffn1_tasks(NGROUP + g, blocks, "out", True)
        active, blocked, running = [], [], []

        def finished(branch):
            parent = branch["parent"]
            if parent is None:
                done.add(branch["name"])
                ended[branch["name"]] = branch["time"]
                running.remove(branch["name"][0])
            else:
                parent["branches"] -= 1
                parent["time"] = max(parent["time"], branch["time"])
                if parent["branches"] == 0:
                    active.append(parent)

        while tasks or active or blocked:
            for t in list(tasks):
                kind = t[0][0]
                if (len(running) < ACTIVE and running.count(kind) < LIMIT.get(kind, ACTIVE)
                        and all(a in done for a in t[2])):
                    tasks.remove(t)
                    running.append(kind)
                    start = max([ended[a] for a in t[2]] + [0.0])
                    active.append({"time": start, "order": t[3], "name": t[0], "steps": t[1](),
                                   "parent": None})
            assert active, ([t["name"] for t in blocked], [t[0] for t in tasks][:5])
            branch = min(active, key=lambda t: (t["time"], t["order"]))
            active.remove(branch)
            q.last = 0.0
            start_time = branch["time"]
            result = next(branch["steps"], "end")
            branch["time"] = max(branch["time"], q.last)
            if result is WAITING:
                blocked.append(branch)
                continue
            if result == "end":
                finished(branch)
            elif isinstance(result, dict):
                branch["time"] = max(start_time, q.finish[result["until"]])
                active.append(branch)
            elif isinstance(result, list):
                branch["branches"] = len(result)
                for gen in result:
                    active.append({"time": branch["time"], "order": branch["order"], "name": branch["name"],
                                   "steps": gen, "parent": branch})
            else:
                active.append(branch)
            active, blocked = active + blocked, []
        q.wait("sync", ("sync_store", q.count["sync_store"]))


def constants():
    u = np.arange(P)
    e = np.arange(E1)
    return {
        "ident": np.eye(P, dtype=np.float32),
        "tri_incl": (u[:, None] <= u[None, :]).astype(np.float32),
        "tri_strict": (u[:, None] > u[None, :]).astype(np.float32),
        "head_mask": (u[:, None] // ADIM == np.arange(AHEADS)[None, :]).astype(np.float32),
        "first_key": (E1 - np.arange(E1, dtype=np.float32))[None, :],
        "below": (e[None, :] < e[:, None]).astype(np.float32).reshape(1, -1),
        "tile_start": (P * np.arange(NT, dtype=np.float32))[None, :],
        "slot_tile": np.arange(MAXT, dtype=np.float32)[None, :],
    }


def kernel(**inputs):
    import concourse.bacc as bacc
    from concourse.bass_utils import run_bass_kernel_spmd

    i = {k: np.asarray(v) for k, v in inputs.items()}
    in_proj = i["L0_attn_in_proj_w"]
    conv = DINNER + 2 * DSTATE
    pad = np.zeros((SCH * SCW - ISHARED, DM), np.float32)
    gate_up = i["L1_ffn_experts_gate_up"].transpose(2, 0, 1)
    down = i["L1_ffn_experts_down"].reshape(E1, DM, 2, IHALF).transpose(3, 0, 2, 1)
    shared_down = np.concatenate([i["L1_ffn_shared_down_w"].T, pad]).reshape(SCH, SCW, DM)
    arrays = {
        "x": i["L0_attn_x"].reshape(-1, DM),
        "w0": i["L0_ffn_weight"].T,
        "u0": i["L0_ffn_lora_U"].reshape(-1, DM).T,
        "gate0": i["L0_ffn_gate_w"].T,
        "v0": i["L0_ffn_lora_V"].transpose(0, 2, 1).reshape(-1, DM),
        "xbc_w": in_proj[DINNER:DINNER + conv].T,
        "zdt_w": np.concatenate([in_proj[:DINNER], in_proj[DINNER + conv:]]).T,
        "conv_w": i["L0_attn_conv_w"].reshape(XBC_CHUNKS, P, DCONV).transpose(1, 0, 2),
        "conv_b": i["L0_attn_conv_b"].reshape(XBC_CHUNKS, P).T,
        "ln_w": i["L0_attn_ln_w"][:, None],
        "ln_b": i["L0_attn_ln_b"][:, None],
        "dt_bias": i["L0_attn_dt_bias"][None, :],
        "a_log": i["L0_attn_A_log"][None, :],
        "d_skip": i["L0_attn_D"][None, :],
        "norm_w": i["L0_attn_norm_w"].reshape(-1, P).T,
        "out_w": i["L0_attn_out_proj_w"].T.reshape(-1, P, DM).transpose(1, 0, 2),
        "gu_w": gate_up.reshape(DM, -1),
        "d_w": down.reshape(IHALF, -1),
        "sg_w": np.concatenate([i["L1_ffn_shared_gate_w"], pad]).T,
        "su_w": np.concatenate([i["L1_ffn_shared_up_w"], pad]).T,
        "sd_w": shared_down.transpose(1, 0, 2),
        "gate1": np.concatenate([i["L1_ffn_gate_w"], i["L1_ffn_shared_expert_gate_w"]]).T,
        "qkv_w": np.concatenate([i["L1_attn_Wq"], i["L1_attn_Wk"], i["L1_attn_Wv"]]).T,
        "qkv_b": np.concatenate([i["L1_attn_bq"], i["L1_attn_bk"], i["L1_attn_bv"]])[None, :],
        "p_w": i["L1_attn_Wp"].T,
        "p_b": i["L1_attn_bp"][None, :],
    }
    arrays.update(constants())
    arrays = {f"in_{k}": np.ascontiguousarray(v) for k, v in arrays.items()}
    nc = bacc.Bacc("TRN2", target_bir_lowering=False, num_devices=1)
    d = {k[3:]: nc.dram_tensor(k, v.shape, mybir.dt.from_np(v.dtype), kind="ExternalInput").ap()
         for k, v in arrays.items()}
    out = nc.dram_tensor("out", (BATCH * SEQ, DM), F32, kind="ExternalOutput").ap()
    build(nc, d, out)
    r = run_bass_kernel_spmd(nc, [arrays], core_ids=[0])
    return r.results[0]["out"].reshape(BATCH, SEQ, DM)
```
